# Optimizing a Trainium2 kernel written in Bass

```python
import numpy as np
import jax
import jax.numpy as jnp

def _softmax(x, axis=-1):
    return jax.nn.softmax(x, axis=axis)

def _gelu(x):
    return jax.nn.gelu(x, approximate=True)

def _silu(x):
    return jax.nn.silu(x)

def _sigmoid(x):
    return jax.nn.sigmoid(x)

def _layernorm(x, axis=-1, eps=1e-05):
    m = jnp.mean(x, axis=axis, keepdims=True)
    v = jnp.var(x, axis=axis, keepdims=True)
    return (x - m) / jnp.sqrt(v + eps)

def _scatter_add(tgt, idx, src, axis=0):
    return tgt.at[idx].add(src)

def _segment_sum(src, seg, n):
    return jax.ops.segment_sum(src, seg, n)
kernel_name = 'mk_flamingo_gated_d2_seqx_r8_1ddd31'

def setup_inputs(seed: int=0):
    np.random.seed(seed)
    _w = jnp.asarray

    def _rec_inputs():
        import jax
        import jax.numpy as jnp
        _rk = jax.random.key(seed)
        x = -0.0002928 + 1 * jax.random.normal(jax.random.fold_in(_rk, 1), (8, 256, 256), jnp.float32)
        _lenS = 256 - jax.random.randint(jax.random.fold_in(_rk, 7), (8,), 0, max(1, 256 // 4) + 1, jnp.int32)
        _lenS2 = 64 - jax.random.randint(jax.random.fold_in(_rk, 8), (8,), 0, max(1, 64 // 4) + 1, jnp.int32)
        _ctx_2048P = jax.random.normal(jax.random.fold_in(_rk, 11), (8, 16, 256), jnp.float32)
        _ctx_2048c = jax.random.dirichlet(jax.random.fold_in(_rk, 511), 0.3 * jnp.ones((16,), jnp.float32), (8, 64))
        _ctx_2048t = jnp.einsum('bsk,bkd->bsd', _ctx_2048c, _ctx_2048P)
        _ctx_2048t = _ctx_2048t * jax.lax.rsqrt(jnp.mean(jnp.square(_ctx_2048t)) + 1e-12) * 0.953939
        ctx_2048 = 4.13588e-05 + 0.999923 * (_ctx_2048t + 0.3 * jax.random.normal(jax.random.fold_in(_rk, 611), (8, 64, 256), jnp.float32))
        _validS = jnp.arange(256)[None, :] < _lenS[:, None]
        _validS2 = jnp.arange(64)[None, :] < _lenS2[:, None]
        _causal = jnp.tril(jnp.ones((256, 256), dtype=bool))
        mask_1xSxS2_ff0 = jnp.where(jnp.ones((1, 256, 64), dtype=bool), 0.0, -1000000000.0).astype(jnp.float32)
        _g = jax.random.normal(jax.random.fold_in(_rk, 9001), (2, 2), jnp.float32)
        _g = jnp.sign(_g) * jnp.maximum(jnp.abs(_g), 1.0) + (_g == 0) * 1.0
        g_xattn = _g[0]
        g_ffn = _g[1]
        return (x, ctx_2048, mask_1xSxS2_ff0, g_xattn, g_ffn)
    x, ctx_2048, mask_1xSxS2_ff0, g_xattn, g_ffn = _rec_inputs()

    def _L0_xattn_setup():
        import jax, jax.numpy as jnp
        import numpy as np
        H = 256
        NH = 16
        NKV = 4
        HD = 128
        GROUPS = NH // NKV
        EPS = 1e-06
        B, S, SE = (1, 256, 512)

        def _rmsnorm(x, w, eps=EPS):
            xf = x.astype(jnp.float32)
            var = jnp.mean(xf * xf, axis=-1, keepdims=True)
            return (xf * jax.lax.rsqrt(var + eps)).astype(x.dtype) * w
        key = jax.random.key(seed)
        ks = jax.random.split(key, 12)
        sc = 0.02
        return {'hidden_states': jax.random.normal(ks[0], (B, S, H), jnp.float32), 'encoder_hidden_states': jax.random.normal(ks[1], (B, SE, H), jnp.float32), 'attention_mask': jnp.zeros((B, S, SE), jnp.float32), 'Wq': jax.random.normal(ks[2], (H, NH * HD), jnp.float32) * sc, 'bq': jax.random.normal(ks[3], (NH * HD,), jnp.float32) * sc, 'Wk': jax.random.normal(ks[4], (H, NKV * HD), jnp.float32) * sc, 'bk': jax.random.normal(ks[5], (NKV * HD,), jnp.float32) * sc, 'Wv': jax.random.normal(ks[6], (H, NKV * HD), jnp.float32) * sc, 'bv': jax.random.normal(ks[7], (NKV * HD,), jnp.float32) * sc, 'Wo': jax.random.normal(ks[8], (NH * HD, H), jnp.float32) * sc, 'qn_w': jnp.ones((HD,), jnp.float32), 'kn_w': jnp.ones((HD,), jnp.float32)}
    _L0_xattn_all = _L0_xattn_setup()
    _L0_xattn_in = {k: v for k, v in _L0_xattn_all.items() if k in ('Wq', 'bq', 'Wk', 'bk', 'Wv', 'bv', 'Wo', 'qn_w', 'kn_w')}
    del _L0_xattn_all

    def _L0_ffn_setup():
        import jax, jax.numpy as jnp
        import numpy as np
        import math
        B, S, D = (2, 256, 256)
        H, HD = (16, 128)
        E, I = (4, 256)
        TOP_K = 2
        ROPE_THETA = 10000.0

        def _layernorm(x, w, b):
            mu = jnp.mean(x, axis=-1, keepdims=True)
            var = jnp.mean(jnp.square(x - mu), axis=-1, keepdims=True)
            return (x - mu) * jax.lax.rsqrt(var + 1e-05) * w + b

        def _rotate_half(x):
            x1, x2 = jnp.split(x, 2, axis=-1)
            return jnp.concatenate((-x2, x1), axis=-1)

        def _attention(h, wq, bq, wk, bk, wv, bv, wo, bo):
            b, s, _ = h.shape
            q = (h @ wq + bq).reshape(b, s, H, HD).transpose(0, 2, 1, 3)
            k = (h @ wk + bk).reshape(b, s, H, HD).transpose(0, 2, 1, 3)
            v = (h @ wv + bv).reshape(b, s, H, HD).transpose(0, 2, 1, 3)
            inv_freq = 1.0 / ROPE_THETA ** (jnp.arange(0, HD, 2, dtype=jnp.float32) / HD)
            freqs = jnp.arange(s, dtype=jnp.float32)[:, None] * inv_freq[None, :]
            emb = jnp.concatenate((freqs, freqs), axis=-1)
            cos = jnp.cos(emb)[None, None]
            sin = jnp.sin(emb)[None, None]
            q = q * cos + _rotate_half(q) * sin
            k = k * cos + _rotate_half(k) * sin
            scores = jnp.einsum('bhqd,bhkd->bhqk', q, k) / math.sqrt(HD)
            causal = jnp.tril(jnp.ones((s, s), bool))
            scores = jnp.where(causal[None, None], scores, jnp.finfo(jnp.float32).min)
            probs = jax.nn.softmax(scores.astype(jnp.float32), axis=-1).astype(q.dtype)
            out = jnp.einsum('bhqk,bhkd->bhqd', probs, v)
            out = out.transpose(0, 2, 1, 3).reshape(b, s, H * HD)
            return out @ wo + bo

        def _moe(h, w_gate, we1, be1, we2, be2):
            b, s, d = h.shape
            x = h.reshape(-1, d)
            t = x.shape[0]
            raw = jax.nn.softmax(x @ w_gate, axis=-1)
            top_vals, top_idx = jax.lax.top_k(raw, TOP_K)
            w = jax.nn.softmax(top_vals, axis=-1)
            comb = jnp.zeros((t, E), x.dtype).at[jnp.arange(t)[:, None], top_idx].add(w)
            hmid = jax.nn.gelu(jnp.einsum('td,edi->tei', x, we1) + be1[None], approximate=False)
            eout = jnp.einsum('tei,eid->ted', hmid, we2) + be2[None]
            out = jnp.einsum('te,ted->td', comb, eout)
            return out.reshape(b, s, d)
        key = jax.random.key(seed)
        ks = jax.random.split(key, 20)
        s = 0.02
        p = {'hidden_states': jax.random.normal(ks[0], (B, S, D), jnp.float32), 'wq': jax.random.normal(ks[1], (D, H * HD), jnp.float32) * s, 'bq': jnp.zeros((H * HD,), jnp.float32), 'wk': jax.random.normal(ks[2], (D, H * HD), jnp.float32) * s, 'bk': jnp.zeros((H * HD,), jnp.float32), 'wv': jax.random.normal(ks[3], (D, H * HD), jnp.float32) * s, 'bv': jnp.zeros((H * HD,), jnp.float32), 'wo': jax.random.normal(ks[4], (H * HD, D), jnp.float32) * s, 'bo': jnp.zeros((D,), jnp.float32), 'ln1_w': jnp.ones((D,), jnp.float32), 'ln1_b': jnp.zeros((D,), jnp.float32), 'ln2_w': jnp.ones((D,), jnp.float32), 'ln2_b': jnp.zeros((D,), jnp.float32), 'w_gate': jax.random.normal(ks[5], (D, E), jnp.float32) * s, 'we1': jax.random.normal(ks[6], (E, D, I), jnp.float32) * s, 'be1': jnp.zeros((E, I), jnp.float32), 'we2': jax.random.normal(ks[7], (E, I, D), jnp.float32) * s, 'be2': jnp.zeros((E, D), jnp.float32)}
        return p
    _L0_ffn_all = _L0_ffn_setup()
    _L0_ffn_in = {k: v for k, v in _L0_ffn_all.items() if k in ('wq', 'bq', 'wk', 'bk', 'wv', 'bv', 'wo', 'bo', 'ln1_w', 'ln1_b', 'ln2_w', 'ln2_b', 'w_gate', 'we1', 'be1', 'we2', 'be2')}
    del _L0_ffn_all

    def _L1_xattn_setup():
        import jax, jax.numpy as jnp
        import numpy as np
        HIDDEN = 256
        NUM_HEADS = 16
        NUM_KV_HEADS = 4
        HEAD_DIM = 128
        ROPE_THETA = 10000.0
        EPS = 1e-06

        def rms_norm(x, w, eps=EPS):
            var = jnp.mean(jnp.square(x), axis=-1, keepdims=True)
            return x * jax.lax.rsqrt(var + eps) * w

        def rope_cache(L, head_dim, theta, dtype):
            inv_freq = 1.0 / theta ** (jnp.arange(0, head_dim, 2, dtype=jnp.float32) / head_dim)
            t = jnp.arange(L, dtype=jnp.float32)
            freqs = jnp.outer(t, inv_freq)
            emb = jnp.concatenate([freqs, freqs], -1)
            cos = jnp.cos(emb).astype(dtype)[None, :, None, :]
            sin = jnp.sin(emb).astype(dtype)[None, :, None, :]
            return (cos, sin)

        def rotate_half(x):
            x1, x2 = jnp.split(x, 2, axis=-1)
            return jnp.concatenate([-x2, x1], axis=-1)
        key = jax.random.key(seed)
        ks = jax.random.split(key, 10)
        B, L, T = (2, 256, 64)
        q_out = NUM_HEADS * HEAD_DIM
        kv_out = NUM_KV_HEADS * HEAD_DIM
        s = lambda fan_in: 1.0 / np.sqrt(fan_in)
        return {'x': jax.random.normal(ks[0], (B, L, HIDDEN), jnp.float32), 'h_ctx_kv': jax.random.normal(ks[1], (B, T, HIDDEN), jnp.float32), 'wq': jax.random.normal(ks[2], (HIDDEN, q_out), jnp.float32) * s(HIDDEN), 'wk': jax.random.normal(ks[3], (HIDDEN, kv_out), jnp.float32) * s(HIDDEN), 'wv': jax.random.normal(ks[4], (HIDDEN, kv_out), jnp.float32) * s(HIDDEN), 'wo': jax.random.normal(ks[5], (q_out, HIDDEN), jnp.float32) * s(q_out), 'wk_ctx': jax.random.normal(ks[6], (HIDDEN, kv_out), jnp.float32) * s(HIDDEN), 'wv_ctx': jax.random.normal(ks[7], (HIDDEN, kv_out), jnp.float32) * s(HIDDEN), 'q_norm_w': jnp.ones((HEAD_DIM,), jnp.float32), 'k_norm_w': jnp.ones((HEAD_DIM,), jnp.float32)}
    _L1_xattn_all = _L1_xattn_setup()
    _L1_xattn_in = {k: v for k, v in _L1_xattn_all.items() if k in ('wq', 'wk', 'wv', 'wo', 'wk_ctx', 'wv_ctx', 'q_norm_w', 'k_norm_w')}
    del _L1_xattn_all

    def _L1_ffn_setup():
        import jax, jax.numpy as jnp
        import numpy as np
        HIDDEN = 256
        INTER = 704
        B, S = (2, 256)

        def _ternary(key, shape):
            return jax.random.randint(key, shape, -1, 2).astype(jnp.float32)
        key = jax.random.key(seed)
        ks = jax.random.split(key, 7)
        x = jax.random.normal(ks[0], (B, S, HIDDEN), dtype=jnp.float32)
        gate_w = _ternary(ks[1], (INTER, HIDDEN))
        up_w = _ternary(ks[2], (INTER, HIDDEN))
        down_w = _ternary(ks[3], (HIDDEN, INTER))
        gate_s = jax.random.uniform(ks[4], (INTER,), minval=0.01, maxval=0.1, dtype=jnp.float32)
        up_s = jax.random.uniform(ks[5], (INTER,), minval=0.01, maxval=0.1, dtype=jnp.float32)
        down_s = jax.random.uniform(ks[6], (HIDDEN,), minval=0.01, maxval=0.1, dtype=jnp.float32)
        return {'x': x, 'gate_w': gate_w, 'up_w': up_w, 'down_w': down_w, 'gate_s': gate_s, 'up_s': up_s, 'down_s': down_s}
    _L1_ffn_all = _L1_ffn_setup()
    _L1_ffn_in = {k: v for k, v in _L1_ffn_all.items() if k in ('gate_w', 'up_w', 'down_w', 'gate_s', 'up_s', 'down_s')}
    del _L1_ffn_all
    return {'x': x, 'ctx_2048': ctx_2048, 'mask_1xSxS2_ff0': mask_1xSxS2_ff0, 'g_xattn': g_xattn, 'g_ffn': g_ffn, 'L0_xattn_Wq': _L0_xattn_in['Wq'], 'L0_xattn_bq': _L0_xattn_in['bq'], 'L0_xattn_Wk': _L0_xattn_in['Wk'], 'L0_xattn_bk': _L0_xattn_in['bk'], 'L0_xattn_Wv': _L0_xattn_in['Wv'], 'L0_xattn_bv': _L0_xattn_in['bv'], 'L0_xattn_Wo': _L0_xattn_in['Wo'], 'L0_xattn_qn_w': _L0_xattn_in['qn_w'], 'L0_xattn_kn_w': _L0_xattn_in['kn_w'], 'L0_ffn_wq': _L0_ffn_in['wq'], 'L0_ffn_bq': _L0_ffn_in['bq'], 'L0_ffn_wk': _L0_ffn_in['wk'], 'L0_ffn_bk': _L0_ffn_in['bk'], 'L0_ffn_wv': _L0_ffn_in['wv'], 'L0_ffn_bv': _L0_ffn_in['bv'], 'L0_ffn_wo': _L0_ffn_in['wo'], 'L0_ffn_bo': _L0_ffn_in['bo'], 'L0_ffn_ln1_w': _L0_ffn_in['ln1_w'], 'L0_ffn_ln1_b': _L0_ffn_in['ln1_b'], 'L0_ffn_ln2_w': _L0_ffn_in['ln2_w'], 'L0_ffn_ln2_b': _L0_ffn_in['ln2_b'], 'L0_ffn_w_gate': _L0_ffn_in['w_gate'], 'L0_ffn_we1': _L0_ffn_in['we1'], 'L0_ffn_be1': _L0_ffn_in['be1'], 'L0_ffn_we2': _L0_ffn_in['we2'], 'L0_ffn_be2': _L0_ffn_in['be2'], 'L1_xattn_wq': _L1_xattn_in['wq'], 'L1_xattn_wk': _L1_xattn_in['wk'], 'L1_xattn_wv': _L1_xattn_in['wv'], 'L1_xattn_wo': _L1_xattn_in['wo'], 'L1_xattn_wk_ctx': _L1_xattn_in['wk_ctx'], 'L1_xattn_wv_ctx': _L1_xattn_in['wv_ctx'], 'L1_xattn_q_norm_w': _L1_xattn_in['q_norm_w'], 'L1_xattn_k_norm_w': _L1_xattn_in['k_norm_w'], 'L1_ffn_gate_w': _L1_ffn_in['gate_w'], 'L1_ffn_up_w': _L1_ffn_in['up_w'], 'L1_ffn_down_w': _L1_ffn_in['down_w'], 'L1_ffn_gate_s': _L1_ffn_in['gate_s'], 'L1_ffn_up_s': _L1_ffn_in['up_s'], 'L1_ffn_down_s': _L1_ffn_in['down_s']}

def reference(x, ctx_2048, mask_1xSxS2_ff0, g_xattn, g_ffn, L0_xattn_Wq, L0_xattn_bq, L0_xattn_Wk, L0_xattn_bk, L0_xattn_Wv, L0_xattn_bv, L0_xattn_Wo, L0_xattn_qn_w, L0_xattn_kn_w, L0_ffn_wq, L0_ffn_bq, L0_ffn_wk, L0_ffn_bk, L0_ffn_wv, L0_ffn_bv, L0_ffn_wo, L0_ffn_bo, L0_ffn_ln1_w, L0_ffn_ln1_b, L0_ffn_ln2_w, L0_ffn_ln2_b, L0_ffn_w_gate, L0_ffn_we1, L0_ffn_be1, L0_ffn_we2, L0_ffn_be2, L1_xattn_wq, L1_xattn_wk, L1_xattn_wv, L1_xattn_wo, L1_xattn_wk_ctx, L1_xattn_wv_ctx, L1_xattn_q_norm_w, L1_xattn_k_norm_w, L1_ffn_gate_w, L1_ffn_up_w, L1_ffn_down_w, L1_ffn_gate_s, L1_ffn_up_s, L1_ffn_down_s):
    import jax
    import jax.numpy as jnp

    def _L0_xattn_ref(hidden_states, encoder_hidden_states, attention_mask, Wq, bq, Wk, bk, Wv, bv, Wo, qn_w, kn_w):
        import jax, jax.numpy as jnp
        import numpy as np
        H = 256
        NH = 16
        NKV = 4
        HD = 128
        GROUPS = NH // NKV
        EPS = 1e-06
        B, S, SE = (1, 256, 512)

        def _rmsnorm(x, w, eps=EPS):
            xf = x.astype(jnp.float32)
            var = jnp.mean(xf * xf, axis=-1, keepdims=True)
            return (xf * jax.lax.rsqrt(var + eps)).astype(x.dtype) * w
        b, s, _ = hidden_states.shape
        se = encoder_hidden_states.shape[1]
        q = (hidden_states @ Wq + bq).reshape(b, s, NH, HD).transpose(0, 2, 1, 3)
        k = (encoder_hidden_states @ Wk + bk).reshape(b, se, NKV, HD).transpose(0, 2, 1, 3)
        v = (encoder_hidden_states @ Wv + bv).reshape(b, se, NKV, HD).transpose(0, 2, 1, 3)
        k = jnp.repeat(k, GROUPS, axis=1)
        v = jnp.repeat(v, GROUPS, axis=1)
        q = _rmsnorm(q, qn_w)
        k = _rmsnorm(k, kn_w)
        scale = 1.0 / np.sqrt(HD).astype(np.float32)
        scores = jnp.einsum('bhsd,bhed->bhse', q, k) * scale
        scores = scores + attention_mask[:, None, :, :]
        probs = jax.nn.softmax(scores.astype(jnp.float32), axis=-1).astype(q.dtype)
        out = jnp.einsum('bhse,bhed->bhsd', probs, v)
        out = out.transpose(0, 2, 1, 3).reshape(b, s, NH * HD)
        return out @ Wo

    def _L0_ffn_ref(hidden_states, wq, bq, wk, bk, wv, bv, wo, bo, ln1_w, ln1_b, ln2_w, ln2_b, w_gate, we1, be1, we2, be2):
        import jax, jax.numpy as jnp
        import numpy as np
        import math
        B, S, D = (2, 256, 256)
        H, HD = (16, 128)
        E, I = (4, 256)
        TOP_K = 2
        ROPE_THETA = 10000.0

        def _layernorm(x, w, b):
            mu = jnp.mean(x, axis=-1, keepdims=True)
            var = jnp.mean(jnp.square(x - mu), axis=-1, keepdims=True)
            return (x - mu) * jax.lax.rsqrt(var + 1e-05) * w + b

        def _rotate_half(x):
            x1, x2 = jnp.split(x, 2, axis=-1)
            return jnp.concatenate((-x2, x1), axis=-1)

        def _attention(h, wq, bq, wk, bk, wv, bv, wo, bo):
            b, s, _ = h.shape
            q = (h @ wq + bq).reshape(b, s, H, HD).transpose(0, 2, 1, 3)
            k = (h @ wk + bk).reshape(b, s, H, HD).transpose(0, 2, 1, 3)
            v = (h @ wv + bv).reshape(b, s, H, HD).transpose(0, 2, 1, 3)
            inv_freq = 1.0 / ROPE_THETA ** (jnp.arange(0, HD, 2, dtype=jnp.float32) / HD)
            freqs = jnp.arange(s, dtype=jnp.float32)[:, None] * inv_freq[None, :]
            emb = jnp.concatenate((freqs, freqs), axis=-1)
            cos = jnp.cos(emb)[None, None]
            sin = jnp.sin(emb)[None, None]
            q = q * cos + _rotate_half(q) * sin
            k = k * cos + _rotate_half(k) * sin
            scores = jnp.einsum('bhqd,bhkd->bhqk', q, k) / math.sqrt(HD)
            causal = jnp.tril(jnp.ones((s, s), bool))
            scores = jnp.where(causal[None, None], scores, jnp.finfo(jnp.float32).min)
            probs = jax.nn.softmax(scores.astype(jnp.float32), axis=-1).astype(q.dtype)
            out = jnp.einsum('bhqk,bhkd->bhqd', probs, v)
            out = out.transpose(0, 2, 1, 3).reshape(b, s, H * HD)
            return out @ wo + bo

        def _moe(h, w_gate, we1, be1, we2, be2):
            b, s, d = h.shape
            x = h.reshape(-1, d)
            t = x.shape[0]
            raw = jax.nn.softmax(x @ w_gate, axis=-1)
            top_vals, top_idx = jax.lax.top_k(raw, TOP_K)
            w = jax.nn.softmax(top_vals, axis=-1)
            comb = jnp.zeros((t, E), x.dtype).at[jnp.arange(t)[:, None], top_idx].add(w)
            hmid = jax.nn.gelu(jnp.einsum('td,edi->tei', x, we1) + be1[None], approximate=False)
            eout = jnp.einsum('tei,eid->ted', hmid, we2) + be2[None]
            out = jnp.einsum('te,ted->td', comb, eout)
            return out.reshape(b, s, d)
        a = _attention(_layernorm(hidden_states, ln1_w, ln1_b), wq, bq, wk, bk, wv, bv, wo, bo)
        h = hidden_states + a
        m = _moe(_layernorm(h, ln2_w, ln2_b), w_gate, we1, be1, we2, be2)
        return h + m

    def _L1_xattn_ref(x, h_ctx_kv, wq, wk, wv, wo, wk_ctx, wv_ctx, q_norm_w, k_norm_w):
        import jax, jax.numpy as jnp
        import numpy as np
        HIDDEN = 256
        NUM_HEADS = 16
        NUM_KV_HEADS = 4
        HEAD_DIM = 128
        ROPE_THETA = 10000.0
        EPS = 1e-06

        def rms_norm(x, w, eps=EPS):
            var = jnp.mean(jnp.square(x), axis=-1, keepdims=True)
            return x * jax.lax.rsqrt(var + eps) * w

        def rope_cache(L, head_dim, theta, dtype):
            inv_freq = 1.0 / theta ** (jnp.arange(0, head_dim, 2, dtype=jnp.float32) / head_dim)
            t = jnp.arange(L, dtype=jnp.float32)
            freqs = jnp.outer(t, inv_freq)
            emb = jnp.concatenate([freqs, freqs], -1)
            cos = jnp.cos(emb).astype(dtype)[None, :, None, :]
            sin = jnp.sin(emb).astype(dtype)[None, :, None, :]
            return (cos, sin)

        def rotate_half(x):
            x1, x2 = jnp.split(x, 2, axis=-1)
            return jnp.concatenate([-x2, x1], axis=-1)
        B, L, _ = x.shape
        T = h_ctx_kv.shape[1]
        rep = NUM_HEADS // NUM_KV_HEADS
        q = (x @ wq).reshape(B, L, NUM_HEADS, HEAD_DIM)
        k = (x @ wk).reshape(B, L, NUM_KV_HEADS, HEAD_DIM)
        v = (x @ wv).reshape(B, L, NUM_KV_HEADS, HEAD_DIM)
        q = rms_norm(q, q_norm_w)
        k = rms_norm(k, k_norm_w)
        k_ctx = (h_ctx_kv @ wk_ctx).reshape(B, T, NUM_KV_HEADS, HEAD_DIM)
        v_ctx = (h_ctx_kv @ wv_ctx).reshape(B, T, NUM_KV_HEADS, HEAD_DIM)
        k_ctx = rms_norm(k_ctx, k_norm_w)
        cos, sin = rope_cache(L, HEAD_DIM, ROPE_THETA, x.dtype)
        q = q * cos + rotate_half(q) * sin
        k = k * cos + rotate_half(k) * sin
        k_full = jnp.concatenate([k_ctx, k], axis=1)
        v_full = jnp.concatenate([v_ctx, v], axis=1)
        k_full = jnp.repeat(k_full, rep, axis=2)
        v_full = jnpp_repeat = jnp.repeat(v_full, rep, axis=2)
        i = jnp.arange(L)[:, None]
        j = jnp.arange(L)[None, :]
        causal = jnp.where(j > i, -jnp.inf, 0.0).astype(x.dtype)
        mask = jnp.concatenate([jnp.zeros((L, T), x.dtype), causal], axis=1)
        scale = 1.0 / np.sqrt(HEAD_DIM)
        scores = jnp.einsum('blhd,bmhd->bhlm', q, k_full) * scale + mask
        probs = jax.nn.softmax(scores, axis=-1)
        out = jnp.einsum('bhlm,bmhd->blhd', probs, v_full)
        out = out.reshape(B, L, NUM_HEADS * HEAD_DIM)
        return out @ wo

    def _L1_ffn_ref(x, gate_w, up_w, down_w, gate_s, up_s, down_s):
        import jax, jax.numpy as jnp
        import numpy as np
        HIDDEN = 256
        INTER = 704
        B, S = (2, 256)

        def _ternary(key, shape):
            return jax.random.randint(key, shape, -1, 2).astype(jnp.float32)
        b, s, h = x.shape
        xf = x.reshape(b * s, h)
        g = jnp.einsum('th,ih->ti', xf, gate_w) * gate_s
        u = jnp.einsum('th,ih->ti', xf, up_w) * up_s
        hdn = jax.nn.silu(g) * u
        out = jnp.einsum('ti,hi->th', hdn, down_w) * down_s
        return out.reshape(b, s, -1)
    x = x + jnp.tanh(g_xattn[0]) * _L0_xattn_ref(_layernorm(x, axis=-1), ctx_2048, mask_1xSxS2_ff0, L0_xattn_Wq, L0_xattn_bq, L0_xattn_Wk, L0_xattn_bk, L0_xattn_Wv, L0_xattn_bv, L0_xattn_Wo, L0_xattn_qn_w, L0_xattn_kn_w)
    x = x + jnp.tanh(g_ffn[0]) * _L0_ffn_ref(_layernorm(x, axis=-1), L0_ffn_wq, L0_ffn_bq, L0_ffn_wk, L0_ffn_bk, L0_ffn_wv, L0_ffn_bv, L0_ffn_wo, L0_ffn_bo, L0_ffn_ln1_w, L0_ffn_ln1_b, L0_ffn_ln2_w, L0_ffn_ln2_b, L0_ffn_w_gate, L0_ffn_we1, L0_ffn_be1, L0_ffn_we2, L0_ffn_be2)
    x = x + jnp.tanh(g_xattn[1]) * _L1_xattn_ref(_layernorm(x, axis=-1), ctx_2048, L1_xattn_wq, L1_xattn_wk, L1_xattn_wv, L1_xattn_wo, L1_xattn_wk_ctx, L1_xattn_wv_ctx, L1_xattn_q_norm_w, L1_xattn_k_norm_w)
    x = x + jnp.tanh(g_ffn[1]) * _L1_ffn_ref(_layernorm(x, axis=-1), L1_ffn_gate_w, L1_ffn_up_w, L1_ffn_down_w, L1_ffn_gate_s, L1_ffn_up_s, L1_ffn_down_s)
    return x

_drawn_inputs = setup_inputs


def setup_inputs(seed=0):
    import zlib

    import numpy as np

    out = dict(_drawn_inputs(seed))
    spreads = {'g_ffn': (-1.0, 0.2),
     'L0_xattn_qn_w': (1.0, 0.6),
     'L0_xattn_kn_w': (1.0, 0.6),
     'L0_ffn_bq': (0.0, 0.771),
     'L0_ffn_bk': (0.0, 0.8),
     'L0_ffn_bv': (0.0, 0.1),
     'L0_ffn_bo': (0.0, 0.1),
     'L0_ffn_ln1_w': (1.0, 0.2),
     'L0_ffn_ln1_b': (0.0, 0.1),
     'L0_ffn_ln2_w': (1.0, 0.2),
     'L0_ffn_ln2_b': (0.0, 0.1),
     'L0_ffn_be1': (0.0, 0.1),
     'L0_ffn_be2': (0.0, 0.1),
     'L1_xattn_q_norm_w': (1.0, 0.2),
     'L1_xattn_k_norm_w': (1.0, 0.2)}
    factors = {'L0_xattn_bq': 5.91, 'L0_xattn_bk': 8.0, 'L0_ffn_wq': 3.069, 'L0_ffn_wk': 3.169}
    for name, (base, spread) in spreads.items():
        noise = np.random.default_rng([zlib.crc32(name.encode()), seed]).standard_normal(out[name].shape)
        drawn = base * np.exp(spread * noise) if base else spread * noise
        out[name] = jnp.asarray(drawn.astype(out[name].dtype))
    for name, factor in factors.items():
        out[name] = (out[name] * factor).astype(out[name].dtype)
    return out
```

```python
from collections import namedtuple
from contextlib import ExitStack

import numpy as np
import concourse.bass as bass
from concourse import mybir

F32 = mybir.dt.float32
F32R = mybir.dt.float32r
ALU = mybir.AluOpType
ACT = mybir.ActivationFunctionType
AX = mybir.AxisListType

P = 128
B, S, D = 8, 256, 256
SC = 64
T = S // P
KD = D // P
HD = 128
NH, NKV = 16, 4
G = 4
HG = NH // G
GW = HG * HD
E = 4
NI = G * B
FM = 6
FW = FM * P
WSLOT = 2 * KD * FW + FM * D
CW_X0, CW_F0, CW_MOE, CW_X1, CW_FF = 256, 512, 512, 320, WSLOT // 8
NEG = -1e30
H2 = HD // 2
Phase = namedtuple("Phase", "sync gpsimd scalar vector tensor")


def ds(i, n=1):
    return bass.ds(i, n)


def pos(n):
    return max(n, 0) if isinstance(n, int) else n


def in_pairs(e, n, body, last_group_from=None):
    cut = last_group_from if last_group_from is not None else n
    for i in (0, 1):
        body(i, i, i >= cut)
    if cut < n:
        with e.Fori(1, cut // 2) as j:
            for s in (0, 1):
                body(e.snap(2 * j + s), s, False)
        with e.Fori(cut // 2, n // 2 - 1) as j:
            for s in (0, 1):
                body(e.snap(2 * j + s), s, True)
    else:
        with e.Fori(1, n // 2 - 1) as j:
            for s in (0, 1):
                body(e.snap(2 * j + s), s, False)
    for s in (0, 1):
        body(n - 2 + s, s, cut < n)


def bc(ap, dim, n):
    u = ap.unsqueeze(dim)
    return u.to_broadcast([*u.shape[:dim], n, *u.shape[dim + 1:]])


def build(nc, d, out, spill, stop=99):
    ctx = ExitStack()
    with ctx:
        def lasting_sem(name):
            return ctx.enter_context(nc.semaphore(name))

        phase_sems = ExitStack()
        numbers = []

        def sem(name):
            h = phase_sems.enter_context(nc.semaphore(name))
            numbers.append(h)
            return h

        def psum(name, shape):
            return ctx.enter_context(nc.psum_tensor(name, shape, F32))

        def sb(name, shape, dt=F32, where=ctx):
            return where.enter_context(nc.sbuf_tensor(name, shape, dt))

        pA = psum("pA", [P, 2, 512])
        pT = psum("pT", [P, 2, 512])
        pS = psum("pS", [P, 2, 512])
        pO = psum("pO", [P, 512])
        pF = psum("pF", [P, 512])

        R = sb("R", [P, B * T, D])
        XT = sb("XT", [P, KD, B * S])
        Wh = sb("Wh", [P, 2, WSLOT], F32R)
        Wl = sb("Wl", [P, 2, WSLOT], F32R)
        RAW = sb("RAW", [P, 2, CW_FF])
        XSh = sb("XSh", [P, 2, KD, S], F32R)
        XSl = sb("XSl", [P, 2, KD, S], F32R)
        ident = sb("ident", [P, P])
        tanhg = sb("tanhg", [P, 4])
        mhalf = sb("mhalf", [P, 8])
        mv = sb("mv", [P, 2, T, 2])
        rstd = sb("rstd", [P, 2, T])

        ticks = lasting_sem("ticks")

        def apart(e, n):
            if not isinstance(n, int):
                e.sem_inc(ticks, 1)

        bar = lasting_sem("bar")
        cleared = lasting_sem("cleared")
        sems_of = {}
        phases = {}

        def phase_end(e, name):
            k = phases.setdefault(name, len(phases) + 1)
            e.drain().then_inc(bar, 1)
            if e is nc.gpsimd:
                e.wait_ge(bar, 5 * k)
                for h in [ticks, *sems_of[name]]:
                    e.sem_clear(h)
                e.nop().then_inc(cleared, 1)
            e.wait_ge(cleared, k)

        def close_phase(name):
            sems_of[name] = list(numbers)
            numbers.clear()
            phase_sems.close()

        def stream_sp(sp, raw_in, split_done, src, cw, step, s, first=0):
            sp.wait_ge(split_done, pos(step - 1))
            sp.dma_start(RAW[:, s:s + 1, 0:cw], src[ds(step - first)].rearrange("a p c -> p a c")
                         ).then_inc(raw_in[s], 16)

        def split(pool, raw_in, split_hi, split_done, cw, step, s, slot):
            col = (step % 8) * cw
            pool.wait_ge(raw_in[s], 16 * (step // 2 + 1))
            apart(pool, 16 * (step // 2 + 1))
            raw = RAW[:, s:s + 1, 0:cw]
            hi = Wh[:, ds(slot), ds(col, cw)]
            pool.tensor_copy(hi, raw).then_inc(split_hi, 1)
            pool.wait_ge(split_hi, step + 1)
            apart(pool, step + 1)
            pool.tensor_tensor(Wl[:, ds(slot), ds(col, cw)], raw, hi.bitcast(F32),
                               ALU.subtract).then_inc(split_done, 1)

        ld_R, ld_c, c_half, c_tanh, out_done = (
            lasting_sem(x) for x in ("ld_R", "ld_c", "c_half", "c_tanh", "out_done"))
        x_rows = d["x"].rearrange("b (t p) n -> p (b t) n", p=P)
        gates = sb("gates", [P, 4])

        def init_sp(sp):
            sp.dma_start(ident[:, :], d["ident"]).then_inc(ld_c, 16)
            sp.dma_start(gates[:, :], d["gates"].partition_broadcast(P)).then_inc(ld_c, 16)
            for k in range(4):
                sp.dma_start(R[:, 4 * k:4 * k + 4, :], x_rows[:, 4 * k:4 * k + 4, :]).then_inc(ld_R, 16)

        def init_pool(pool):
            pool.memset(mhalf[:, :], -0.5).then_inc(c_half, 1)

        def init_act(act):
            act.wait_ge(ld_c, 32)
            act.activation(tanhg[:, :], gates[:, :], ACT.Tanh).then_inc(c_tanh, 1)

        def init_all(e):
            e.wait_ge(ld_c, 32)
            e.wait_ge(ld_R, 64)
            e.wait_ge(c_half, 1)
            e.wait_ge(c_tanh, 1)

        def layer_norm(name, double=False, affine=None, after=None):
            s_st = sem(name + "_stats")
            s_rs = sem(name + "_rstd")
            s_v = sem(name + "_dve")
            s_p = sem(name + "_pool")
            s_hid = sem(name + "_hid")
            s_xn = sem(name + "_xn")
            s_tr = sem(name + "_tr")
            s_ev = sem(name + "_ev")
            rounds = 2 if double else 1
            scope = ExitStack()
            bst = sb(name + "_bst", [P, T, 6], F32, scope)
            xn = sb(name + "_xn", [P, 2, T, D], F32, scope)

            def pool_rstd(pool, n, s):
                pool.wait_ge(s_st, n + 1)
                apart(pool, n + 1)
                pool.tensor_scalar(rstd[:, s, :], mv[:, s, :, 1], 1e-5, None, ALU.add).then_inc(s_p, 1)
                pool.wait_ge(s_p, 2 * n + 1)
                apart(pool, 2 * n + 1)
                pool.tensor_tensor(rstd[:, s, :], rstd[:, s, :], mhalf[:, 0:T], ALU.pow).then_inc(s_rs, 1)
                pool.nop().then_inc(s_p, 1)

            def pool(e):
                def body(i, s, _):
                    for r in range(rounds):
                        pool_rstd(e, rounds * i + r, s)
                    if after is not None:
                        e.wait_ge(s_xn, i + 1)
                        apart(e, i + 1)
                        e.tensor_tensor(R[:, ds(2 * i, T), :], R[:, ds(2 * i, T), :],
                                        bc(after[:, :], 1, T), ALU.add)
                in_pairs(e, B, body)
                phase_end(e, name)

            def dve(e):
                def stats(i, s, n):
                    for t in range(T):
                        e.bn_stats(bst[:, t, :], R[:, ds(2 * i + t), :]).then_inc(s_v, 1)
                    e.wait_ge(s_v, T * (n + 1))
                    apart(e, T * (n + 1))
                    for t in range(T):
                        ins = e.bn_aggr(mv[:, s, t, :], bst[:, t, :])
                    ins.then_inc(s_st, 1)
                    e.wait_ge(s_st, n + 1)

                def body(i, s, _):
                    for r in range(rounds):
                        n = rounds * i + r
                        stats(i, s, n)
                        e.wait_ge(s_rs, n + 1)
                        if double and r == 0:
                            for t in range(T):
                                ins = e.tensor_scalar(R[:, ds(2 * i + t), :], R[:, ds(2 * i + t), :],
                                                      mv[:, s, t, 0:1], rstd[:, s, t:t + 1],
                                                      ALU.subtract, ALU.mult)
                            ins.then_inc(s_hid, 1)
                            e.wait_ge(s_hid, i + 1)
                            apart(e, i + 1)
                            continue
                        e.wait_ge(s_tr, pos(i - 1))
                        for t in range(T):
                            ins = e.tensor_scalar(xn[:, s, t, :], R[:, ds(2 * i + t), :],
                                                  mv[:, s, t, 0:1], rstd[:, s, t:t + 1],
                                                  ALU.subtract, ALU.mult)
                        ins.then_inc(s_xn, 1)
                        e.wait_ge(s_xn, i + 1)
                        apart(e, i + 1)
                in_pairs(e, B, body)
                phase_end(e, name)

            def pe(e):
                def body(i, s, _):
                    e.wait_ge(s_xn, i + 1)
                    e.wait_ge(s_ev, pos(i - 1))
                    for k in range(KD):
                        for t in range(T):
                            ins = e.transpose(pT[:, s, k * S + t * P:k * S + t * P + P],
                                              xn[:, s, t, k * P:k * P + P], ident[:, :])
                    ins.then_inc(s_tr, 1)
                in_pairs(e, B, body)
                phase_end(e, name)

            def act(e):
                def body(i, s, _):
                    e.wait_ge(s_tr, i + 1)
                    if affine is None:
                        ins = e.activation(XT[:, :, ds(i * S, S)],
                                           pT[:, s, :].rearrange("p (k n) -> p k n", k=KD), ACT.Copy)
                    else:
                        w, b = affine
                        for k in range(KD):
                            ins = e.activation(XT[:, k, ds(i * S, S)], pT[:, s, k * S:(k + 1) * S],
                                               ACT.Identity, scale=w[:, k:k + 1], bias=b[:, k:k + 1])
                    ins.then_inc(s_ev, 1)
                in_pairs(e, B, body)
                phase_end(e, name)

            def sp(e):
                phase_end(e, name)

            close_phase(name)
            scope.close()
            return Phase(sp, pool, act, dve, pe)

        def context(name, scope, wk, wv, KT, w_col, bk=None, VT=None, bv=None, VC=None, first_stream=None):
            cT = sb(name + "_cT", [P, KD, 512], F32, scope)
            wkv = sb(name + "_wkv", [P, 2, KD, 512], F32, scope)
            kb = sb(name + "_kb", [P, 2, 512], F32, scope)
            sq = sb(name + "_sq", [P, 2, 512], F32, scope)
            ss = sb(name + "_ss", [P, 2, 4], F32, scope)
            s_ld, s_k, s_kb, s_sq, s_ss, s_p, s_rk, s_kn, s_t, s_te, s_v, s_ve = (
                sem(f"{name}_{x}") for x in ("ld", "k", "kb", "sq", "ss", "pool", "rk", "kn", "t", "te",
                                             "v", "ve"))
            raw_in = [sem(f"{name}_raw{x}") for x in range(2)]
            split_hi, split_done = sem(name + "_hi"), sem(name + "_split")
            NC = B * SC // P

            def sp(e):
                e.dma_start(cT[:, :, :], d["ctxT"].rearrange("(k p) n -> p k n", p=P)).then_inc(s_ld, 16)
                e.dma_start(wkv[:, 0], wk.rearrange("(k p) n -> p k n", p=P)).then_inc(s_ld, 16)
                e.dma_start(wkv[:, 1], wv.rearrange("(k p) n -> p k n", p=P)).then_inc(s_ld, 16)
                if first_stream:
                    src, cw = first_stream
                    for c in range(8):
                        stream_sp(e, raw_in, split_done, src, cw, c, c % 2)
                phase_end(e, name)

            def pe(e):
                e.wait_ge(s_ld, 48)
                for c in range(NC):
                    e.wait_ge(s_kb, pos(c - 1))
                    for k in range(KD):
                        ins = e.matmul(pA[:, c % 2, :], cT[:, k, c * P:(c + 1) * P], wkv[:, 0, k, :],
                                       start=(k == 0), stop=(k == KD - 1))
                    ins.then_inc(s_k, 1)
                for c in range(4):
                    e.wait_ge(s_ve, pos(c - 1))
                    for k in range(KD):
                        if VT is not None:
                            ins = e.matmul(pS[:, c % 2, :], wkv[:, 1, k, c * HD:(c + 1) * HD], cT[:, k, :],
                                           start=(k == 0), stop=(k == KD - 1))
                        else:
                            ins = e.matmul(pS[:, c % 2, :], cT[:, k, c * P:(c + 1) * P], wkv[:, 1, k, :],
                                           start=(k == 0), stop=(k == KD - 1))
                    ins.then_inc(s_v, 1)
                for c in range(NC):
                    e.wait_ge(s_kn, c + 1)
                    e.wait_ge(s_te, pos(c - 1))
                    for h in range(NKV):
                        ins = e.transpose(pT[:, c % 2, h * P:(h + 1) * P], kb[:, c % 2, h * P:(h + 1) * P],
                                          ident[:, :])
                    ins.then_inc(s_t, 1)
                phase_end(e, name)

            def dve(e):
                for c in range(NC):
                    s = c % 2
                    e.wait_ge(s_k, c + 1)
                    e.wait_ge(s_t, pos(c - 1))
                    if bk is not None:
                        e.tensor_tensor(kb[:, s, :], pA[:, s, :], bk[:, :], ALU.add).then_inc(s_kb, 1)
                    else:
                        e.tensor_copy(kb[:, s, :], pA[:, s, :]).then_inc(s_kb, 1)
                    e.wait_ge(s_sq, c + 1)
                    e.tensor_reduce(ss[:, s, :], sq[:, s, :].rearrange("p (h d) -> p h d", h=NKV),
                                    AX.X, ALU.add).then_inc(s_ss, 1)
                    e.wait_ge(s_rk, c + 1)
                    v = kb[:, s, :].rearrange("p (h d) -> p h d", h=NKV)
                    e.tensor_tensor(v, v, bc(ss[:, s, :], 2, HD), ALU.mult).then_inc(s_kn, 1)
                phase_end(e, name)

            def pool(e):
                for c in range(NC):
                    s = c % 2
                    e.wait_ge(s_kb, c + 1)
                    apart(e, c + 1)
                    e.wait_ge(s_ss, pos(c - 1))
                    apart(e, c - 1)
                    e.tensor_tensor(sq[:, s, :], kb[:, s, :], kb[:, s, :], ALU.mult).then_inc(s_sq, 1)
                    e.wait_ge(s_ss, c + 1)
                    apart(e, c + 1)
                    e.tensor_scalar(ss[:, s, :], ss[:, s, :], 1.0 / HD, 1e-6, ALU.mult, ALU.add).then_inc(s_p, 1)
                    e.wait_ge(s_p, c + 1)
                    apart(e, c + 1)
                    e.tensor_tensor(ss[:, s, :], ss[:, s, :], mhalf[:, 0:4], ALU.pow).then_inc(s_rk, 1)
                if first_stream:
                    src, cw = first_stream
                    for c in range(8):
                        split(e, raw_in, split_hi, split_done, cw, c, c % 2, 0)
                phase_end(e, name)

            def act(e):
                for c in range(4):
                    e.wait_ge(s_v, c + 1)
                    if VT is not None:
                        e.activation(VT[:, c, :], pS[:, c % 2, :], ACT.Identity,
                                     bias=bv[:, c:c + 1]).then_inc(s_ve, 1)
                    else:
                        for r in range(2):
                            for q in range(2):
                                ins = e.activation(VC[q * SC:(q + 1) * SC, 2 * c + r, :],
                                                   pS[r * SC:(r + 1) * SC, c % 2, :], ACT.Copy)
                        ins.then_inc(s_ve, 1)
                for c in range(NC):
                    e.wait_ge(s_t, c + 1)
                    e.activation(KT[:, :, c * P:(c + 1) * P],
                                 pT[:, c % 2, :].rearrange("p (h n) -> p h n", h=NKV),
                                 ACT.Copy, scale=w_col[:, 0:1]).then_inc(s_te, 1)
                phase_end(e, name)

            close_phase(name)
            return Phase(sp, pool, act, dve, pe)

        def three(e, o, ah, al, bh, bl, first, last):
            e.matmul(o, ah, bh, start=first, stop=False)
            e.matmul(o, ah, bl, start=False, stop=False)
            return e.matmul(o, al, bh, start=False, stop=last)

        def copy_x(pool, s, i, ready, hi_done):
            src = XT[:, :, ds((i % B) * S, S)]
            pool.tensor_copy(XSh[:, s], src).then_inc(hi_done, 1)
            pool.wait_ge(hi_done, i + 1)
            apart(pool, i + 1)
            pool.tensor_tensor(XSl[:, s], src, XSh[:, s].bitcast(F32), ALU.subtract).then_inc(ready, 1)

        x0 = ExitStack()

        def cross_attention_0():
            name = "x0"
            KT = sb("x0_KT", [P, NKV, B * SC], F32, x0)
            VT = sb("x0_VT", [P, NKV, B * SC], F32, x0)
            bq = sb("x0_bq", [P, NH * HD], F32, x0)
            bk = sb("x0_bk", [P, NKV * HD], F32, x0)
            bv = sb("x0_bv", [P, NKV], F32, x0)
            wcol = sb("x0_w", [P, 3], F32, x0)
            mask = sb("x0_mask", [P, T, SC], F32, x0)
            s_c, s_w = sem("x0_c"), sem("x0_wq")

            def pre_sp(e):
                e.dma_start(bq[:, :], d["x0_bq"].partition_broadcast(P)).then_inc(s_c, 16)
                e.dma_start(bk[:, :], d["x0_bk"].partition_broadcast(P)).then_inc(s_c, 16)
                e.dma_start(bv[:, :], d["x0_bv"]).then_inc(s_c, 16)
                e.dma_start(wcol[:, 0:2], d["x0_w"]).then_inc(s_c, 16)
                e.dma_start(mask[:, :, :], d["mask"].rearrange("a (t p) k -> p (a t) k", p=P)).then_inc(s_c, 16)

            def pre_dve(e):
                e.wait_ge(s_c, 80)
                e.tensor_tensor(wcol[:, 2:3], wcol[:, 0:1], wcol[:, 1:2], ALU.mult).then_inc(s_w, 1)

            def pre_act(e):
                e.wait_ge(s_w, 1)

            with ExitStack() as tmp:
                before = context("c0", tmp, d["x0_Wk"], d["x0_Wv"], KT, wcol[:, 2:3], bk=bk, VT=VT, bv=bv,
                        first_stream=(d["w_x0"], CW_X0))
            norm = layer_norm("n0")

            qb = sb("x0_qb", [P, T, GW], F32, x0)
            sq = sb("x0_sq", [P, T, GW], F32, x0)
            ssq = sb("x0_ss", [P, T, HG], F32, x0)
            rq = sb("x0_rq", [P, T, HG], F32, x0)
            qT = sb("x0_qT", [P, HG, S], F32, x0)
            PB = sb("x0_P", [P, T, HG, SC], F32, x0)
            mx = sb("x0_mx", [P, T, HG], F32, x0)
            sm = sb("x0_sm", [P, T, HG], F32, x0)
            PT = sb("x0_PT", [P, 2, S], F32, x0)
            VSh = sb("x0_VSh", [P, P], F32R, x0)
            VSl = sb("x0_VSl", [P, P], F32R, x0)
            VW = sb("x0_VW", [P, 2, 2, D], F32, x0)
            names = ("raw0", "raw1", "hi", "split", "xhi", "xs", "proj", "qb", "sq", "ssq", "rqa", "rq", "tr", "te",
                     "sc", "s1", "s2", "mx", "s3", "ex", "sm", "rs", "pn", "pt", "pte", "f", "acc",
                     "vhi", "vs", "vw", "vwe")
            q = {x: sem("x0_" + x) for x in names}
            raw_in = [q["raw0"], q["raw1"]]
            WO = KD * GW

            def sp(e):
                def body(i, s, nxt):
                    if nxt:
                        stream_sp(e, raw_in, q["split"], d["w_f0"], CW_F0, i, s, 24)
                    else:
                        stream_sp(e, raw_in, q["split"], d["w_x0"][8:32], CW_X0, i, s)
                in_pairs(e, NI, body, 24)
                phase_end(e, name)

            def pool(e):
                def xs(i, s):
                    e.wait_ge(q["proj"], pos(T * (i - 1)))
                    apart(e, T * (i - 1))
                    copy_x(e, s, i, q["xs"], q["xhi"])

                def vs(i):
                    j = i // 2
                    e.wait_ge(q["vw"], 2 * j)
                    apart(e, 2 * j)
                    src = VT[:, ds(i // B), ds((i % B) * SC, P)]
                    e.tensor_copy(VSh[:, :], src).then_inc(q["vhi"], 1)
                    e.wait_ge(q["vhi"], j + 1)
                    apart(e, j + 1)
                    e.tensor_tensor(VSl[:, :], src, VSh[:, :].bitcast(F32), ALU.subtract).then_inc(q["vs"], 1)

                def norms(i):
                    for t in range(T):
                        e.wait_ge(q["qb"], T * i + t + 1)
                        apart(e, T * i + t + 1)
                        e.wait_ge(q["ssq"], pos(T * i + t - 1))
                        apart(e, T * i + t - 1)
                        e.tensor_tensor(sq[:, t, :], qb[:, t, :], qb[:, t, :], ALU.mult).then_inc(q["sq"], 1)
                    e.wait_ge(q["ssq"], T * i + T)
                    apart(e, T * i + T)
                    e.wait_ge(q["s1"], i)
                    apart(e, i)
                    e.tensor_scalar(rq[:, :, :], ssq[:, :, :], HD * 1e-6, None, ALU.add).then_inc(q["rqa"], 1)
                    e.wait_ge(q["rqa"], i + 1)
                    apart(e, i + 1)
                    e.tensor_tensor(rq[:, :, :].rearrange("p t h -> p (t h)"),
                                    rq[:, :, :].rearrange("p t h -> p (t h)"),
                                    mhalf[:, 0:T * HG], ALU.pow).then_inc(q["rq"], 1)

                def mask_add(i):
                    e.wait_ge(q["s1"], i + 1)
                    apart(e, i + 1)
                    for t in range(T):
                        ins = e.tensor_tensor(PB[:, t], PB[:, t], bc(mask[:, t, :], 1, HG), ALU.add)
                    ins.then_inc(q["s2"], 1)
                    e.wait_ge(q["mx"], i + 1)
                    apart(e, i + 1)
                    ins = e.tensor_tensor(PB[:, :, :, :], PB[:, :, :, :], bc(mx[:, :, :], 3, SC), ALU.subtract)
                    ins.then_inc(q["s3"], 1)

                def normalise(i):
                    e.wait_ge(q["rs"], i + 1)
                    apart(e, i + 1)
                    e.tensor_tensor(PB[:, :, :, :], PB[:, :, :, :], bc(sm[:, :, :], 3, SC),
                                    ALU.mult).then_inc(q["pn"], 1)

                def body(i, s, nxt):
                    first, last = isinstance(i, int) and i == 0, isinstance(i, int) and i == NI - 1
                    if first:
                        xs(0, 0)
                        vs(0)
                        norms(0)
                        xs(1, 1)
                        mask_add(0)
                    normalise(i)
                    if not last:
                        norms(i + 1)
                    if s == 1 and not last:
                        vs(i + 1)
                    e.wait_ge(q["proj"], T * i)
                    apart(e, T * i)
                    if nxt:
                        split(e, raw_in, q["hi"], q["split"], CW_F0, i, s, 0)
                    else:
                        split(e, raw_in, q["hi"], q["split"], CW_X0, i, s, (i // 8 + 1) % 2)
                    if not (isinstance(i, int) and i >= NI - 2):
                        xs(i + 2, s)
                    if not last:
                        mask_add(i + 1)
                in_pairs(e, NI, body, 24)
                phase_end(e, name)

            def pe(e):
                def proj(i, s):
                    e.wait_ge(q["xs"], i + 1)
                    e.wait_ge(q["split"], pos(i - 2))
                    slot = (i // 8) % 2
                    for t in range(T):
                        e.wait_ge(q["qb"], pos(T * (i - 1) + t + 1))
                        for k in range(KD):
                            w = slice(k * GW, (k + 1) * GW)
                            ins = three(e, pA[:, t, :], XSh[:, s, k, t * P:(t + 1) * P],
                                        XSl[:, s, k, t * P:(t + 1) * P], Wh[:, ds(slot), w],
                                        Wl[:, ds(slot), w], k == 0, k == KD - 1)
                        ins.then_inc(q["proj"], 1)

                def vw(i):
                    e.wait_ge(q["vs"], i // 2 + 1)
                    e.wait_ge(q["split"], i)
                    slot = (i // 8) % 2
                    for hp, bank in ((0, pO[:, :]), (1, pS[:, 1, :])):
                        e.wait_ge(q["vwe"], pos(i + hp - 1))
                        w = slice(WO + hp * 512, WO + (hp + 1) * 512)
                        ins = three(e, bank, VSh[:, :], VSl[:, :], Wh[:, ds(slot), w], Wl[:, ds(slot), w],
                                    True, True)
                        ins.then_inc(q["vw"], 1)

                def q_tr(i):
                    for t in range(T):
                        e.wait_ge(q["qb"], T * i + t + 1)
                        e.wait_ge(q["te"], pos(T * (i - 1) + t + 1))
                        if t == 0:
                            e.wait_ge(q["pte"], i)
                        for h in range(HG):
                            ins = e.transpose(pT[:, t, h * P:(h + 1) * P], qb[:, t, h * HD:(h + 1) * HD],
                                              ident[:, :])
                        ins.then_inc(q["tr"], 1)

                def scores(i):
                    e.wait_ge(q["te"], T * i + T)
                    e.wait_ge(q["s1"], i)
                    g, b = i // 8, i % 8
                    for t in range(T):
                        for h in range(HG):
                            c = (t * HG + h) * SC
                            ins = e.matmul(pS[:, 0, c:c + SC], qT[:, h, t * P:(t + 1) * P],
                                           KT[:, ds(g), ds(b * SC, SC)], start=True, stop=True)
                    ins.then_inc(q["sc"], 1)

                def p_tr(i):
                    e.wait_ge(q["pn"], i + 1)
                    e.wait_ge(q["te"], T * i + 1)
                    for hp in range(2):
                        for t in range(T):
                            c = (hp * T + t) * P
                            ins = e.transpose(pT[:, 0, c:c + P],
                                              PB[:, t, 2 * hp:2 * hp + 2, :].rearrange("p h k -> p (h k)"),
                                              ident[:, :])
                    ins.then_inc(q["pt"], 1)

                def out_proj(i, s):
                    e.wait_ge(q["pte"], i + 1)
                    e.wait_ge(q["vwe"], pos((i - s if not isinstance(i, int) else 2 * (i // 2)) + 2))
                    e.wait_ge(q["acc"], i)
                    for t in range(T):
                        for hp in range(2):
                            ins = e.matmul(pF[:, t * D:(t + 1) * D], PT[:, hp, t * P:(t + 1) * P],
                                           VW[:, s, hp, :], start=(hp == 0), stop=(hp == 1))
                    ins.then_inc(q["f"], 1)

                def body(i, s, nxt):
                    first, last = isinstance(i, int) and i == 0, isinstance(i, int) and i == NI - 1
                    if first:
                        proj(0, 0)
                        q_tr(0)
                        scores(0)
                    if s == 0:
                        vw(i)
                    if not last:
                        proj(i + 1, 1 - s)
                    p_tr(i)
                    if not last:
                        q_tr(i + 1)
                    out_proj(i, s)
                    if not last:
                        scores(i + 1)
                in_pairs(e, NI, body, 24)
                phase_end(e, name)

            def act(e):
                def q_ev(i):
                    for t in range(T):
                        e.wait_ge(q["tr"], T * i + t + 1)
                        e.wait_ge(q["sc"], i)
                        e.activation(qT[:, :, t * P:(t + 1) * P],
                                     pT[:, t, :].rearrange("p (h n) -> p h n", h=HG), ACT.Copy
                                     ).then_inc(q["te"], 1)

                def exp(i):
                    e.wait_ge(q["s3"], i + 1)
                    e.activation(PB[:, :, :, :], PB[:, :, :, :], ACT.Exp).then_inc(q["ex"], 1)

                def vw_ev(i):
                    for hp, bank in ((0, pO[:, :]), (1, pS[:, 1, :])):
                        e.wait_ge(q["vw"], i + hp + 1)
                        e.wait_ge(q["f"], i)
                        for r in range(2):
                            for par in range(2):
                                ins = e.activation(VW[par * SC:(par + 1) * SC, r, hp, :],
                                                   bank[r * SC:(r + 1) * SC, par * D:(par + 1) * D], ACT.Copy)
                        ins.then_inc(q["vwe"], 1)

                def body(i, s, nxt):
                    first, last = isinstance(i, int) and i == 0, isinstance(i, int) and i == NI - 1
                    if first:
                        q_ev(0)
                        exp(0)
                    if s == 0:
                        vw_ev(i)
                    e.wait_ge(q["pt"], i + 1)
                    e.wait_ge(q["f"], i)
                    e.activation(PT[:, :, :], pT[:, 0, :].rearrange("p (a n) -> p a n", a=2), ACT.Copy
                                 ).then_inc(q["pte"], 1)
                    if not last:
                        q_ev(i + 1)
                        exp(i + 1)
                in_pairs(e, NI, body, 24)
                phase_end(e, name)

            def dve(e):
                def queries(i):
                    g = i // 8
                    for t in range(T):
                        e.wait_ge(q["proj"], T * i + t + 1)
                        e.wait_ge(q["tr"], pos(T * (i - 1) + t + 1))
                        e.wait_ge(q["sq"], pos(T * (i - 1) + t + 1))
                        e.tensor_tensor(qb[:, t, :], pA[:, t, :], bq[:, ds(g * GW, GW)], ALU.add
                                        ).then_inc(q["qb"], 1)
                    for t in range(T):
                        e.wait_ge(q["sq"], T * i + t + 1)
                        e.wait_ge(q["rq"], i)
                        e.tensor_reduce(ssq[:, t, :], sq[:, t, :].rearrange("p (h d) -> p h d", h=HG),
                                        AX.X, ALU.add).then_inc(q["ssq"], 1)

                def softmax(i):
                    e.wait_ge(q["sc"], i + 1)
                    e.wait_ge(q["rq"], i + 1)
                    e.wait_ge(q["pt"], i)
                    e.tensor_tensor(PB[:, :, :, :].rearrange("p t h k -> p (t h) k"),
                                    pS[:, 0, :].rearrange("p (a k) -> p a k", k=SC),
                                    bc(rq[:, :, :].rearrange("p t h -> p (t h)"), 2, SC), ALU.mult
                                    ).then_inc(q["s1"], 1)
                    e.wait_ge(q["s2"], i + 1)
                    e.tensor_reduce(mx[:, :, :], PB[:, :, :, :], AX.X, ALU.max).then_inc(q["mx"], 1)
                    e.wait_ge(q["ex"], i + 1)
                    e.tensor_reduce(sm[:, :, :], PB[:, :, :, :], AX.X, ALU.add).then_inc(q["sm"], 1)
                    e.wait_ge(q["sm"], i + 1)
                    e.reciprocal(sm[:, :, :], sm[:, :, :]).then_inc(q["rs"], 1)

                def body(i, s, nxt):
                    first, last = isinstance(i, int) and i == 0, isinstance(i, int) and i == NI - 1
                    if first:
                        queries(0)
                        softmax(0)
                    if not last:
                        queries(i + 1)
                    e.wait_ge(q["f"], i + 1)
                    e.wait_ge(q["acc"], i)
                    b = i % 8
                    r = R[:, ds(T * b, T), :]
                    e.scalar_tensor_tensor(r, pF[:, :].rearrange("p (t n) -> p t n", t=T), tanhg[:, 0:1], r,
                                           ALU.mult, ALU.add).then_inc(q["acc"], 1)
                    if not last:
                        softmax(i + 1)
                in_pairs(e, NI, body, 24)
                phase_end(e, name)

            close_phase(name)
            return Phase(pre_sp, None, pre_act, pre_dve, None), before, norm, Phase(sp, pool, act, dve, pe)

        pre0, context0, n0, cross0 = cross_attention_0()
        x0.close()

        def causal_attention(name, scope, cross, w_here, cw_here, w_next, cw_next, slot0,
                             KT=None, VC=None):
            SW = 512 if cross else 384
            OFF = (0, SC + P) if cross else (0, P)
            WID = (SC + P, SC + S) if cross else (P, S)
            KW = HD if cross else GW
            NQ = 4 if cross else 6
            NT = 3 if cross else 4
            NTI = NT + HG
            WK = KD * GW
            WV = 2 * KD * GW
            WO = KD * (GW + 2 * KW)

            cosT = sb(name + "_cos", [P, T, HD], F32, scope)
            sinT = sb(name + "_sin", [P, T, HD], F32, scope)
            mask = sb(name + "_mask", [P, SW], F32, scope)
            qb = sb(name + "_qb", [P, 2, GW], F32, scope)
            t2 = sb(name + "_t2", [P, 2, GW], F32, scope)
            QR = sb(name + "_QR", [P, T, GW], F32, scope)
            KR = sb(name + "_KR", [P, T, KW], F32, scope)
            qT = sb(name + "_qT", [P, HG, S], F32, scope)
            kT = sb(name + "_kT", [P, KW // HD, S], F32, scope)
            V = sb(name + "_V", [P, 2, T, KW], F32, scope)
            PB = sb(name + "_P", [P, HG, SW], F32, scope)
            nm = sb(name + "_nm", [P, HG, T], F32, scope)
            sm = sb(name + "_sm", [P, HG, T], F32, scope)
            rs = sb(name + "_rs", [P, HG, T], F32, scope)
            PT = sb(name + "_PT", [P, 2, SW], F32, scope)
            OTh = sb(name + "_OTh", [P, 2, HG, S], F32R, scope)
            OTl = sb(name + "_OTl", [P, 2, HG, S], F32R, scope)
            names = ("raw0", "raw1", "hi", "split", "xhi", "xs", "proj", "taken", "rot", "rc", "rope", "tr",
                     "te", "sc", "sct", "ex", "rs", "pn", "pv", "oth", "ot", "f", "acc", "const", "table")
            q = {x: sem(f"{name}_{x}") for x in names}
            raw_in = [q["raw0"], q["raw1"]]
            if cross:
                wrow = sb(name + "_w", [P, 4, HD], F32, scope)
                cosk = sb(name + "_cosk", [P, T, HD], F32, scope)
                sink = sb(name + "_sink", [P, T, HD], F32, scope)
                sq = sb(name + "_sq", [P, GW], F32, scope)
                sqk = sb(name + "_sqk", [P, HD], F32, scope)
                ssq = sb(name + "_ssq", [P, T, HG], F32, scope)
                nrq = sb(name + "_nrq", [P, T, HG], F32, scope)
                ssk = sb(name + "_ssk", [P, T], F32, scope)
                kb = sb(name + "_kb", [P, T, HD], F32, scope)
                tk = sb(name + "_tk", [P, T, HD], F32, scope)
                VS = sb(name + "_VS", [P, 2, T, HD], F32, scope)
                q.update({x: sem(f"{name}_{x}") for x in ("sq", "ssq", "rqa", "rqb", "rq", "sqk", "ssk", "rka",
                                                         "rk", "k1", "vs", "vz")})
            else:
                bias = sb(name + "_bias", [P, G, 3, GW], F32, scope)

            def isfirst(i):
                return isinstance(i, int) and i == 0

            def islast(i):
                return isinstance(i, int) and i == NI - 1

            def use(i, what, n, s):
                if what == "w":
                    early = 0 if islast(i) else (1 if cross else 2)
                    c = NT + (n if n < 3 else 3 + early)
                    return NTI * i + c, (NTI * s + c) % 2
                if isfirst(i):
                    return n, n % 2
                early = 1 if cross else 2
                c = NT + (3 + n if n < early else 4 + n)
                return NTI * (i - 1) + c, (NTI * (s + 1) + c) % 2

            def sp(e):
                e.dma_start(cosT[:, :, :], d["cos"].rearrange("(t p) n -> p t n", p=P)).then_inc(q["const"], 16)
                e.dma_start(sinT[:, :, :], d["sin"].rearrange("(t p) n -> p t n", p=P)).then_inc(q["const"], 16)
                e.dma_start(mask[:, :], d["mask_x1" if cross else "mask_f0"]).then_inc(q["const"], 16)
                if cross:
                    e.dma_start(wrow[:, :, :].rearrange("p a n -> p (a n)"),
                                d["x1_w"].partition_broadcast(P)).then_inc(q["const"], 16)
                else:
                    e.dma_start(bias[:, :, :, :].rearrange("p g a n -> p (g a n)"),
                                d["f0_b"].partition_broadcast(P)).then_inc(q["const"], 16)

                def body(i, s, nxt):
                    if nxt:
                        stream_sp(e, raw_in, q["split"], w_next, cw_next, i, s, 24)
                    else:
                        stream_sp(e, raw_in, q["split"], w_here[8:32], cw_here, i, s)
                in_pairs(e, NI, body, 24)
                phase_end(e, name)

            def pe(e):
                def proj(i, s, n):
                    c = NQ * i + n
                    e.wait_ge(q["xs"], i + 1)
                    e.wait_ge(q["split"], pos(i - 2))
                    e.wait_ge(q["taken"], pos(c - 1))
                    slot = (i // 8 + slot0) % 2
                    t = n // 2 if n < 4 else n - 4
                    if cross:
                        at, w = (WK, 2 * HD) if n % 2 else (0, GW)
                    else:
                        at, w = (WV if n >= 4 else WK * (n % 2)), GW
                    for k in range(KD):
                        cc = slice(at + k * w, at + (k + 1) * w)
                        ins = three(e, pA[:, n % 2, 0:w], XSh[:, s, k, t * P:(t + 1) * P],
                                    XSl[:, s, k, t * P:(t + 1) * P], Wh[:, ds(slot), cc],
                                    Wl[:, ds(slot), cc], k == 0, k == KD - 1)
                    ins.then_inc(q["proj"], 1)

                def qk_tr(i, s, n):
                    c, bank = use(i, "qk", n, s)
                    e.wait_ge(q["te"], pos(c - 1))
                    if cross:
                        e.wait_ge(q["rope"], 4 * i + (1, 3, 4)[n])
                        src = [QR[:, n, h * HD:(h + 1) * HD] for h in range(HG)] if n < 2 else \
                              [KR[:, t, :] for t in range(T)]
                    else:
                        e.wait_ge(q["rope"], 4 * i + n + 1)
                        x = KR if n % 2 else QR
                        src = [x[:, n // 2, h * HD:(h + 1) * HD] for h in range(HG)]
                    for j, a in enumerate(src):
                        ins = e.transpose(pT[:, bank, j * P:(j + 1) * P], a, ident[:, :])
                    ins.then_inc(q["tr"], 1)

                def scores(i, s, h):
                    c, _ = use(i, "qk", NT - 1, s)
                    e.wait_ge(q["te"], c + 1)
                    e.wait_ge(q["sct"], pos(HG * i + h - 1))
                    bank = pS[:, h % 2, :]
                    for t in range(T):
                        o, n = t * P, (t + 1) * P
                        if cross:
                            o = 2 * t * P
                            c = P + t * SC
                            e.matmul(bank[:, c:c + SC], qT[:, h, t * P:(t + 1) * P],
                                     KT[:, ds(i // 8), ds((i % 8) * SC, SC)], start=True, stop=True)
                        ins = e.matmul(bank[:, o:o + n], qT[:, h, t * P:(t + 1) * P],
                                       kT[:, 0 if cross else h, 0:n], start=True, stop=True)
                    ins.then_inc(q["sc"], 1)

                def p_tr(i, s, h):
                    c, bank = use(i, "w", h, s)
                    e.wait_ge(q["pn"], HG * i + h + 1)
                    e.wait_ge(q["te"], pos(c - 1))
                    x = PB[:, h, :]
                    if cross:
                        src = [x[:, P:2 * P], x[:, 0:P], x[:, 2 * P:3 * P], x[:, 3 * P:4 * P]]
                    else:
                        src = [x[:, j * P:(j + 1) * P] for j in range(3)]
                    for j, a in enumerate(src):
                        ins = e.transpose(pT[:, bank, j * P:(j + 1) * P], a, ident[:, :])
                    ins.then_inc(q["tr"], 1)

                def attend(i, s, h):
                    c, _ = use(i, "w", h, s)
                    e.wait_ge(q["te"], c + 1)
                    e.wait_ge(q["ot"], HG * i + h)
                    k0 = P if cross else 0
                    v = slice(0, HD) if cross else slice(h * HD, (h + 1) * HD)
                    if h == 0:
                        e.wait_ge(q["taken"], NQ * i + NQ)
                    e.matmul(pO[:, 0:S], V[:, s, 0, v], PT[:, h % 2, k0:k0 + S], start=True, stop=False)
                    ins = e.matmul(pO[:, P:S], V[:, s, 1, v], PT[:, h % 2, k0 + S:k0 + S + P],
                                   start=False, stop=not cross)
                    if cross:
                        e.wait_ge(q["vs"], i + 1)
                        for t in range(T):
                            ins = e.matmul(pO[:, t * P:(t + 1) * P], VS[:, s, t, :], PT[:, h % 2, 0:P],
                                           start=False, stop=(t == 1))
                    ins.then_inc(q["pv"], 1)

                def out_proj(i, s):
                    e.wait_ge(q["ot"], HG * i + HG)
                    e.wait_ge(q["split"], i)
                    e.wait_ge(q["acc"], i)
                    slot = (i // 8 + slot0) % 2
                    for t in range(T):
                        r = slice(t * P, (t + 1) * P)
                        for h in range(HG):
                            cc = slice(WO + h * D, WO + (h + 1) * D)
                            ins = three(e, pF[:, t * D:(t + 1) * D], OTh[:, s, h, r], OTl[:, s, h, r],
                                        Wh[:, ds(slot), cc], Wl[:, ds(slot), cc], h == 0, h == HG - 1)
                    ins.then_inc(q["f"], 1)

                def body(i, s, nxt):
                    n = 1 - s
                    if isfirst(i):
                        for k in range(NQ):
                            proj(0, 0, k)
                        for k in range(NT):
                            qk_tr(0, 0, k)
                        scores(0, 0, 0)
                    last = islast(i)
                    if not last:
                        j = i + 1
                    p_tr(i, s, 0)
                    scores(i, s, 1)
                    if not last:
                        proj(j, n, 0)
                    attend(i, s, 0)
                    if not last:
                        proj(j, n, 1)
                    p_tr(i, s, 1)
                    scores(i, s, 2)
                    if not last:
                        proj(j, n, 2)
                    attend(i, s, 1)
                    if not last:
                        proj(j, n, 3)
                    p_tr(i, s, 2)
                    scores(i, s, 3)
                    if not last and not cross:
                        proj(j, n, 4)
                    attend(i, s, 2)
                    if not last:
                        if not cross:
                            proj(j, n, 5)
                        qk_tr(j, n, 0)
                        if not cross:
                            qk_tr(j, n, 1)
                    p_tr(i, s, 3)
                    if not last:
                        for k in range(1 if cross else 2, NT):
                            qk_tr(j, n, k)
                    if not isfirst(i):
                        out_proj(i - 1, n)
                    attend(i, s, 3)
                    if not last:
                        scores(j, n, 0)
                    else:
                        out_proj(i, s)
                in_pairs(e, NI, body, 24)
                phase_end(e, name)

            def act(e):
                def qk_ev(i, s, n):
                    c, bank = use(i, "qk", n, s)
                    e.wait_ge(q["tr"], c + 1)
                    e.wait_ge(q["sc"], HG * i)
                    if cross and n == 2:
                        o, a = kT[:, 0, :], pT[:, bank, 0:S]
                    else:
                        x, t = (qT, n) if cross else ((kT if n % 2 else qT), n // 2)
                        o = x[:, :, t * P:(t + 1) * P]
                        a = pT[:, bank, :].rearrange("p (h n) -> p h n", h=HG)
                    e.activation(o, a, ACT.Copy).then_inc(q["te"], 1)

                def p_ev(i, s, h):
                    c, bank = use(i, "w", h, s)
                    e.wait_ge(q["tr"], c + 1)
                    e.wait_ge(q["pv"], pos(HG * i + h - 1))
                    e.activation(PT[:, h % 2, :], pT[:, bank, 0:SW], ACT.Copy).then_inc(q["te"], 1)

                def exp(i, s, h):
                    e.wait_ge(q["sct"], HG * i + h + 1)
                    if cross:
                        e.wait_ge(q["rs"], pos(HG * (i - 1) + h + 1))
                    for t in range(T):
                        x = PB[:, h, OFF[t]:OFF[t] + WID[t]]
                        ins = e.activation(x, x, ACT.Exp, scale=-1.0, bias=nm[:, h, t:t + 1],
                                           accum_out=sm[:, h, t:t + 1])
                    ins.then_inc(q["ex"], 1)

                def o_ev(i, s, h):
                    e.wait_ge(q["pv"], HG * i + h + 1)
                    e.wait_ge(q["f"], pos(i - 1))
                    e.activation(OTh[:, s, h, :], pO[:, 0:S], ACT.Copy).then_inc(q["oth"], 1)

                def q_ev(i, s, n):
                    t = n // 2
                    e.wait_ge(q["proj"], NQ * i + n + 1)
                    if n % 2 == 0:
                        e.wait_ge(q["rope"], pos(4 * (i - 1) + (1, 3)[t]))
                        e.wait_ge(q["sq"], pos(T * (i - 1) + t + 1))
                        e.activation(qb[:, t, :], pA[:, 0, :], ACT.Copy).then_inc(q["taken"], 1)
                    else:
                        e.wait_ge(q["k1"], pos(T * (i - 1) + t + 1))
                        e.wait_ge(q["sqk"], pos(T * (i - 1) + t + 1))
                        e.wait_ge(q["pv"], pos(HG * (i - 1)))
                        e.activation(kb[:, t, :], pA[:, 1, 0:HD], ACT.Copy)
                        e.activation(V[:, s, t, :], pA[:, 1, HD:2 * HD], ACT.Copy).then_inc(q["taken"], 1)

                def context_values(i, s):
                    e.wait_ge(q["pv"], pos(HG * (i - 1)))
                    for t in range(T):
                        k = slice(t * SC, (t + 1) * SC)
                        ins = e.activation(VS[k, s, t, :], VC[k, ds(i % 8), ds((i // 8) * HD, HD)]
                                           .rearrange("p a n -> p (a n)"), ACT.Copy)
                    ins.then_inc(q["vs"], 1)

                if cross:
                    e.wait_ge(q["vz"], 1)

                def body(i, s, nxt):
                    n, last = 1 - s, islast(i)
                    if isfirst(i):
                        if cross:
                            for k in range(NQ):
                                q_ev(0, 0, k)
                            context_values(0, 0)
                        for k in range(NT):
                            qk_ev(0, 0, k)
                        exp(0, 0, 0)
                    for h in range(3):
                        p_ev(i, s, h)
                        if cross and not last and h < 2:
                            q_ev(i + 1, n, 2 * h)
                        exp(i, s, h + 1)
                        if cross and not last and h < 2:
                            q_ev(i + 1, n, 2 * h + 1)
                        o_ev(i, s, h)
                    if not last:
                        for k in range(1 if cross else 2):
                            qk_ev(i + 1, n, k)
                    p_ev(i, s, 3)
                    if not last:
                        for k in range(1 if cross else 2, NT):
                            qk_ev(i + 1, n, k)
                    o_ev(i, s, 3)
                    if not last:
                        exp(i + 1, n, 0)
                        if cross:
                            context_values(i + 1, n)
                in_pairs(e, NI, body, 24)
                phase_end(e, name)

            def heads(x, swap=False):
                v = x.rearrange("p (h a d) -> p h a d", a=2, d=H2)
                return v[:, :, ::-1, :] if swap else v

            def table(x, t, n):
                return bc(x[:, t, :].rearrange("p (a d) -> p a d", a=2), 1, n)

            def dve(e):
                if cross:
                    e.wait_ge(q["const"], 64)
                    for j, (o, a, w) in enumerate(((cosk, cosT, 2), (sink, sinT, 3), (cosT, cosT, 0),
                                                   (sinT, sinT, 1))):
                        e.tensor_tensor(o[:, :, :], a[:, :, :], bc(wrow[:, w, :], 1, T), ALU.mult
                                        ).then_inc(q["table"], 1)
                        e.wait_ge(q["table"], j + 1)
                else:
                    e.wait_ge(q["const"], 64)

                def take(i, s, n):
                    t, g = (n // 2 if n < 4 else n - 4), i // 8
                    e.wait_ge(q["proj"], NQ * i + n + 1)
                    if n < 4:
                        b = n % 2
                        e.wait_ge(q["rc"], pos(4 * i + n - 1))
                        e.tensor_tensor(qb[:, b, :], pA[:, b, :],
                                        bias[:, ds(g), n % 2, :].rearrange("p a n -> p (a n)"), ALU.add
                                        ).then_inc(q["taken"], 1)
                        e.wait_ge(q["taken"], NQ * i + n + 1)
                        e.wait_ge(q["rope"], pos(4 * i + n - 1))
                        e.tensor_tensor(heads(t2[:, b, :]), heads(qb[:, b, :], True), table(sinT, t, HG),
                                        ALU.mult).then_inc(q["rot"], 1)
                    else:
                        e.wait_ge(q["pv"], pos(HG * (i - 1)))
                        e.tensor_tensor(V[:, s, t, :], pA[:, n % 2, :],
                                        bias[:, ds(g), 2, :].rearrange("p a n -> p (a n)"), ALU.add
                                        ).then_inc(q["taken"], 1)

                def rotate_q(i, s, t):
                    e.wait_ge(q["sq"], T * i + t + 1)
                    if t == 0:
                        e.wait_ge(q["rqa"], i)
                    e.tensor_reduce(ssq[:, t, :], sq[:, :].rearrange("p (h d) -> p h d", h=HG), AX.X,
                                    ALU.add).then_inc(q["ssq"], 1)
                    e.wait_ge(q["rope"], pos(4 * (i - 1) + (1, 3)[t]))
                    e.tensor_tensor(heads(t2[:, t, :]), heads(qb[:, t, :], True), table(sinT, t, HG),
                                    ALU.mult).then_inc(q["rot"], 1)

                def rotate_k(i, s, t):
                    e.wait_ge(q["sqk"], T * i + t + 1)
                    e.wait_ge(q["rk"], T * i + t)
                    e.tensor_reduce(ssk[:, t:t + 1], sqk[:, :], AX.X, ALU.add).then_inc(q["ssk"], 1)
                    e.wait_ge(q["rk"], T * i + t + 1)
                    e.wait_ge(q["rope"], pos(4 * (i - 1) + 4))
                    c, _ = use(i, "qk", 2, s)
                    if not isfirst(i):
                        p, _ = use(i - 1, "qk", 2, 1 - s) if not (isinstance(i, int) and i == 1) else use(0, "qk", 2, 0)
                        e.wait_ge(q["tr"], p + 1)
                    r = ssk[:, t:t + 1]
                    o = heads(KR[:, t, :]).rearrange("p h a d -> p (h a) d")
                    kv = heads(kb[:, t, :]).rearrange("p h a d -> p (h a) d")
                    e.scalar_tensor_tensor(o, kv, r, cosk[:, t, :].rearrange("p (a d) -> p a d", a=2),
                                           ALU.mult, ALU.mult)
                    e.scalar_tensor_tensor(tk[:, t, :].rearrange("p (a d) -> p a d", a=2), kv[:, ::-1, :], r,
                                           sink[:, t, :].rearrange("p (a d) -> p a d", a=2),
                                           ALU.mult, ALU.mult).then_inc(q["k1"], 1)

                def soft(i, s, h):
                    c, _ = use(i, "w", h, s)
                    e.wait_ge(q["sc"], HG * i + h + 1)
                    if cross and h == 0:
                        e.wait_ge(q["rq"], i + 1)
                    if not isfirst(i):
                        pi = i - 1
                        p, _ = use(pi, "w", h, 1 - s)
                        e.wait_ge(q["tr"], p + 1)
                        apart(e, p + 1)
                    for t in range(T):
                        x = slice(OFF[t], OFF[t] + WID[t])
                        scale = nrq[:, t, h:h + 1] if cross else -float(HD) ** -0.5
                        ins = e.tensor_tensor_reduce(PB[:, h, x], pS[:, h % 2, x], mask[:, x], scale, 1e38,
                                                     ALU.add, ALU.min, nm[:, h, t:t + 1])
                    ins.then_inc(q["sct"], 1)

                def recip(i, h):
                    e.wait_ge(q["ex"], HG * i + h + 1)
                    e.wait_ge(q["pn"], pos(HG * (i - 1) + h + 1))
                    e.reciprocal(rs[:, h, :], sm[:, h, :]).then_inc(q["rs"], 1)

                def o_low(i, s, h):
                    e.wait_ge(q["oth"], HG * i + h + 1)
                    e.tensor_tensor(OTl[:, s, h, :], pO[:, 0:S], OTh[:, s, h, :].bitcast(F32), ALU.subtract
                                    ).then_inc(q["ot"], 1)

                def add_out(i):
                    e.wait_ge(q["f"], i + 1)
                    e.wait_ge(q["acc"], i)
                    r = R[:, ds(T * (i % 8), T), :]
                    o = pF[:, :].rearrange("p (t n) -> p t n", t=T)
                    if cross:
                        e.scalar_tensor_tensor(r, o, tanhg[:, 2:3], r, ALU.mult, ALU.add).then_inc(q["acc"], 1)
                    else:
                        e.tensor_tensor(r, o, r, ALU.add).then_inc(q["acc"], 1)

                def part(i, s, n):
                    if cross:
                        if n % 2 == 0:
                            rotate_q(i, s, n // 2)
                        else:
                            rotate_k(i, s, n // 2)
                    else:
                        take(i, s, n)

                def body(i, s, nxt):
                    n, last = 1 - s, islast(i)
                    if isfirst(i):
                        for k in range(NQ):
                            part(0, 0, k)
                        soft(0, 0, 0)
                        recip(0, 0)
                    for h in range(3):
                        soft(i, s, h + 1)
                        if not last and (h < 2 or not cross):
                            part(i + 1, n, 2 * h)
                        recip(i, h + 1)
                        o_low(i, s, h)
                        if not last and (h < 2 or not cross):
                            part(i + 1, n, 2 * h + 1)
                    if not isfirst(i):
                        add_out(i - 1)
                    o_low(i, s, 3)
                    if not last:
                        soft(i + 1, n, 0)
                        recip(i + 1, 0)
                    else:
                        add_out(i)
                in_pairs(e, NI, body, 24)
                phase_end(e, name)

            def pool(e):
                if cross:
                    e.memset(VS[:, :, :, :], 0.0).then_inc(q["vz"], 1)
                    e.wait_ge(q["table"], 4)
                else:
                    e.wait_ge(q["const"], 64)

                def xs(i, s):
                    e.wait_ge(q["proj"], pos(NQ * (i - 1)))
                    apart(e, NQ * (i - 1))
                    copy_x(e, s, i, q["xs"], q["xhi"])

                def rotate(i, s, n):
                    x = (KR if n % 2 else QR)[:, n // 2, :]
                    e.wait_ge(q["taken"], NQ * i + n + 1)
                    apart(e, NQ * i + n + 1)
                    if not isfirst(i):
                        p, _ = use(i - 1, "qk", n, 1 - s) if not (isinstance(i, int) and i == 1) else use(0, "qk", n, 0)
                        e.wait_ge(q["tr"], p + 1)
                        apart(e, p + 1)
                    e.tensor_tensor(heads(x), heads(qb[:, n % 2, :]), table(cosT, n // 2, HG), ALU.mult
                                    ).then_inc(q["rc"], 1)
                    e.wait_ge(q["rc"], 4 * i + n + 1)
                    apart(e, 4 * i + n + 1)
                    e.wait_ge(q["rot"], 4 * i + n + 1)
                    apart(e, 4 * i + n + 1)
                    e.tensor_tensor(x, x, t2[:, n % 2, :], ALU.add).then_inc(q["rope"], 1)

                def rotate_q(i, s, t):
                    e.wait_ge(q["taken"], NQ * i + 2 * t + 1)
                    apart(e, NQ * i + 2 * t + 1)
                    e.wait_ge(q["ssq"], T * i + t)
                    apart(e, T * i + t)
                    e.tensor_tensor(sq[:, :], qb[:, t, :], qb[:, t, :], ALU.mult).then_inc(q["sq"], 1)
                    x = QR[:, t, :]
                    if not isfirst(i):
                        p, _ = use(i - 1, "qk", t, 1 - s) if not (isinstance(i, int) and i == 1) else use(0, "qk", t, 0)
                        e.wait_ge(q["tr"], p + 1)
                        apart(e, p + 1)
                    e.tensor_tensor(heads(x), heads(qb[:, t, :]), table(cosT, t, HG), ALU.mult
                                    ).then_inc(q["rc"], 1)
                    e.wait_ge(q["rc"], T * i + t + 1)
                    apart(e, T * i + t + 1)
                    e.wait_ge(q["rot"], T * i + t + 1)
                    apart(e, T * i + t + 1)
                    e.tensor_tensor(x, x, t2[:, t, :], ALU.add).then_inc(q["rope"], 1)

                def rotate_k(i, s, t):
                    e.wait_ge(q["taken"], NQ * i + 2 * t + 2)
                    apart(e, NQ * i + 2 * t + 2)
                    e.wait_ge(q["ssk"], T * i + t)
                    apart(e, T * i + t)
                    e.tensor_tensor(sqk[:, :], kb[:, t, :], kb[:, t, :], ALU.mult).then_inc(q["sqk"], 1)
                    e.wait_ge(q["ssk"], T * i + t + 1)
                    apart(e, T * i + t + 1)
                    r = ssk[:, t:t + 1]
                    e.tensor_scalar(r, r, 1.0 / HD, 1e-6, ALU.mult, ALU.add).then_inc(q["rka"], 1)
                    e.wait_ge(q["rka"], T * i + t + 1)
                    apart(e, T * i + t + 1)
                    e.tensor_tensor(r, r, mhalf[:, 0:1], ALU.pow).then_inc(q["rk"], 1)
                    e.wait_ge(q["k1"], T * i + t + 1)
                    apart(e, T * i + t + 1)
                    e.tensor_tensor(KR[:, t, :], KR[:, t, :], tk[:, t, :], ALU.add).then_inc(q["rope"], 1)

                def inverse_norms(i):
                    e.wait_ge(q["ssq"], T * i + T)
                    apart(e, T * i + T)
                    e.wait_ge(q["sct"], HG * i)
                    apart(e, HG * i)
                    a = nrq[:, :, :].rearrange("p t h -> p (t h)")
                    e.tensor_scalar(a, ssq[:, :, :].rearrange("p t h -> p (t h)"), HD * 1e-6, None, ALU.add
                                    ).then_inc(q["rqa"], 1)
                    e.wait_ge(q["rqa"], i + 1)
                    apart(e, i + 1)
                    e.tensor_tensor(a, a, mhalf[:, :], ALU.pow).then_inc(q["rqb"], 1)
                    e.wait_ge(q["rqb"], i + 1)
                    apart(e, i + 1)
                    e.tensor_scalar(a, a, -1.0, None, ALU.mult).then_inc(q["rq"], 1)

                def normalise(i, h):
                    e.wait_ge(q["rs"], HG * i + h + 1)
                    apart(e, HG * i + h + 1)
                    for t in range(T):
                        x = PB[:, h, OFF[t]:OFF[t] + WID[t]]
                        ins = e.tensor_scalar(x, x, rs[:, h, t:t + 1], None, ALU.mult)
                    ins.then_inc(q["pn"], 1)

                def part(i, s, n):
                    if not cross:
                        rotate(i, s, n)
                    elif n % 2 == 0:
                        rotate_q(i, s, n // 2)
                    else:
                        rotate_k(i, s, n // 2)

                def body(i, s, nxt):
                    n, last = 1 - s, islast(i)
                    if isfirst(i):
                        xs(0, 0)
                        for k in range(4):
                            part(0, 0, k)
                        if cross:
                            inverse_norms(0)
                        xs(1, 1)
                        normalise(0, 0)
                    if not last:
                        part(i + 1, n, 0)
                    normalise(i, 1)
                    if not last:
                        part(i + 1, n, 1)
                        part(i + 1, n, 2)
                    normalise(i, 2)
                    if not last:
                        part(i + 1, n, 3)
                        if cross:
                            e.wait_ge(q["sct"], HG * i + 4)
                            apart(e, HG * i + 4)
                            inverse_norms(i + 1)
                    normalise(i, 3)
                    e.wait_ge(q["proj"], NQ * i)
                    apart(e, NQ * i)
                    e.wait_ge(q["f"], pos(i - 1))
                    apart(e, i - 1)
                    if nxt:
                        split(e, raw_in, q["hi"], q["split"], cw_next, i, s, slot0)
                    else:
                        split(e, raw_in, q["hi"], q["split"], cw_here, i, s, (i // 8 + 1 + slot0) % 2)
                    if not (isinstance(i, int) and i >= NI - 2):
                        xs(i + 2, s)
                    if not last:
                        normalise(i + 1, 0)
                in_pairs(e, NI, body, 24)
                phase_end(e, name)

            close_phase(name)
            return Phase(sp, pool, act, dve, pe)

        if stop >= 2:
            lnp = sb("lnp", [P, 4, KD])
            s_lnp, s_sp = sem("s_lnp"), sem("s_spill")
            sc_bo = ExitStack()
            bo = sb("bo", [P, D], F32, sc_bo)

            def ln_sp(e):
                for j, n in enumerate(("ln1_w", "ln1_b", "ln2_w", "ln2_b")):
                    e.dma_start(lnp[:, j, :], d["f0_" + n]).then_inc(s_lnp, 16)
                e.dma_start(bo[:, :], d["f0_bo"].partition_broadcast(P)).then_inc(s_lnp, 16)
                e.dma_start(spill, R[:, :, :]).then_inc(s_sp, 16)

            def ln_wait(e):
                e.wait_ge(s_lnp, 80)
                e.wait_ge(s_sp, 16)

            n1 = layer_norm("n1", double=True, affine=(lnp[:, 0, :], lnp[:, 1, :]), after=bo)
            sc_bo.close()
            f0 = ExitStack()
            self0 = causal_attention("f0", f0, False, d["w_f0"], CW_F0, d["w_moe"], CW_MOE, 0)
            f0.close()

        def experts(scope):
            name = "moe"
            NM = D // P
            W2 = E * KD * D
            wg = sb("moe_wg", [P, KD, E], F32, scope)
            be1 = sb("moe_be1", [P, E * NM], F32, scope)
            be2 = sb("moe_be2", [P, E, D], F32, scope)
            before = sb("moe_before", [P, E, E], F32, scope)
            xc = sb("moe_x", [P, 2, KD, S], F32, scope)
            xsp = sb("moe_xs", [P, 2, T, D], F32, scope)
            HM = sb("moe_h", [P, 2, NM, S], F32, scope)
            HMh = sb("moe_hh", [P, 2, NM, S], F32R, scope)
            HMl = sb("moe_hl", [P, 2, NM, S], F32R, scope)
            lg = sb("moe_lg", [P, T, E], F32, scope)
            mx = sb("moe_mx", [P, T, 1], F32, scope)
            sm = sb("moe_sm", [P, T, 1], F32, scope)
            cmp = sb("moe_cmp", [P, T, E, E], F32, scope)
            eq = sb("moe_eq", [P, T, E, E], F32, scope)
            rank = sb("moe_rank", [P, T, E], F32, scope)
            is0 = sb("moe_is0", [P, T, E], F32, scope)
            is1 = sb("moe_is1", [P, T, E], F32, scope)
            tmp = sb("moe_tmp", [P, T, E], F32, scope)
            v2 = sb("moe_v2", [P, T, 1], F32, scope)
            w1 = sb("moe_w1", [P, T, 1], F32, scope)
            w2 = sb("moe_w2", [P, T, 1], F32, scope)
            comb = sb("moe_comb", [P, T, E], F32, scope)
            q = {x: sem("moe_" + x) for x in
                 ("raw0", "raw1", "hi", "split", "const", "xc", "xhi", "xs", "lg", "l1", "ex", "v", "cb",
                  "up", "ge", "hhi", "hlo", "dn", "dt", "acc", "spl0", "spl1", "y", "e2")}
            raw_in = [q["raw0"], q["raw1"]]
            spl = [q["spl0"], q["spl1"]]

            def sp(e):
                e.dma_start(wg[:, :, :].rearrange("p k e -> p (k e)"), d["w_gate"]).then_inc(q["const"], 16)
                e.dma_start(be1[:, :], d["be1"]).then_inc(q["const"], 16)
                e.dma_start(be2[:, :, :].rearrange("p e n -> p (e n)"),
                            d["be2"].partition_broadcast(P)).then_inc(q["const"], 16)
                e.dma_start(before[:, :, :].rearrange("p e n -> p (e n)"),
                            d["earlier"].partition_broadcast(P)).then_inc(q["const"], 16)

                def body(i, s, _):
                    e.wait_ge(q["y"], pos(i - 1))
                    e.dma_start(xsp[:, s], spill[:, ds(T * i, T), :]).then_inc(spl[s], 16)
                    stream_sp(e, raw_in, q["split"], d["w_x1"], CW_X1, i, s)
                in_pairs(e, B, body)
                phase_end(e, name)

            def pe(e):
                e.wait_ge(q["const"], 64)

                def gate(i, s):
                    e.wait_ge(q["xs"], i + 1)
                    e.wait_ge(q["l1"], i)
                    for t in range(T):
                        for k in range(KD):
                            ins = e.matmul(pT[:, 0, t * E:(t + 1) * E], xc[:, s, k, t * P:(t + 1) * P],
                                           wg[:, k, :], start=(k == 0), stop=(k == KD - 1))
                    ins.then_inc(q["lg"], 1)

                def up(i, s, x):
                    c = E * i + x
                    e.wait_ge(q["ge"], pos(c - 1))
                    for m in range(NM):
                        for k in range(KD):
                            w = slice((x * KD + k) * D + m * P, (x * KD + k) * D + (m + 1) * P)
                            o = pA[:, x % 2, m * S:(m + 1) * S]
                            e.matmul(o, Wh[:, 0, w], XSh[:, s, k, :], start=(k == 0), stop=False)
                            e.matmul(o, Wh[:, 0, w], XSl[:, s, k, :], start=False, stop=False)
                            ins = e.matmul(o, Wl[:, 0, w], XSh[:, s, k, :], start=False, stop=(k == KD - 1))
                    ins.then_inc(q["up"], 1)

                def down(i, x):
                    c = E * i + x
                    e.wait_ge(q["hlo"], c + 1)
                    e.wait_ge(q["dt"], pos(c - 1))
                    for t in range(T):
                        r = slice(t * P, (t + 1) * P)
                        for k in range(NM):
                            w = slice(W2 + (x * NM + k) * D, W2 + (x * NM + k + 1) * D)
                            ins = three(e, pS[:, x % 2, t * D:(t + 1) * D], HMh[:, x % 2, k, r],
                                        HMl[:, x % 2, k, r], Wh[:, 0, w], Wl[:, 0, w], k == 0, k == NM - 1)
                    ins.then_inc(q["dn"], 1)

                def body(i, s, _):
                    if isinstance(i, int) and i == 0:
                        gate(0, 0)
                        up(0, 0, 0)
                        up(0, 0, 1)
                    last = isinstance(i, int) and i == B - 1
                    for x in range(E):
                        down_next = None
                        if x < 2:
                            up_args = (i, s, x + 2)
                            up(*up_args)
                        elif not last:
                            if x == 2:
                                gate(i + 1, 1 - s)
                            up(i + 1, 1 - s, x - 2)
                        down(i, x)
                in_pairs(e, B, body)
                phase_end(e, name)

            def act(e):
                def gelu(i, s, x):
                    c = E * i + x
                    e.wait_ge(q["up"], c + 1)
                    e.wait_ge(q["hlo"], pos(c - 1))
                    for m in range(NM):
                        ins = e.activation(HM[:, x % 2, m, :], pA[:, x % 2, m * S:(m + 1) * S], ACT.Gelu,
                                           bias=be1[:, x * NM + m:x * NM + m + 1])
                    ins.then_inc(q["ge"], 1)

                e.wait_ge(q["const"], 64)

                def exps(i):
                    e.wait_ge(q["v"], GV * i + 2)
                    e.activation(lg[:, :, :], lg[:, :, :], ACT.Exp).then_inc(q["ex"], 1)
                    e.wait_ge(q["v"], GV * i + 9)
                    e.activation(v2[:, :, :], v2[:, :, :], ACT.Exp).then_inc(q["ex"], 1)

                def body(i, s, _):
                    exps(i)
                    for x in range(E):
                        gelu(i, s, x)
                in_pairs(e, B, body)
                phase_end(e, name)

            GV = 14

            def dve(e):
                e.wait_ge(q["const"], 64)

                def step(i, n, ins):
                    ins.then_inc(q["v"], 1)
                    e.wait_ge(q["v"], GV * i + n)

                def gates(i):
                    e.wait_ge(q["lg"], i + 1)
                    e.wait_ge(q["ex"], 2 * i)
                    ps = pT[:, 0, 0:T * E].rearrange("p (t e) -> p t e", t=T)
                    step(i, 1, e.tensor_reduce(mx[:, :, 0], ps, AX.X, ALU.max))
                    e.tensor_tensor(lg[:, :, :], ps, mx[:, :, :].to_broadcast([P, T, E]), ALU.subtract
                                    ).then_inc(q["l1"], 1)
                    e.wait_ge(q["l1"], i + 1)
                    step(i, 2, e.tensor_copy(tmp[:, :, :], lg[:, :, :]))
                    e.wait_ge(q["ex"], 2 * i + 1)
                    step(i, 3, e.tensor_reduce(sm[:, :, 0], lg[:, :, :], AX.X, ALU.add))
                    step(i, 4, e.reciprocal(sm[:, :, :], sm[:, :, :]))
                    step(i, 5, e.tensor_tensor(lg[:, :, :], lg[:, :, :], sm[:, :, :].to_broadcast([P, T, E]),
                                               ALU.mult))
                    for t in range(T):
                        mine = lg[:, t, :].unsqueeze(2).to_broadcast([P, E, E])
                        other = lg[:, t, :].unsqueeze(1).to_broadcast([P, E, E])
                        e.tensor_tensor(cmp[:, t], other, mine, ALU.is_gt)
                        ins = e.tensor_tensor(eq[:, t], other, mine, ALU.is_equal)
                    step(i, 6, ins)
                    for t in range(T):
                        ins = e.tensor_tensor(eq[:, t], eq[:, t], before[:, :, :], ALU.mult)
                    step(i, 7, ins)
                    ins = e.tensor_tensor(cmp[:, :, :, :], cmp[:, :, :, :], eq[:, :, :, :], ALU.add)
                    ins.then_inc(q["l2"], 1)
                    e.wait_ge(q["l2"], i + 1)
                    e.tensor_reduce(rank[:, :, :], cmp[:, :, :, :], AX.X, ALU.add).then_inc(q["l3"], 1)
                    e.wait_ge(q["l3"], i + 1)
                    e.wait_ge(q["dt"], E * i)
                    e.wait_ge(q["e2"], E * i)
                    e.tensor_scalar(is0[:, :, :], rank[:, :, :], 0.0, None, ALU.is_equal)
                    e.tensor_scalar(is1[:, :, :], rank[:, :, :], 1.0, None, ALU.is_equal).then_inc(q["l4"], 1)
                    e.wait_ge(q["l4"], i + 1)
                    step(i, 8, e.tensor_tensor(tmp[:, :, :], is1[:, :, :], lg[:, :, :], ALU.mult))
                    e.tensor_reduce(v2[:, :, 0], tmp[:, :, :], AX.X, ALU.add)
                    e.tensor_reduce(w1[:, :, 0], lg[:, :, :], AX.X, ALU.max).then_inc(q["l5"], 1)
                    e.wait_ge(q["l5"], i + 1)
                    step(i, 9, e.tensor_tensor(v2[:, :, :], v2[:, :, :], w1[:, :, :], ALU.subtract))
                    e.wait_ge(q["ex"], 2 * i + 2)
                    step(i, 10, e.tensor_scalar(w1[:, :, :], v2[:, :, :], 1.0, None, ALU.add))
                    step(i, 11, e.reciprocal(w1[:, :, :], w1[:, :, :]))
                    step(i, 12, e.tensor_tensor(w2[:, :, :], v2[:, :, :], w1[:, :, :], ALU.mult))
                    e.tensor_tensor(is0[:, :, :], is0[:, :, :], w1[:, :, :].to_broadcast([P, T, E]), ALU.mult)
                    step(i, 13, e.tensor_tensor(is1[:, :, :], is1[:, :, :], w2[:, :, :].to_broadcast([P, T, E]),
                                                ALU.mult))
                    step(i, 14, e.tensor_tensor(comb[:, :, :], is0[:, :, :], is1[:, :, :], ALU.add))

                def low(i, x):
                    c = E * i + x
                    e.wait_ge(q["hhi"], c + 1)
                    e.tensor_tensor(HMl[:, x % 2], HM[:, x % 2], HMh[:, x % 2].bitcast(F32), ALU.subtract
                                    ).then_inc(q["hlo"], 1)

                def combine(i, s, x):
                    c = E * i + x
                    e.wait_ge(q["dn"], c + 1)
                    e.wait_ge(q["e2"], c + 1)
                    for t in range(T):
                        r = R[:, ds(T * i + t), :].rearrange("p a n -> p (a n)")
                        ins = e.scalar_tensor_tensor(r, pS[:, x % 2, t * D:(t + 1) * D], comb[:, t, x:x + 1],
                                                     r, ALU.mult, ALU.add)
                    ins.then_inc(q["dt"], 1)
                    e.wait_ge(q["dt"], c + 1)

                def body(i, s, _):
                    gates(i)
                    for x in range(E):
                        low(i, x)
                        if x:
                            combine(i, s, x - 1)
                    combine(i, s, E - 1)
                    e.wait_ge(spl[s], 16 * (i // 2 + 1))
                    r = R[:, ds(T * i, T), :]
                    e.scalar_tensor_tensor(r, r, tanhg[:, 1:2], xsp[:, s], ALU.mult, ALU.add
                                           ).then_inc(q["y"], 1)
                in_pairs(e, B, body)
                phase_end(e, name)

            q.update({x: sem("moe_" + x) for x in ("l2", "l3", "l4", "l5")})
            tb = sb("moe_tb", [P, T, D], F32, scope)

            def pool(e):
                e.wait_ge(q["const"], 64)

                def xs(i, s):
                    src = XT[:, :, ds(i * S, S)]
                    e.wait_ge(q["up"], pos(E * (i - 1)))
                    apart(e, E * (i - 1))
                    e.wait_ge(q["lg"], pos(i - 1))
                    apart(e, i - 1)
                    e.tensor_copy(xc[:, s], src)
                    copy_x(e, s, i, q["xs"], q["xhi"])

                def high(i, x):
                    c = E * i + x
                    e.wait_ge(q["ge"], c + 1)
                    apart(e, c + 1)
                    e.wait_ge(q["dn"], pos(c - 1))
                    apart(e, c - 1)
                    e.tensor_copy(HMh[:, x % 2], HM[:, x % 2]).then_inc(q["hhi"], 1)

                def biases(i, x):
                    c = E * i + x
                    e.wait_ge(q["v"], GV * i + GV)
                    apart(e, GV * i + GV)
                    e.wait_ge(q["dt"], c)
                    apart(e, c)
                    for t in range(T):
                        ins = e.tensor_scalar(tb[:, t, :], be2[:, x, :], comb[:, t, x:x + 1], None, ALU.mult)
                    ins.then_inc(q["cb"], 1)
                    e.wait_ge(q["cb"], c + 1)
                    apart(e, c + 1)
                    r = R[:, ds(T * i, T), :]
                    e.tensor_tensor(r, r, tb[:, :, :], ALU.add).then_inc(q["e2"], 1)
                    e.wait_ge(q["e2"], c + 1)
                    apart(e, c + 1)

                def body(i, s, _):
                    if isinstance(i, int) and i == 0:
                        xs(0, 0)
                        xs(1, 1)
                    for x in range(E):
                        high(i, x)
                        biases(i, x)
                    split(e, raw_in, q["hi"], q["split"], CW_X1, i, s, 1)
                    if not (isinstance(i, int) and i >= B - 2):
                        xs(i + 2, s)
                in_pairs(e, B, body)
                phase_end(e, name)

            close_phase(name)
            return Phase(sp, pool, act, dve, pe)

        if stop >= 3:
            n2 = layer_norm("n2", affine=(lnp[:, 2, :], lnp[:, 3, :]))
            sc_moe = ExitStack()
            moe = experts(sc_moe)
            sc_moe.close()

        if stop >= 4:
            x1 = ExitStack()
            KT1 = sb("x1_KT", [P, NKV, B * SC], F32, x1)
            VC1 = sb("x1_VC", [P, B, NKV * HD], F32, x1)
            kn = sb("x1_kn", [P, 1], F32, x1)
            s_kn = sem("x1_kn")
            with ExitStack() as tmp:
                context1 = context("c1", tmp, d["x1_Wk"], d["x1_Wv"], KT1, kn, VC=VC1)
            n3 = layer_norm("n3")
            cross1 = causal_attention("x1", x1, True, d["w_x1"], CW_X1, d["w_ff"], CW_FF, 1, KT=KT1, VC=VC1)
            x1.close()

        def feed_forward(scope):
            name = "ff"
            WU, WD = KD * FW, 2 * KD * FW
            gs = sb("ff_gs", [P, FM], F32, scope)
            us = sb("ff_us", [P, FM], F32, scope)
            dsc = sb("ff_ds", [P, D], F32, scope)
            act_g = sb("ff_g", [P, 2, S], F32, scope)
            HDf = sb("ff_h", [P, 2, S], F32, scope)
            HDh = sb("ff_hh", [P, 2, FM, S], F32R, scope)
            HDl = sb("ff_hl", [P, 2, FM, S], F32R, scope)
            y = sb("ff_y", [P, T, D], F32, scope)
            q = {x: sem("ff_" + x) for x in ("const", "ds", "xhi", "xs", "gu", "g", "h", "hh", "hl", "f", "y",
                                            "acc")}

            def sp(e):
                e.dma_start(gs[:, :], d["ff_gs"]).then_inc(q["const"], 16)
                e.dma_start(us[:, :], d["ff_us"]).then_inc(q["const"], 16)
                e.dma_start(dsc[:, :], d["ff_ds"].partition_broadcast(P)).then_inc(q["const"], 16)

                def body(i, s, _):
                    e.wait_ge(q["acc"], i + 1)
                    e.dma_start(out[ds(i)].rearrange("b (t p) n -> p (b t) n", p=P), R[:, ds(T * i, T), :]
                                ).then_inc(out_done, 16)
                in_pairs(e, B, body)
                e.wait_ge(out_done, 16 * B)

            def pe(e):
                def up(i, s, m):
                    c = FM * i + m
                    e.wait_ge(q["xs"], i + 1)
                    e.wait_ge(q["h"], pos(c - 1))
                    for j, at in ((0, 0), (1, WU)):
                        o = pA[:, m % 2, j * S:(j + 1) * S]
                        for k in range(KD):
                            w = slice(at + k * FW + m * P, at + k * FW + (m + 1) * P)
                            e.matmul(o, Wh[:, 1, w], XSh[:, s, k, :], start=(k == 0), stop=False)
                            e.matmul(o, Wh[:, 1, w], XSl[:, s, k, :], start=False, stop=False)
                            ins = e.matmul(o, Wl[:, 1, w], XSh[:, s, k, :], start=False, stop=(k == KD - 1))
                    ins.then_inc(q["gu"], 1)

                def down(i, s):
                    e.wait_ge(q["hl"], FM * i + FM)
                    e.wait_ge(q["y"], i)
                    for t in range(T):
                        r = slice(t * P, (t + 1) * P)
                        for k in range(FM):
                            w = slice(WD + k * D, WD + (k + 1) * D)
                            ins = three(e, pF[:, t * D:(t + 1) * D], HDh[:, s, k, r], HDl[:, s, k, r],
                                        Wh[:, 1, w], Wl[:, 1, w], k == 0, k == FM - 1)
                    ins.then_inc(q["f"], 1)

                def body(i, s, _):
                    for m in range(FM):
                        up(i, s, m)
                        if m == 1 and not (isinstance(i, int) and i == 0):
                            down(i - 1, 1 - s)
                    if isinstance(i, int) and i == B - 1:
                        down(i, s)
                in_pairs(e, B, body)

            def act(e):
                e.wait_ge(q["const"], 48)

                def body(i, s, _):
                    for m in range(FM):
                        c = FM * i + m
                        e.wait_ge(q["gu"], c + 1)
                        e.wait_ge(q["h"], pos(c - 1))
                        e.activation(act_g[:, m % 2, :], pA[:, m % 2, 0:S], ACT.Silu, scale=gs[:, m:m + 1]
                                     ).then_inc(q["g"], 1)
                in_pairs(e, B, body)

            def dve(e):
                e.wait_ge(q["const"], 48)
                e.tensor_scalar(dsc[:, :], dsc[:, :], tanhg[:, 3:4], None, ALU.mult).then_inc(q["ds"], 1)
                e.wait_ge(q["ds"], 1)

                def result(i):
                    e.wait_ge(q["f"], i + 1)
                    e.wait_ge(q["acc"], i)
                    e.tensor_tensor(y[:, :, :], pF[:, :].rearrange("p (t n) -> p t n", t=T),
                                    bc(dsc[:, :], 1, T), ALU.mult).then_inc(q["y"], 1)

                def body(i, s, _):
                    for m in range(FM):
                        c = FM * i + m
                        e.wait_ge(q["g"], c + 1)
                        e.wait_ge(q["hl"], pos(c - 1))
                        e.scalar_tensor_tensor(HDf[:, m % 2, :], pA[:, m % 2, S:2 * S], us[:, m:m + 1],
                                               act_g[:, m % 2, :], ALU.mult, ALU.mult).then_inc(q["h"], 1)
                        if m == 3 and not (isinstance(i, int) and i == 0):
                            result(i - 1)
                    if isinstance(i, int) and i == B - 1:
                        result(i)
                in_pairs(e, B, body)

            def pool(e):
                def xs(i, s):
                    e.wait_ge(q["gu"], pos(FM * (i - 1)))
                    apart(e, FM * (i - 1))
                    copy_x(e, s, i, q["xs"], q["xhi"])

                def add(i):
                    e.wait_ge(q["y"], i + 1)
                    apart(e, i + 1)
                    r = R[:, ds(T * i, T), :]
                    e.tensor_tensor(r, r, y[:, :, :], ALU.add).then_inc(q["acc"], 1)

                def body(i, s, _):
                    if isinstance(i, int) and i == 0:
                        xs(0, 0)
                        xs(1, 1)
                    for m in range(FM):
                        c = FM * i + m
                        e.wait_ge(q["h"], c + 1)
                        apart(e, c + 1)
                        e.wait_ge(q["f"], pos(i - 1))
                        apart(e, i - 1)
                        e.tensor_copy(HDh[:, s, m, :], HDf[:, m % 2, :]).then_inc(q["hh"], 1)
                        e.wait_ge(q["hh"], c + 1)
                        apart(e, c + 1)
                        e.tensor_tensor(HDl[:, s, m, :], HDf[:, m % 2, :], HDh[:, s, m, :].bitcast(F32),
                                        ALU.subtract).then_inc(q["hl"], 1)
                        if m == 4 and not (isinstance(i, int) and i == 0):
                            add(i - 1)
                    if not (isinstance(i, int) and i >= B - 2):
                        xs(i + 2, s)
                    if isinstance(i, int) and i == B - 1:
                        add(i)
                in_pairs(e, B, body)

            close_phase(name)
            return Phase(sp, pool, act, dve, pe)

        if stop >= 5:
            n4 = layer_norm("n4")
            sc_ff = ExitStack()
            ffn1 = feed_forward(sc_ff)
            sc_ff.close()

        def dump_sp(sp):
            sp.dma_start(out.rearrange("b (t p) n -> p (b t) n", p=P), R[:, :, :]).then_inc(out_done, 16)
            sp.wait_ge(out_done, 16)

        block = ctx.enter_context(nc.Block())

        @block.sync
        def _(sp):
            init_sp(sp)
            init_all(sp)
            pre0.sync(sp)
            context0.sync(sp)
            n0.sync(sp)
            cross0.sync(sp)
            if stop >= 2:
                ln_sp(sp)
                n1.sync(sp)
                self0.sync(sp)
            if stop >= 3:
                n2.sync(sp)
                moe.sync(sp)
            if stop >= 4:
                sp.dma_start(kn[:, :], d["x1_kn"]).then_inc(s_kn, 16)
                context1.sync(sp)
                n3.sync(sp)
                cross1.sync(sp)
            if stop >= 5:
                n4.sync(sp)
                ffn1.sync(sp)
            if stop < 99:
                dump_sp(sp)

        @block.gpsimd
        def _(pool):
            init_pool(pool)
            init_all(pool)
            context0.gpsimd(pool)
            n0.gpsimd(pool)
            cross0.gpsimd(pool)
            if stop >= 2:
                ln_wait(pool)
                n1.gpsimd(pool)
                self0.gpsimd(pool)
            if stop >= 3:
                n2.gpsimd(pool)
                moe.gpsimd(pool)
            if stop >= 4:
                context1.gpsimd(pool)
                n3.gpsimd(pool)
                cross1.gpsimd(pool)
            if stop >= 5:
                n4.gpsimd(pool)
                ffn1.gpsimd(pool)

        @block.scalar
        def _(act):
            init_act(act)
            init_all(act)
            pre0.scalar(act)
            context0.scalar(act)
            n0.scalar(act)
            cross0.scalar(act)
            if stop >= 2:
                ln_wait(act)
                n1.scalar(act)
                self0.scalar(act)
            if stop >= 3:
                n2.scalar(act)
                moe.scalar(act)
            if stop >= 4:
                act.wait_ge(s_kn, 16)
                context1.scalar(act)
                n3.scalar(act)
                cross1.scalar(act)
            if stop >= 5:
                n4.scalar(act)
                ffn1.scalar(act)

        @block.vector
        def _(dve):
            init_all(dve)
            pre0.vector(dve)
            context0.vector(dve)
            n0.vector(dve)
            cross0.vector(dve)
            if stop >= 2:
                ln_wait(dve)
                n1.vector(dve)
                self0.vector(dve)
            if stop >= 3:
                n2.vector(dve)
                moe.vector(dve)
            if stop >= 4:
                context1.vector(dve)
                n3.vector(dve)
                cross1.vector(dve)
            if stop >= 5:
                n4.vector(dve)
                ffn1.vector(dve)

        @block.tensor
        def _(pe):
            init_all(pe)
            context0.tensor(pe)
            n0.tensor(pe)
            cross0.tensor(pe)
            if stop >= 2:
                n1.tensor(pe)
                self0.tensor(pe)
            if stop >= 3:
                n2.tensor(pe)
                moe.tensor(pe)
            if stop >= 4:
                context1.tensor(pe)
                n3.tensor(pe)
                cross1.tensor(pe)
            if stop >= 5:
                n4.tensor(pe)
                ffn1.tensor(pe)


def layout(v):
    a = {k: np.asarray(x) for k, x in v.items()}
    c = np.ascontiguousarray

    def steps(groups):
        w = np.stack(groups)
        n = w.shape[0]
        return c(w.reshape(n, P, 8, -1).transpose(0, 2, 1, 3).reshape(n * 8, P, -1))

    def rows(w):
        return w.reshape(-1, P, w.shape[1]).transpose(1, 0, 2).reshape(P, -1)

    def cols(w, g, n=GW):
        return rows(w[:, g * n:(g + 1) * n])

    def col(x):
        return c(x.reshape(-1, P).T)

    o = {"x": a["x"], "ctxT": c(a["ctx_2048"].reshape(B * SC, D).T), "mask": a["mask_1xSxS2_ff0"]}
    o["gates"] = c(np.stack([a["g_xattn"][0], a["g_ffn"][0], a["g_xattn"][1], a["g_ffn"][1]]))
    o["ident"] = np.eye(P, dtype=np.float32)
    x0 = "L0_xattn_"
    o["w_x0"] = steps([np.concatenate([cols(a[x0 + "Wq"], g), rows(a[x0 + "Wo"][g * GW:(g + 1) * GW])], 1)
                       for g in range(G)])
    o["x0_Wk"], o["x0_Wv"] = a[x0 + "Wk"], a[x0 + "Wv"]
    o["x0_bq"], o["x0_bk"], o["x0_bv"] = a[x0 + "bq"], a[x0 + "bk"], col(a[x0 + "bv"])
    o["x0_w"] = c(np.stack([a[x0 + "qn_w"], a[x0 + "kn_w"]], 1))
    f0 = "L0_ffn_"
    o["w_f0"] = steps([np.concatenate([cols(a[f0 + "wq"], g), cols(a[f0 + "wk"], g), cols(a[f0 + "wv"], g),
                                       rows(a[f0 + "wo"][g * GW:(g + 1) * GW])], 1) for g in range(G)])
    o["f0_b"] = c(np.concatenate([a[f0 + n].reshape(G, 1, GW) for n in ("bq", "bk", "bv")], 1).reshape(-1))
    o["f0_bo"] = a[f0 + "bo"]
    for n in ("ln1_w", "ln1_b", "ln2_w", "ln2_b"):
        o["f0_" + n] = col(a[f0 + n])
    inv = (1.0 / np.float32(10000.0) ** (np.arange(0, HD, 2, dtype=np.float32) / np.float32(HD))).astype(np.float32)
    fr = np.arange(S, dtype=np.float32)[:, None] * inv[None]
    o["cos"] = c(np.concatenate([np.cos(fr), np.cos(fr)], 1).astype(np.float32))
    o["sin"] = c(np.concatenate([-np.sin(fr), np.sin(fr)], 1).astype(np.float32))
    tri = np.where(np.arange(P)[None] > np.arange(P)[:, None], np.float32(NEG), np.float32(0)).astype(np.float32)
    z = np.zeros((P, P), np.float32)
    o["mask_f0"] = c(np.concatenate([tri, z, tri], 1))
    o["mask_x1"] = c(np.concatenate([tri, z, z, tri], 1))
    o["w_moe"] = steps([np.concatenate([rows(a[f0 + "we1"][e]) for e in range(E)]
                                       + [rows(a[f0 + "we2"][e]) for e in range(E)], 1)])
    o["w_gate"] = c(rows(a[f0 + "w_gate"]))
    o["be1"] = col(a[f0 + "be1"].reshape(-1))
    o["be2"] = c(a[f0 + "be2"].reshape(-1))
    earlier = np.tril(np.ones((E, E), np.float32), -1)
    o["earlier"] = c(earlier.reshape(-1))
    x1 = "L1_xattn_"
    o["w_x1"] = steps([np.concatenate([cols(a[x1 + "wq"], g),
                                       rows(np.concatenate([a[x1 + "wk"][:, g * HD:(g + 1) * HD],
                                                            a[x1 + "wv"][:, g * HD:(g + 1) * HD]], 1)),
                                       rows(a[x1 + "wo"][g * GW:(g + 1) * GW])], 1) for g in range(G)])
    o["x1_Wk"], o["x1_Wv"] = a[x1 + "wk_ctx"], a[x1 + "wv_ctx"]
    qn, kn = a[x1 + "q_norm_w"], a[x1 + "k_norm_w"]

    def swap(w):
        return np.concatenate([w[H2:], w[:H2]])
    o["x1_w"] = c(np.concatenate([qn, swap(qn), kn, swap(kn)]))
    o["x1_kn"] = col(kn)
    f1 = "L1_ffn_"
    pad = FW - a[f1 + "gate_w"].shape[0]

    def padded(w):
        return np.concatenate([w, np.zeros((pad, *w.shape[1:]), np.float32)])
    o["w_ff"] = steps([np.concatenate([rows(padded(a[f1 + "gate_w"]).T), rows(padded(a[f1 + "up_w"]).T),
                                       rows(padded(a[f1 + "down_w"].T))], 1)])
    o["ff_gs"], o["ff_us"] = col(padded(a[f1 + "gate_s"])), col(padded(a[f1 + "up_s"]))
    o["ff_ds"] = a[f1 + "down_s"]
    return o


def kernel(**inputs):
    import concourse.bacc as bacc
    from concourse.bass_utils import run_bass_kernel_spmd

    nc = bacc.Bacc("TRN2", target_bir_lowering=False, num_devices=1)
    arrays = layout(inputs)
    aps = {k: nc.dram_tensor(f"in_{k}", x.shape, mybir.dt.from_np(x.dtype), kind="ExternalInput").ap()
           for k, x in arrays.items()}
    out = nc.dram_tensor("out", (B, S, D), F32, kind="ExternalOutput").ap()
    spill = nc.dram_tensor("x_spill", (P, B * T, D), F32).ap()
    build(nc, aps, out, spill)
    r = run_bass_kernel_spmd(nc, [{f"in_{k}": x for k, x in arrays.items()}], core_ids=[0])
    return r.results[0]["out"]
```

```python
from collections import namedtuple
from contextlib import ExitStack

import numpy as np
import concourse.bass as bass
from concourse import mybir

F32 = mybir.dt.float32
F32R = mybir.dt.float32r
ALU = mybir.AluOpType
ACT = mybir.ActivationFunctionType
AX = mybir.AxisListType

P = 128
B, S, D = 8, 256, 256
SC = 64
T = S // P
KD = D // P
HD = 128
NH, NKV = 16, 4
G = 4
HG = NH // G
GW = HG * HD
E = 4
NI = G * B
FM = 6
FW = FM * P
WSLOT = 2 * KD * FW + FM * D
CW_X0, CW_F0, CW_MOE, CW_X1, CW_FF = 256, 512, 512, 320, WSLOT // 8
NEG = -1e30
H2 = HD // 2
Phase = namedtuple("Phase", "sync gpsimd scalar vector tensor")


def ds(i, n=1):
    return bass.ds(i, n)


def pos(n):
    return max(n, 0) if isinstance(n, int) else n


def in_pairs(e, n, body, last_group_from=None):
    cut = last_group_from if last_group_from is not None else n
    for i in (0, 1):
        body(i, i, i >= cut)
    if cut < n:
        with e.Fori(1, cut // 2) as j:
            for s in (0, 1):
                body(e.snap(2 * j + s), s, False)
        with e.Fori(cut // 2, n // 2 - 1) as j:
            for s in (0, 1):
                body(e.snap(2 * j + s), s, True)
    else:
        with e.Fori(1, n // 2 - 1) as j:
            for s in (0, 1):
                body(e.snap(2 * j + s), s, False)
    for s in (0, 1):
        body(n - 2 + s, s, cut < n)


def bc(ap, dim, n):
    u = ap.unsqueeze(dim)
    return u.to_broadcast([*u.shape[:dim], n, *u.shape[dim + 1:]])


def build(nc, d, out, spill, stop=99):
    ctx = ExitStack()
    with ctx:
        def lasting_sem(name):
            return ctx.enter_context(nc.semaphore(name))

        phase_sems = ExitStack()
        numbers = []

        def sem(name):
            h = phase_sems.enter_context(nc.semaphore(name))
            numbers.append(h)
            return h

        def psum(name, shape):
            return ctx.enter_context(nc.psum_tensor(name, shape, F32))

        def sb(name, shape, dt=F32, where=ctx):
            return where.enter_context(nc.sbuf_tensor(name, shape, dt))

        pA = psum("pA", [P, 2, 512])
        pT = psum("pT", [P, 2, 512])
        pS = psum("pS", [P, 2, 512])
        pO = psum("pO", [P, 512])
        pF = psum("pF", [P, 512])

        R = sb("R", [P, B * T, D])
        XT = sb("XT", [P, KD, B * S])
        Wh = sb("Wh", [P, 2, WSLOT], F32R)
        Wl = sb("Wl", [P, 2, WSLOT], F32R)
        RAW = sb("RAW", [P, 2, CW_FF])
        XSh = sb("XSh", [P, 2, KD, S], F32R)
        XSl = sb("XSl", [P, 2, KD, S], F32R)
        ident = sb("ident", [P, P])
        tanhg = sb("tanhg", [P, 4])
        mhalf = sb("mhalf", [P, 8])
        mv = sb("mv", [P, 2, T, 2])
        rstd = sb("rstd", [P, 2, T])

        ticks = lasting_sem("ticks")

        def apart(e, n):
            if not isinstance(n, int):
                e.sem_inc(ticks, 1)

        bar = lasting_sem("bar")
        cleared = lasting_sem("cleared")
        sems_of = {}
        phases = {}

        def phase_end(e, name):
            k = phases.setdefault(name, len(phases) + 1)
            e.drain().then_inc(bar, 1)
            if e is nc.gpsimd:
                e.wait_ge(bar, 5 * k)
                for h in [ticks, *sems_of[name]]:
                    e.sem_clear(h)
                e.nop().then_inc(cleared, 1)
            e.wait_ge(cleared, k)

        def close_phase(name):
            sems_of[name] = list(numbers)
            numbers.clear()
            phase_sems.close()

        def stream_sp(sp, raw_in, split_done, src, cw, step, s, first=0):
            sp.wait_ge(split_done, pos(step - 1))
            sp.dma_start(RAW[:, s:s + 1, 0:cw], src[ds(step - first)].rearrange("a p c -> p a c")
                         ).then_inc(raw_in[s], 16)

        def split(pool, raw_in, split_hi, split_done, cw, step, s, slot):
            col = (step % 8) * cw
            pool.wait_ge(raw_in[s], 16 * (step // 2 + 1))
            apart(pool, 16 * (step // 2 + 1))
            raw = RAW[:, s:s + 1, 0:cw]
            hi = Wh[:, ds(slot), ds(col, cw)]
            pool.tensor_copy(hi, raw).then_inc(split_hi, 1)
            pool.wait_ge(split_hi, step + 1)
            apart(pool, step + 1)
            pool.tensor_tensor(Wl[:, ds(slot), ds(col, cw)], raw, hi.bitcast(F32),
                               ALU.subtract).then_inc(split_done, 1)

        ld_R, ld_c, c_half, c_tanh, out_done = (
            lasting_sem(x) for x in ("ld_R", "ld_c", "c_half", "c_tanh", "out_done"))
        x_rows = d["x"].rearrange("b (t p) n -> p (b t) n", p=P)
        gates = sb("gates", [P, 4])

        def init_sp(sp):
            sp.dma_start(ident[:, :], d["ident"]).then_inc(ld_c, 16)
            sp.dma_start(gates[:, :], d["gates"].partition_broadcast(P)).then_inc(ld_c, 16)
            for k in range(4):
                sp.dma_start(R[:, 4 * k:4 * k + 4, :], x_rows[:, 4 * k:4 * k + 4, :]).then_inc(ld_R, 16)

        def init_pool(pool):
            pool.memset(mhalf[:, :], -0.5).then_inc(c_half, 1)

        def init_act(act):
            act.wait_ge(ld_c, 32)
            act.activation(tanhg[:, :], gates[:, :], ACT.Tanh).then_inc(c_tanh, 1)

        def init_all(e):
            e.wait_ge(ld_c, 32)
            e.wait_ge(ld_R, 64)
            e.wait_ge(c_half, 1)
            e.wait_ge(c_tanh, 1)

        def layer_norm(name, double=False, affine=None, after=None):
            s_st = sem(name + "_stats")
            s_rs = sem(name + "_rstd")
            s_v = sem(name + "_dve")
            s_p = sem(name + "_pool")
            s_hid = sem(name + "_hid")
            s_xn = sem(name + "_xn")
            s_tr = sem(name + "_tr")
            s_ev = sem(name + "_ev")
            rounds = 2 if double else 1
            scope = ExitStack()
            bst = sb(name + "_bst", [P, T, 6], F32, scope)
            xn = sb(name + "_xn", [P, 2, T, D], F32, scope)

            def pool_rstd(pool, n, s):
                pool.wait_ge(s_st, n + 1)
                apart(pool, n + 1)
                pool.tensor_scalar(rstd[:, s, :], mv[:, s, :, 1], 1e-5, None, ALU.add).then_inc(s_p, 1)
                pool.wait_ge(s_p, 2 * n + 1)
                apart(pool, 2 * n + 1)
                pool.tensor_tensor(rstd[:, s, :], rstd[:, s, :], mhalf[:, 0:T], ALU.pow).then_inc(s_rs, 1)
                pool.nop().then_inc(s_p, 1)

            def pool(e):
                def body(i, s, _):
                    for r in range(rounds):
                        pool_rstd(e, rounds * i + r, s)
                    if after is not None:
                        e.wait_ge(s_xn, i + 1)
                        apart(e, i + 1)
                        e.tensor_tensor(R[:, ds(2 * i, T), :], R[:, ds(2 * i, T), :],
                                        bc(after[:, :], 1, T), ALU.add)
                in_pairs(e, B, body)
                phase_end(e, name)

            def dve(e):
                def stats(i, s, n):
                    for t in range(T):
                        e.bn_stats(bst[:, t, :], R[:, ds(2 * i + t), :]).then_inc(s_v, 1)
                    e.wait_ge(s_v, T * (n + 1))
                    apart(e, T * (n + 1))
                    for t in range(T):
                        ins = e.bn_aggr(mv[:, s, t, :], bst[:, t, :])
                    ins.then_inc(s_st, 1)
                    e.wait_ge(s_st, n + 1)

                def body(i, s, _):
                    for r in range(rounds):
                        n = rounds * i + r
                        stats(i, s, n)
                        e.wait_ge(s_rs, n + 1)
                        if double and r == 0:
                            for t in range(T):
                                ins = e.tensor_scalar(R[:, ds(2 * i + t), :], R[:, ds(2 * i + t), :],
                                                      mv[:, s, t, 0:1], rstd[:, s, t:t + 1],
                                                      ALU.subtract, ALU.mult)
                            ins.then_inc(s_hid, 1)
                            e.wait_ge(s_hid, i + 1)
                            apart(e, i + 1)
                            continue
                        e.wait_ge(s_tr, pos(i - 1))
                        for t in range(T):
                            ins = e.tensor_scalar(xn[:, s, t, :], R[:, ds(2 * i + t), :],
                                                  mv[:, s, t, 0:1], rstd[:, s, t:t + 1],
                                                  ALU.subtract, ALU.mult)
                        ins.then_inc(s_xn, 1)
                        e.wait_ge(s_xn, i + 1)
                        apart(e, i + 1)
                in_pairs(e, B, body)
                phase_end(e, name)

            def pe(e):
                def body(i, s, _):
                    e.wait_ge(s_xn, i + 1)
                    e.wait_ge(s_ev, pos(i - 1))
                    for k in range(KD):
                        for t in range(T):
                            ins = e.transpose(pT[:, s, k * S + t * P:k * S + t * P + P],
                                              xn[:, s, t, k * P:k * P + P], ident[:, :])
                    ins.then_inc(s_tr, 1)
                in_pairs(e, B, body)
                phase_end(e, name)

            def act(e):
                def body(i, s, _):
                    e.wait_ge(s_tr, i + 1)
                    if affine is None:
                        ins = e.activation(XT[:, :, ds(i * S, S)],
                                           pT[:, s, :].rearrange("p (k n) -> p k n", k=KD), ACT.Copy)
                    else:
                        w, b = affine
                        for k in range(KD):
                            ins = e.activation(XT[:, k, ds(i * S, S)], pT[:, s, k * S:(k + 1) * S],
                                               ACT.Identity, scale=w[:, k:k + 1], bias=b[:, k:k + 1])
                    ins.then_inc(s_ev, 1)
                in_pairs(e, B, body)
                phase_end(e, name)

            def sp(e):
                phase_end(e, name)

            close_phase(name)
            scope.close()
            return Phase(sp, pool, act, dve, pe)

        def context(name, scope, wk, wv, KT, w_col, bk=None, VT=None, bv=None, VC=None, first_stream=None):
            cT = sb(name + "_cT", [P, KD, 512], F32, scope)
            wkv = sb(name + "_wkv", [P, 2, KD, 512], F32, scope)
            kb = sb(name + "_kb", [P, 2, 512], F32, scope)
            sq = sb(name + "_sq", [P, 2, 512], F32, scope)
            ss = sb(name + "_ss", [P, 2, 4], F32, scope)
            s_ld, s_k, s_kb, s_sq, s_ss, s_p, s_rk, s_kn, s_t, s_te, s_v, s_ve = (
                sem(f"{name}_{x}") for x in ("ld", "k", "kb", "sq", "ss", "pool", "rk", "kn", "t", "te",
                                             "v", "ve"))
            raw_in = [sem(f"{name}_raw{x}") for x in range(2)]
            split_hi, split_done = sem(name + "_hi"), sem(name + "_split")
            NC = B * SC // P

            def sp(e):
                e.dma_start(cT[:, :, :], d["ctxT"].rearrange("(k p) n -> p k n", p=P)).then_inc(s_ld, 16)
                e.dma_start(wkv[:, 0], wk.rearrange("(k p) n -> p k n", p=P)).then_inc(s_ld, 16)
                e.dma_start(wkv[:, 1], wv.rearrange("(k p) n -> p k n", p=P)).then_inc(s_ld, 16)
                if first_stream:
                    src, cw = first_stream
                    for c in range(8):
                        stream_sp(e, raw_in, split_done, src, cw, c, c % 2)
                phase_end(e, name)

            def pe(e):
                e.wait_ge(s_ld, 48)
                for c in range(NC):
                    e.wait_ge(s_kb, pos(c - 1))
                    for k in range(KD):
                        ins = e.matmul(pA[:, c % 2, :], cT[:, k, c * P:(c + 1) * P], wkv[:, 0, k, :],
                                       start=(k == 0), stop=(k == KD - 1))
                    ins.then_inc(s_k, 1)
                for c in range(4):
                    e.wait_ge(s_ve, pos(c - 1))
                    for k in range(KD):
                        if VT is not None:
                            ins = e.matmul(pS[:, c % 2, :], wkv[:, 1, k, c * HD:(c + 1) * HD], cT[:, k, :],
                                           start=(k == 0), stop=(k == KD - 1))
                        else:
                            ins = e.matmul(pS[:, c % 2, :], cT[:, k, c * P:(c + 1) * P], wkv[:, 1, k, :],
                                           start=(k == 0), stop=(k == KD - 1))
                    ins.then_inc(s_v, 1)
                for c in range(NC):
                    e.wait_ge(s_kn, c + 1)
                    e.wait_ge(s_te, pos(c - 1))
                    for h in range(NKV):
                        ins = e.transpose(pT[:, c % 2, h * P:(h + 1) * P], kb[:, c % 2, h * P:(h + 1) * P],
                                          ident[:, :])
                    ins.then_inc(s_t, 1)
                phase_end(e, name)

            def dve(e):
                for c in range(NC):
                    s = c % 2
                    e.wait_ge(s_k, c + 1)
                    e.wait_ge(s_t, pos(c - 1))
                    if bk is not None:
                        e.tensor_tensor(kb[:, s, :], pA[:, s, :], bk[:, :], ALU.add).then_inc(s_kb, 1)
                    else:
                        e.tensor_copy(kb[:, s, :], pA[:, s, :]).then_inc(s_kb, 1)
                    e.wait_ge(s_sq, c + 1)
                    e.tensor_reduce(ss[:, s, :], sq[:, s, :].rearrange("p (h d) -> p h d", h=NKV),
                                    AX.X, ALU.add).then_inc(s_ss, 1)
                    e.wait_ge(s_rk, c + 1)
                    v = kb[:, s, :].rearrange("p (h d) -> p h d", h=NKV)
                    e.tensor_tensor(v, v, bc(ss[:, s, :], 2, HD), ALU.mult).then_inc(s_kn, 1)
                phase_end(e, name)

            def pool(e):
                for c in range(NC):
                    s = c % 2
                    e.wait_ge(s_kb, c + 1)
                    apart(e, c + 1)
                    e.wait_ge(s_ss, pos(c - 1))
                    apart(e, c - 1)
                    e.tensor_tensor(sq[:, s, :], kb[:, s, :], kb[:, s, :], ALU.mult).then_inc(s_sq, 1)
                    e.wait_ge(s_ss, c + 1)
                    apart(e, c + 1)
                    e.tensor_scalar(ss[:, s, :], ss[:, s, :], 1.0 / HD, 1e-6, ALU.mult, ALU.add).then_inc(s_p, 1)
                    e.wait_ge(s_p, c + 1)
                    apart(e, c + 1)
                    e.tensor_tensor(ss[:, s, :], ss[:, s, :], mhalf[:, 0:4], ALU.pow).then_inc(s_rk, 1)
                if first_stream:
                    src, cw = first_stream
                    for c in range(8):
                        split(e, raw_in, split_hi, split_done, cw, c, c % 2, 0)
                phase_end(e, name)

            def act(e):
                for c in range(4):
                    e.wait_ge(s_v, c + 1)
                    if VT is not None:
                        e.activation(VT[:, c, :], pS[:, c % 2, :], ACT.Identity,
                                     bias=bv[:, c:c + 1]).then_inc(s_ve, 1)
                    else:
                        for r in range(2):
                            for q in range(2):
                                ins = e.activation(VC[q * SC:(q + 1) * SC, 2 * c + r, :],
                                                   pS[r * SC:(r + 1) * SC, c % 2, :], ACT.Copy)
                        ins.then_inc(s_ve, 1)
                for c in range(NC):
                    e.wait_ge(s_t, c + 1)
                    e.activation(KT[:, :, c * P:(c + 1) * P],
                                 pT[:, c % 2, :].rearrange("p (h n) -> p h n", h=NKV),
                                 ACT.Copy, scale=w_col[:, 0:1]).then_inc(s_te, 1)
                phase_end(e, name)

            close_phase(name)
            return Phase(sp, pool, act, dve, pe)

        def high_w(act, raw_in, split_hi, cw, step, s, slot):
            act.wait_ge(raw_in[s], 16 * (step // 2 + 1))
            act.activation(Wh[:, ds(slot), ds((step % 8) * cw, cw)], RAW[:, s:s + 1, 0:cw], ACT.Copy
                           ).then_inc(split_hi, 1)

        def low_w(pool, split_hi, split_done, cw, step, s, slot):
            at = (ds(slot), ds((step % 8) * cw, cw))
            pool.wait_ge(split_hi, step + 1)
            apart(pool, step + 1)
            pool.tensor_tensor(Wl[:, at[0], at[1]], RAW[:, s:s + 1, 0:cw], Wh[:, at[0], at[1]].bitcast(F32),
                               ALU.subtract).then_inc(split_done, 1)

        def high_x(act, s, i, hi_done):
            act.activation(XSh[:, s], XT[:, :, ds((i % B) * S, S)], ACT.Copy).then_inc(hi_done, 1)

        def low_x(pool, s, i, hi_done, ready):
            pool.wait_ge(hi_done, i + 1)
            apart(pool, i + 1)
            pool.tensor_tensor(XSl[:, s], XT[:, :, ds((i % B) * S, S)], XSh[:, s].bitcast(F32),
                               ALU.subtract).then_inc(ready, 1)

        def three(e, o, ah, al, bh, bl, first, last):
            e.matmul(o, ah, bh, start=first, stop=False)
            e.matmul(o, ah, bl, start=False, stop=False)
            return e.matmul(o, al, bh, start=False, stop=last)

        def copy_x(pool, s, i, ready, hi_done):
            src = XT[:, :, ds((i % B) * S, S)]
            pool.tensor_copy(XSh[:, s], src).then_inc(hi_done, 1)
            pool.wait_ge(hi_done, i + 1)
            apart(pool, i + 1)
            pool.tensor_tensor(XSl[:, s], src, XSh[:, s].bitcast(F32), ALU.subtract).then_inc(ready, 1)

        x0 = ExitStack()

        def cross_attention_0():
            name = "x0"
            KT = sb("x0_KT", [P, NKV, B * SC], F32, x0)
            VT = sb("x0_VT", [P, NKV, B * SC], F32, x0)
            bq = sb("x0_bq", [P, NH * HD], F32, x0)
            bk = sb("x0_bk", [P, NKV * HD], F32, x0)
            bv = sb("x0_bv", [P, NKV], F32, x0)
            wcol = sb("x0_w", [P, 3], F32, x0)
            mask = sb("x0_mask", [P, T, SC], F32, x0)
            s_c, s_w = sem("x0_c"), sem("x0_wq")

            def pre_sp(e):
                e.dma_start(bq[:, :], d["x0_bq"].partition_broadcast(P)).then_inc(s_c, 16)
                e.dma_start(bk[:, :], d["x0_bk"].partition_broadcast(P)).then_inc(s_c, 16)
                e.dma_start(bv[:, :], d["x0_bv"]).then_inc(s_c, 16)
                e.dma_start(wcol[:, 0:2], d["x0_w"]).then_inc(s_c, 16)
                e.dma_start(mask[:, :, :], d["mask"].rearrange("a (t p) k -> p (a t) k", p=P)).then_inc(s_c, 16)

            def pre_dve(e):
                e.wait_ge(s_c, 80)
                e.tensor_tensor(wcol[:, 2:3], wcol[:, 0:1], wcol[:, 1:2], ALU.mult).then_inc(s_w, 1)

            def pre_act(e):
                e.wait_ge(s_w, 1)

            with ExitStack() as tmp:
                before = context("c0", tmp, d["x0_Wk"], d["x0_Wv"], KT, wcol[:, 2:3], bk=bk, VT=VT, bv=bv,
                        first_stream=(d["w_x0"], CW_X0))
            norm = layer_norm("n0")

            qb = sb("x0_qb", [P, 2, T, GW], F32, x0)
            sq = sb("x0_sq", [P, T, GW], F32, x0)
            ssq = sb("x0_ss", [P, T, HG], F32, x0)
            rq = sb("x0_rq", [P, 2, T, HG], F32, x0)
            qT = sb("x0_qT", [P, HG, S], F32, x0)
            PB = sb("x0_P", [P, T, HG, SC], F32, x0)
            mx = sb("x0_mx", [P, T, HG], F32, x0)
            sm = sb("x0_sm", [P, T, HG], F32, x0)
            PT = sb("x0_PT", [P, 2, S], F32, x0)
            VSh = sb("x0_VSh", [P, P], F32R, x0)
            VSl = sb("x0_VSl", [P, P], F32R, x0)
            VW = sb("x0_VW", [P, 2, 2, D], F32, x0)
            names = ("raw0", "raw1", "hi", "split", "xhi", "xs", "proj", "qb", "sq", "rqa", "rq", "tr", "te",
                     "sc", "s1", "s2", "mx", "s3", "ex", "sm", "rs", "pn", "pt", "pte", "f", "acc",
                     "vhi", "vs", "vw", "vwe")
            q = {x: sem("x0_" + x) for x in names}
            raw_in = [q["raw0"], q["raw1"]]
            WO = KD * GW

            def sp(e):
                def body(i, s, nxt):
                    if nxt:
                        stream_sp(e, raw_in, q["split"], d["w_f0"], CW_F0, i, s, 24)
                    else:
                        stream_sp(e, raw_in, q["split"], d["w_x0"][8:32], CW_X0, i, s)
                in_pairs(e, NI, body, 24)
                phase_end(e, name)

            def pool(e):
                def vs(i):
                    j = i // 2
                    e.wait_ge(q["vw"], 2 * j)
                    apart(e, 2 * j)
                    src = VT[:, ds(i // B), ds((i % B) * SC, P)]
                    e.tensor_copy(VSh[:, :], src).then_inc(q["vhi"], 1)
                    e.wait_ge(q["vhi"], j + 1)
                    apart(e, j + 1)
                    e.tensor_tensor(VSl[:, :], src, VSh[:, :].bitcast(F32), ALU.subtract).then_inc(q["vs"], 1)

                def norms(i, s):
                    e.wait_ge(q["sq"], T * i + T)
                    apart(e, T * i + T)
                    e.wait_ge(q["s1"], pos(i - 1))
                    apart(e, i - 1)
                    e.tensor_scalar(rq[:, s], ssq[:, :, :], HD * 1e-6, None, ALU.add).then_inc(q["rqa"], 1)
                    e.wait_ge(q["rqa"], i + 1)
                    apart(e, i + 1)
                    r = rq[:, s].rearrange("p t h -> p (t h)")
                    e.tensor_tensor(r, r, mhalf[:, 0:T * HG], ALU.pow).then_inc(q["rq"], 1)

                def body(i, s, nxt):
                    first, last = isinstance(i, int) and i == 0, isinstance(i, int) and i == NI - 1
                    if first:
                        low_x(e, 0, 0, q["xhi"], q["xs"])
                        low_x(e, 1, 1, q["xhi"], q["xs"])
                        vs(0)
                        low_x(e, 0, 2, q["xhi"], q["xs"])
                        norms(0, 0)
                        norms(1, 1)
                    if not (isinstance(i, int) and i >= NI - 3):
                        low_x(e, 1 - s, i + 3, q["xhi"], q["xs"])
                    if nxt:
                        low_w(e, q["hi"], q["split"], CW_F0, i, s, 0)
                    else:
                        low_w(e, q["hi"], q["split"], CW_X0, i, s, (i // 8 + 1) % 2)
                    if s == 1 and not last:
                        vs(i + 1)
                    if not (isinstance(i, int) and i >= NI - 2):
                        norms(i + 2, s)
                in_pairs(e, NI, body, 24)
                phase_end(e, name)

            def pe(e):
                def proj(i, s, t):
                    e.wait_ge(q["xs"], i + 1)
                    e.wait_ge(q["split"], pos(i - 3))
                    slot = (i // 8) % 2
                    e.wait_ge(q["qb"], pos(T * (i - 1) + t + 1))
                    for k in range(KD):
                        w = slice(k * GW, (k + 1) * GW)
                        ins = three(e, pA[:, t, :], XSh[:, s, k, t * P:(t + 1) * P],
                                    XSl[:, s, k, t * P:(t + 1) * P], Wh[:, ds(slot), w],
                                    Wl[:, ds(slot), w], k == 0, k == KD - 1)
                    ins.then_inc(q["proj"], 1)

                def vw(i, hp):
                    e.wait_ge(q["vs"], i // 2 + 1)
                    e.wait_ge(q["split"], i)
                    slot = (i // 8) % 2
                    e.wait_ge(q["vwe"], i + hp)
                    w = slice(WO + hp * 512, WO + (hp + 1) * 512)
                    three(e, pO[:, :], VSh[:, :], VSl[:, :], Wh[:, ds(slot), w], Wl[:, ds(slot), w],
                          True, True).then_inc(q["vw"], 1)

                def q_tr(i, s):
                    for t in range(T):
                        e.wait_ge(q["qb"], T * i + t + 1)
                        e.wait_ge(q["te"], pos(T * (i - 1) + t + 1))
                        for h in range(HG):
                            ins = e.transpose(pT[:, t, h * P:(h + 1) * P], qb[:, s, t, h * HD:(h + 1) * HD],
                                              ident[:, :])
                        ins.then_inc(q["tr"], 1)

                def scores(i):
                    e.wait_ge(q["te"], T * i + T)
                    e.wait_ge(q["s1"], i)
                    g, b = i // 8, i % 8
                    for t in range(T):
                        for h in range(HG):
                            c = (t * HG + h) * SC
                            ins = e.matmul(pS[:, 0, c:c + SC], qT[:, h, t * P:(t + 1) * P],
                                           KT[:, ds(g), ds(b * SC, SC)], start=True, stop=True)
                    ins.then_inc(q["sc"], 1)

                def p_tr(i):
                    e.wait_ge(q["pn"], i + 1)
                    e.wait_ge(q["pte"], i)
                    for hp in range(2):
                        for t in range(T):
                            c = (hp * T + t) * P
                            ins = e.transpose(pS[:, 1, c:c + P],
                                              PB[:, t, 2 * hp:2 * hp + 2, :].rearrange("p h k -> p (h k)"),
                                              ident[:, :])
                    ins.then_inc(q["pt"], 1)

                def out_proj(i, s):
                    e.wait_ge(q["pte"], i + 1)
                    e.wait_ge(q["vwe"], pos((i - s if not isinstance(i, int) else 2 * (i // 2)) + 2))
                    e.wait_ge(q["acc"], i)
                    for t in range(T):
                        for hp in range(2):
                            ins = e.matmul(pF[:, t * D:(t + 1) * D], PT[:, hp, t * P:(t + 1) * P],
                                           VW[:, s, hp, :], start=(hp == 0), stop=(hp == 1))
                    ins.then_inc(q["f"], 1)

                def body(i, s, nxt):
                    first, last = isinstance(i, int) and i == 0, isinstance(i, int) and i == NI - 1
                    if first:
                        for t in range(T):
                            proj(0, 0, t)
                        for t in range(T):
                            proj(1, 1, t)
                        q_tr(0, 0)
                        scores(0)
                    two_more = not (isinstance(i, int) and i >= NI - 2)
                    if s == 0:
                        vw(i, 0)
                    if two_more:
                        proj(i + 2, s, 0)
                    if not last:
                        q_tr(i + 1, 1 - s)
                    if s == 0:
                        vw(i, 1)
                    if two_more:
                        proj(i + 2, s, 1)
                    if not last:
                        scores(i + 1)
                    p_tr(i)
                    out_proj(i, s)
                in_pairs(e, NI, body, 24)
                phase_end(e, name)

            def act(e):
                def q_ev(i, t):
                    e.wait_ge(q["tr"], T * i + t + 1)
                    e.wait_ge(q["sc"], i)
                    e.activation(qT[:, :, t * P:(t + 1) * P],
                                 pT[:, t, :].rearrange("p (h n) -> p h n", h=HG), ACT.Copy
                                 ).then_inc(q["te"], 1)

                def squares(i, s, t):
                    e.wait_ge(q["qb"], T * i + t + 1)
                    e.wait_ge(q["rqa"], i)
                    e.wait_ge(q["sq"], pos(T * i + t - 1))
                    for h in range(HG):
                        x = slice(h * HD, (h + 1) * HD)
                        ins = e.activation(sq[:, t, x], qb[:, s, t, x], ACT.Square, accum_out=ssq[:, t, h:h + 1])
                    ins.then_inc(q["sq"], 1)

                def exp(i):
                    e.wait_ge(q["s3"], i + 1)
                    e.activation(PB[:, :, :, :], PB[:, :, :, :], ACT.Exp).then_inc(q["ex"], 1)

                def vw_ev(i, hp):
                    e.wait_ge(q["vw"], i + hp + 1)
                    e.wait_ge(q["f"], i)
                    for r in range(2):
                        for par in range(2):
                            ins = e.activation(VW[par * SC:(par + 1) * SC, r, hp, :],
                                               pO[r * SC:(r + 1) * SC, par * D:(par + 1) * D], ACT.Copy)
                    ins.then_inc(q["vwe"], 1)

                def body(i, s, nxt):
                    first, last = isinstance(i, int) and i == 0, isinstance(i, int) and i == NI - 1
                    if first:
                        for k in (0, 1):
                            high_x(e, k, k, q["xhi"])
                        e.wait_ge(q["proj"], T)
                        high_x(e, 0, 2, q["xhi"])
                        q_ev(0, 0)
                        q_ev(0, 1)
                        for k in (0, 1):
                            squares(k, k, 0)
                            squares(k, k, 1)
                    if s == 0:
                        vw_ev(i, 0)
                    if not (isinstance(i, int) and i >= NI - 3):
                        e.wait_ge(q["proj"], T * (i + 2))
                        high_x(e, 1 - s, i + 3, q["xhi"])
                    e.wait_ge(q["proj"], T * i)
                    if nxt:
                        high_w(e, raw_in, q["hi"], CW_F0, i, s, 0)
                    else:
                        high_w(e, raw_in, q["hi"], CW_X0, i, s, (i // 8 + 1) % 2)
                    exp(i)
                    if not last:
                        q_ev(i + 1, 0)
                        q_ev(i + 1, 1)
                    if not (isinstance(i, int) and i >= NI - 2):
                        squares(i + 2, s, 0)
                    if s == 0:
                        vw_ev(i, 1)
                    e.wait_ge(q["pt"], i + 1)
                    e.wait_ge(q["f"], i)
                    e.activation(PT[:, :, :], pS[:, 1, :].rearrange("p (a n) -> p a n", a=2), ACT.Copy
                                 ).then_inc(q["pte"], 1)
                    if not (isinstance(i, int) and i >= NI - 2):
                        squares(i + 2, s, 1)
                in_pairs(e, NI, body, 24)
                phase_end(e, name)

            def dve(e):
                def queries(i, s, t):
                    e.wait_ge(q["proj"], T * i + t + 1)
                    e.wait_ge(q["tr"], pos(T * (i - 2) + t + 1))
                    e.wait_ge(q["sq"], pos(T * (i - 2) + t + 1))
                    e.tensor_tensor(qb[:, s, t, :], pA[:, t, :], bq[:, ds((i // 8) * GW, GW)], ALU.add
                                    ).then_inc(q["qb"], 1)

                def softmax(i, s, two_more):
                    e.wait_ge(q["sc"], i + 1)
                    e.wait_ge(q["rq"], i + 1)
                    e.wait_ge(q["pt"], i)
                    e.tensor_tensor(PB[:, :, :, :].rearrange("p t h k -> p (t h) k"),
                                    pS[:, 0, :].rearrange("p (a k) -> p a k", k=SC),
                                    bc(rq[:, s].rearrange("p t h -> p (t h)"), 2, SC), ALU.mult
                                    ).then_inc(q["s1"], 1)
                    e.wait_ge(q["s1"], i + 1)
                    for t in range(T):
                        ins = e.tensor_tensor(PB[:, t], PB[:, t], bc(mask[:, t, :], 1, HG), ALU.add)
                    ins.then_inc(q["s2"], 1)
                    e.wait_ge(q["s2"], i + 1)
                    e.tensor_reduce(mx[:, :, :], PB[:, :, :, :], AX.X, ALU.max).then_inc(q["mx"], 1)
                    e.wait_ge(q["mx"], i + 1)
                    e.tensor_tensor(PB[:, :, :, :], PB[:, :, :, :], bc(mx[:, :, :], 3, SC), ALU.subtract
                                    ).then_inc(q["s3"], 1)
                    if two_more:
                        queries(i + 2, s, 0)
                    e.wait_ge(q["ex"], i + 1)
                    e.tensor_reduce(sm[:, :, :], PB[:, :, :, :], AX.X, ALU.add).then_inc(q["sm"], 1)
                    e.wait_ge(q["sm"], i + 1)
                    e.reciprocal(sm[:, :, :], sm[:, :, :]).then_inc(q["rs"], 1)
                    e.wait_ge(q["rs"], i + 1)
                    e.tensor_tensor(PB[:, :, :, :], PB[:, :, :, :], bc(sm[:, :, :], 3, SC), ALU.mult
                                    ).then_inc(q["pn"], 1)

                def add_out(i):
                    e.wait_ge(q["f"], i + 1)
                    e.wait_ge(q["acc"], i)
                    r = R[:, ds(T * (i % 8), T), :]
                    e.scalar_tensor_tensor(r, pF[:, :].rearrange("p (t n) -> p t n", t=T), tanhg[:, 0:1], r,
                                           ALU.mult, ALU.add).then_inc(q["acc"], 1)

                def body(i, s, nxt):
                    first, last = isinstance(i, int) and i == 0, isinstance(i, int) and i == NI - 1
                    if first:
                        for k in (0, 1):
                            queries(k, k, 0)
                            queries(k, k, 1)
                    two_more = not (isinstance(i, int) and i >= NI - 2)
                    softmax(i, s, two_more)
                    if not first:
                        add_out(i - 1)
                    if two_more:
                        queries(i + 2, s, 1)
                    if last:
                        add_out(i)
                in_pairs(e, NI, body, 24)
                phase_end(e, name)

            close_phase(name)
            return Phase(pre_sp, None, pre_act, pre_dve, None), before, norm, Phase(sp, pool, act, dve, pe)

        pre0, context0, n0, cross0 = cross_attention_0()
        x0.close()

        def causal_attention(name, scope, cross, w_here, cw_here, w_next, cw_next, slot0,
                             KT=None, VC=None):
            SW = 512 if cross else 384
            OFF = (0, SC + P) if cross else (0, P)
            WID = (SC + P, SC + S) if cross else (P, S)
            KW = HD if cross else GW
            NQ = 4 if cross else 6
            NT = 3 if cross else 4
            NTI = NT + HG
            WK = KD * GW
            WV = 2 * KD * GW
            WO = KD * (GW + 2 * KW)

            cosT = sb(name + "_cos", [P, T, HD], F32, scope)
            sinT = sb(name + "_sin", [P, T, HD], F32, scope)
            mask = sb(name + "_mask", [P, SW], F32, scope)
            qb = sb(name + "_qb", [P, 2, GW], F32, scope)
            t2 = sb(name + "_t2", [P, 2, GW], F32, scope)
            QR = sb(name + "_QR", [P, T, GW], F32, scope)
            KR = sb(name + "_KR", [P, T, KW], F32, scope)
            qT = sb(name + "_qT", [P, HG, S], F32, scope)
            kT = sb(name + "_kT", [P, KW // HD, S], F32, scope)
            V = sb(name + "_V", [P, 2, T, KW], F32, scope)
            PB = sb(name + "_P", [P, HG, SW], F32, scope)
            nm = sb(name + "_nm", [P, HG, T], F32, scope)
            sm = sb(name + "_sm", [P, HG, T], F32, scope)
            rs = sb(name + "_rs", [P, HG, T], F32, scope)
            PT = sb(name + "_PT", [P, 2, SW], F32, scope)
            OTh = sb(name + "_OTh", [P, 2, HG, S], F32R, scope)
            OTl = sb(name + "_OTl", [P, 2, HG, S], F32R, scope)
            names = ("raw0", "raw1", "hi", "split", "xhi", "xs", "proj", "taken", "rot", "rc", "rope", "tr",
                     "te", "sc", "sct", "ex", "rs", "pn", "pv", "oth", "ot", "f", "acc", "const", "table")
            q = {x: sem(f"{name}_{x}") for x in names}
            raw_in = [q["raw0"], q["raw1"]]
            if cross:
                wrow = sb(name + "_w", [P, 4, HD], F32, scope)
                cosk = sb(name + "_cosk", [P, T, HD], F32, scope)
                sink = sb(name + "_sink", [P, T, HD], F32, scope)
                sq = sb(name + "_sq", [P, GW], F32, scope)
                ssq = sb(name + "_ssq", [P, T, HG], F32, scope)
                nrq = sb(name + "_nrq", [P, 2, T, HG], F32, scope)
                ssk = sb(name + "_ssk", [P, T], F32, scope)
                kb = sb(name + "_kb", [P, T, HD], F32, scope)
                tk = sb(name + "_tk", [P, T, HD], F32, scope)
                VS = sb(name + "_VS", [P, 2, T, HD], F32, scope)
                q.update({x: sem(f"{name}_{x}") for x in ("rqa", "rqb", "rq", "rka", "rk", "k1", "vs", "vz")})
            else:
                bias = sb(name + "_bias", [P, G, 3, GW], F32, scope)

            def isfirst(i):
                return isinstance(i, int) and i == 0

            def islast(i):
                return isinstance(i, int) and i == NI - 1

            def use(i, what, n, s):
                if what == "w":
                    early = 0 if islast(i) else (1 if cross else 2)
                    c = NT + (n if n < 3 else 3 + early)
                    return NTI * i + c, (NTI * s + c) % 2
                if isfirst(i):
                    return n, n % 2
                early = 1 if cross else 2
                c = NT + (3 + n if n < early else 4 + n)
                return NTI * (i - 1) + c, (NTI * (s + 1) + c) % 2

            def sp(e):
                e.dma_start(cosT[:, :, :], d["cos"].rearrange("(t p) n -> p t n", p=P)).then_inc(q["const"], 16)
                e.dma_start(sinT[:, :, :], d["sin"].rearrange("(t p) n -> p t n", p=P)).then_inc(q["const"], 16)
                e.dma_start(mask[:, :], d["mask_x1" if cross else "mask_f0"]).then_inc(q["const"], 16)
                if cross:
                    e.dma_start(wrow[:, :, :].rearrange("p a n -> p (a n)"),
                                d["x1_w"].partition_broadcast(P)).then_inc(q["const"], 16)
                else:
                    e.dma_start(bias[:, :, :, :].rearrange("p g a n -> p (g a n)"),
                                d["f0_b"].partition_broadcast(P)).then_inc(q["const"], 16)

                def body(i, s, nxt):
                    if nxt:
                        stream_sp(e, raw_in, q["split"], w_next, cw_next, i, s, 24)
                    else:
                        stream_sp(e, raw_in, q["split"], w_here[8:32], cw_here, i, s)
                in_pairs(e, NI, body, 24)
                phase_end(e, name)

            def pe(e):
                def proj(i, s, n):
                    c = NQ * i + n
                    e.wait_ge(q["xs"], i + 1)
                    e.wait_ge(q["split"], pos(i - 2))
                    e.wait_ge(q["taken"], pos(c - 1))
                    slot = (i // 8 + slot0) % 2
                    t = n // 2 if n < 4 else n - 4
                    if cross:
                        at, w = (WK, 2 * HD) if n % 2 else (0, GW)
                    else:
                        at, w = (WV if n >= 4 else WK * (n % 2)), GW
                    for k in range(KD):
                        cc = slice(at + k * w, at + (k + 1) * w)
                        ins = three(e, pA[:, n % 2, 0:w], XSh[:, s, k, t * P:(t + 1) * P],
                                    XSl[:, s, k, t * P:(t + 1) * P], Wh[:, ds(slot), cc],
                                    Wl[:, ds(slot), cc], k == 0, k == KD - 1)
                    ins.then_inc(q["proj"], 1)

                def qk_tr(i, s, n):
                    c, bank = use(i, "qk", n, s)
                    e.wait_ge(q["te"], pos(c - 1))
                    if cross:
                        e.wait_ge(q["rope"], 4 * i + (1, 3, 4)[n])
                        src = [QR[:, n, h * HD:(h + 1) * HD] for h in range(HG)] if n < 2 else \
                              [KR[:, t, :] for t in range(T)]
                    else:
                        e.wait_ge(q["rope"], 4 * i + n + 1)
                        x = KR if n % 2 else QR
                        src = [x[:, n // 2, h * HD:(h + 1) * HD] for h in range(HG)]
                    for j, a in enumerate(src):
                        ins = e.transpose(pT[:, bank, j * P:(j + 1) * P], a, ident[:, :])
                    ins.then_inc(q["tr"], 1)

                def scores(i, s, h):
                    c, _ = use(i, "qk", NT - 1, s)
                    e.wait_ge(q["te"], c + 1)
                    e.wait_ge(q["sct"], pos(HG * i + h - 1))
                    bank = pS[:, h % 2, :]
                    for t in range(T):
                        o, n = t * P, (t + 1) * P
                        if cross:
                            o = 2 * t * P
                            c = P + t * SC
                            e.matmul(bank[:, c:c + SC], qT[:, h, t * P:(t + 1) * P],
                                     KT[:, ds(i // 8), ds((i % 8) * SC, SC)], start=True, stop=True)
                        ins = e.matmul(bank[:, o:o + n], qT[:, h, t * P:(t + 1) * P],
                                       kT[:, 0 if cross else h, 0:n], start=True, stop=True)
                    ins.then_inc(q["sc"], 1)

                def p_tr(i, s, h):
                    c, bank = use(i, "w", h, s)
                    e.wait_ge(q["pn"], HG * i + h + 1)
                    e.wait_ge(q["te"], pos(c - 1))
                    x = PB[:, h, :]
                    if cross:
                        src = [x[:, P:2 * P], x[:, 0:P], x[:, 2 * P:3 * P], x[:, 3 * P:4 * P]]
                    else:
                        src = [x[:, j * P:(j + 1) * P] for j in range(3)]
                    for j, a in enumerate(src):
                        ins = e.transpose(pT[:, bank, j * P:(j + 1) * P], a, ident[:, :])
                    ins.then_inc(q["tr"], 1)

                def attend(i, s, h):
                    c, _ = use(i, "w", h, s)
                    e.wait_ge(q["te"], c + 1)
                    e.wait_ge(q["ot"], HG * i + h)
                    k0 = P if cross else 0
                    v = slice(0, HD) if cross else slice(h * HD, (h + 1) * HD)
                    if h == 0:
                        e.wait_ge(q["taken"], NQ * i + NQ)
                    e.matmul(pO[:, 0:S], V[:, s, 0, v], PT[:, h % 2, k0:k0 + S], start=True, stop=False)
                    ins = e.matmul(pO[:, P:S], V[:, s, 1, v], PT[:, h % 2, k0 + S:k0 + S + P],
                                   start=False, stop=not cross)
                    if cross:
                        e.wait_ge(q["vs"], i + 1)
                        for t in range(T):
                            ins = e.matmul(pO[:, t * P:(t + 1) * P], VS[:, s, t, :], PT[:, h % 2, 0:P],
                                           start=False, stop=(t == 1))
                    ins.then_inc(q["pv"], 1)

                def out_proj(i, s, t):
                    e.wait_ge(q["ot"], HG * i + HG)
                    e.wait_ge(q["split"], i)
                    e.wait_ge(q["acc"], i)
                    slot = (i // 8 + slot0) % 2
                    r = slice(t * P, (t + 1) * P)
                    for h in range(HG):
                        cc = slice(WO + h * D, WO + (h + 1) * D)
                        ins = three(e, pF[:, t * D:(t + 1) * D], OTh[:, s, h, r], OTl[:, s, h, r],
                                    Wh[:, ds(slot), cc], Wl[:, ds(slot), cc], h == 0, h == HG - 1)
                    if t == T - 1:
                        ins.then_inc(q["f"], 1)

                def body(i, s, nxt):
                    n = 1 - s
                    if isfirst(i):
                        for k in range(NQ):
                            proj(0, 0, k)
                        for k in range(NT):
                            qk_tr(0, 0, k)
                        scores(0, 0, 0)
                    last = islast(i)
                    if not last:
                        j = i + 1
                    for h in range(3):
                        p_tr(i, s, h)
                        scores(i, s, h + 1)
                        if not last and h < 2:
                            proj(j, n, 2 * h)
                            attend(i, s, h)
                            proj(j, n, 2 * h + 1)
                        elif not last and not cross:
                            proj(j, n, 4)
                            attend(i, s, h)
                            proj(j, n, 5)
                        else:
                            attend(i, s, h)
                    if cross and not isfirst(i):
                        out_proj(i - 1, n, 0)
                    if not last:
                        for k in range(1 if cross else 2):
                            qk_tr(j, n, k)
                    p_tr(i, s, 3)
                    if not last:
                        for k in range(1 if cross else 2, NT):
                            qk_tr(j, n, k)
                        scores(j, n, 0)
                    attend(i, s, 3)
                    if not isfirst(i):
                        for t in range(1 if cross else 0, T):
                            out_proj(i - 1, n, t)
                    if last:
                        for t in range(T):
                            out_proj(i, s, t)
                in_pairs(e, NI, body, 24)
                phase_end(e, name)

            def act(e):
                def qk_ev(i, s, n):
                    c, bank = use(i, "qk", n, s)
                    e.wait_ge(q["tr"], c + 1)
                    e.wait_ge(q["sc"], HG * i)
                    if cross and n == 2:
                        o, a = kT[:, 0, :], pT[:, bank, 0:S]
                    else:
                        x, t = (qT, n) if cross else ((kT if n % 2 else qT), n // 2)
                        o = x[:, :, t * P:(t + 1) * P]
                        a = pT[:, bank, :].rearrange("p (h n) -> p h n", h=HG)
                    e.activation(o, a, ACT.Copy).then_inc(q["te"], 1)

                def p_ev(i, s, h):
                    c, bank = use(i, "w", h, s)
                    e.wait_ge(q["tr"], c + 1)
                    e.wait_ge(q["pv"], pos(HG * i + h - 1))
                    e.activation(PT[:, h % 2, :], pT[:, bank, 0:SW], ACT.Copy).then_inc(q["te"], 1)

                def exp(i, s, h):
                    e.wait_ge(q["sct"], HG * i + h + 1)
                    e.wait_ge(q["rs"], pos(HG * (i - 1) + h + 1))
                    for t in range(T):
                        x = PB[:, h, OFF[t]:OFF[t] + WID[t]]
                        ins = e.activation(x, x, ACT.Exp, scale=-1.0, bias=nm[:, h, t:t + 1],
                                           accum_out=sm[:, h, t:t + 1])
                    ins.then_inc(q["ex"], 1)

                def o_ev(i, s, h):
                    e.wait_ge(q["pv"], HG * i + h + 1)
                    e.wait_ge(q["f"], pos(i - 1))
                    e.activation(OTh[:, s, h, :], pO[:, 0:S], ACT.Copy).then_inc(q["oth"], 1)

                def q_ev(i, s, n):
                    t = n // 2
                    e.wait_ge(q["proj"], NQ * i + n + 1)
                    if n % 2 == 0:
                        e.wait_ge(q["rope"], pos(4 * (i - 1) + (1, 3)[t]))
                        e.wait_ge(q["rqa"], i)
                        e.wait_ge(q["taken"], NQ * i + n)
                        for h in range(HG):
                            x = slice(h * HD, (h + 1) * HD)
                            e.activation(sq[:, x], pA[:, 0, x], ACT.Square, accum_out=ssq[:, t, h:h + 1])
                        e.activation(qb[:, t, :], pA[:, 0, :], ACT.Copy).then_inc(q["taken"], 1)
                    else:
                        e.wait_ge(q["k1"], pos(T * (i - 1) + t + 1))
                        e.wait_ge(q["pv"], pos(HG * (i - 1)))
                        e.wait_ge(q["taken"], NQ * i + n)
                        e.activation(sq[:, 0:HD], pA[:, 1, 0:HD], ACT.Square, accum_out=ssk[:, t:t + 1])
                        e.activation(kb[:, t, :], pA[:, 1, 0:HD], ACT.Copy)
                        e.activation(V[:, s, t, :], pA[:, 1, HD:2 * HD], ACT.Copy).then_inc(q["taken"], 1)

                def context_values(i, s):
                    e.wait_ge(q["pv"], pos(HG * (i - 1)))
                    for t in range(T):
                        k = slice(t * SC, (t + 1) * SC)
                        ins = e.activation(VS[k, s, t, :], VC[k, ds(i % 8), ds((i // 8) * HD, HD)]
                                           .rearrange("p a n -> p (a n)"), ACT.Copy)
                    ins.then_inc(q["vs"], 1)

                def x_high(i, s):
                    e.wait_ge(q["proj"], pos(NQ * (i - 1)))
                    high_x(e, s, i, q["xhi"])

                def w_high(i, s, nxt):
                    e.wait_ge(q["proj"], NQ * i)
                    e.wait_ge(q["f"], pos(i - 1))
                    if nxt:
                        high_w(e, raw_in, q["hi"], cw_next, i, s, slot0)
                    else:
                        high_w(e, raw_in, q["hi"], cw_here, i, s, (i // 8 + 1 + slot0) % 2)

                if cross:
                    e.wait_ge(q["vz"], 1)

                def body(i, s, nxt):
                    n, last = 1 - s, islast(i)
                    if isfirst(i):
                        x_high(0, 0)
                        x_high(1, 1)
                        if cross:
                            for k in range(NQ):
                                q_ev(0, 0, k)
                            context_values(0, 0)
                        for k in range(NT):
                            qk_ev(0, 0, k)
                        exp(0, 0, 0)
                    for h in range(3):
                        p_ev(i, s, h)
                        exp(i, s, h + 1)
                        if h == 0 and not (isinstance(i, int) and i >= NI - 2):
                            x_high(i + 2, s)
                        if h == 1:
                            w_high(i, s, nxt)
                        if cross and not last and h < 2:
                            q_ev(i + 1, n, 2 * h)
                        o_ev(i, s, h)
                        if cross and not last and h < 2:
                            q_ev(i + 1, n, 2 * h + 1)
                    if not last:
                        for k in range(1 if cross else 2):
                            qk_ev(i + 1, n, k)
                    p_ev(i, s, 3)
                    if not last:
                        for k in range(1 if cross else 2, NT):
                            qk_ev(i + 1, n, k)
                        exp(i + 1, n, 0)
                    o_ev(i, s, 3)
                    if not last and cross:
                        context_values(i + 1, n)
                in_pairs(e, NI, body, 24)
                phase_end(e, name)

            def heads(x, swap=False):
                v = x.rearrange("p (h a d) -> p h a d", a=2, d=H2)
                return v[:, :, ::-1, :] if swap else v

            def table(x, t, n):
                return bc(x[:, t, :].rearrange("p (a d) -> p a d", a=2), 1, n)

            def dve(e):
                if cross:
                    e.wait_ge(q["const"], 64)
                    for j, (o, a, w) in enumerate(((cosk, cosT, 2), (sink, sinT, 3), (cosT, cosT, 0),
                                                   (sinT, sinT, 1))):
                        e.tensor_tensor(o[:, :, :], a[:, :, :], bc(wrow[:, w, :], 1, T), ALU.mult
                                        ).then_inc(q["table"], 1)
                        e.wait_ge(q["table"], j + 1)
                else:
                    e.wait_ge(q["const"], 64)

                def take(i, s, n):
                    t, g = (n // 2 if n < 4 else n - 4), i // 8
                    e.wait_ge(q["proj"], NQ * i + n + 1)
                    if n < 4:
                        b = n % 2
                        e.wait_ge(q["rc"], pos(4 * i + n - 1))
                        e.tensor_tensor(qb[:, b, :], pA[:, b, :],
                                        bias[:, ds(g), n % 2, :].rearrange("p a n -> p (a n)"), ALU.add
                                        ).then_inc(q["taken"], 1)
                        e.wait_ge(q["taken"], NQ * i + n + 1)
                        e.wait_ge(q["rope"], pos(4 * i + n - 1))
                        e.tensor_tensor(heads(t2[:, b, :]), heads(qb[:, b, :], True), table(sinT, t, HG),
                                        ALU.mult).then_inc(q["rot"], 1)
                    else:
                        e.wait_ge(q["pv"], pos(HG * (i - 1)))
                        e.tensor_tensor(V[:, s, t, :], pA[:, n % 2, :],
                                        bias[:, ds(g), 2, :].rearrange("p a n -> p (a n)"), ALU.add
                                        ).then_inc(q["taken"], 1)

                def rotate_q(i, s, t):
                    e.wait_ge(q["taken"], NQ * i + 2 * t + 1)
                    e.wait_ge(q["rope"], pos(4 * (i - 1) + (1, 3)[t]))
                    e.tensor_tensor(heads(t2[:, t, :]), heads(qb[:, t, :], True), table(sinT, t, HG),
                                    ALU.mult).then_inc(q["rot"], 1)

                def rotate_k(i, s, t):
                    e.wait_ge(q["rk"], T * i + t + 1)
                    e.wait_ge(q["rope"], pos(4 * (i - 1) + 4))
                    c, _ = use(i, "qk", 2, s)
                    if not isfirst(i):
                        p, _ = use(i - 1, "qk", 2, 1 - s) if not (isinstance(i, int) and i == 1) else use(0, "qk", 2, 0)
                        e.wait_ge(q["tr"], p + 1)
                    r = ssk[:, t:t + 1]
                    o = heads(KR[:, t, :]).rearrange("p h a d -> p (h a) d")
                    kv = heads(kb[:, t, :]).rearrange("p h a d -> p (h a) d")
                    e.scalar_tensor_tensor(o, kv, r, cosk[:, t, :].rearrange("p (a d) -> p a d", a=2),
                                           ALU.mult, ALU.mult)
                    e.scalar_tensor_tensor(tk[:, t, :].rearrange("p (a d) -> p a d", a=2), kv[:, ::-1, :], r,
                                           sink[:, t, :].rearrange("p (a d) -> p a d", a=2),
                                           ALU.mult, ALU.mult).then_inc(q["k1"], 1)

                def soft(i, s, h):
                    c, _ = use(i, "w", h, s)
                    e.wait_ge(q["sc"], HG * i + h + 1)
                    if cross and h == 0:
                        e.wait_ge(q["rq"], i + 1)
                    if not isfirst(i):
                        pi = i - 1
                        p, _ = use(pi, "w", h, 1 - s)
                        e.wait_ge(q["tr"], p + 1)
                        apart(e, p + 1)
                    for t in range(T):
                        x = slice(OFF[t], OFF[t] + WID[t])
                        scale = nrq[:, s, t, h:h + 1] if cross else -float(HD) ** -0.5
                        ins = e.tensor_tensor_reduce(PB[:, h, x], pS[:, h % 2, x], mask[:, x], scale, 1e38,
                                                     ALU.add, ALU.min, nm[:, h, t:t + 1])
                    ins.then_inc(q["sct"], 1)

                def recip(i, h):
                    e.wait_ge(q["ex"], HG * i + h + 1)
                    e.wait_ge(q["pn"], pos(HG * (i - 1) + h + 1))
                    e.reciprocal(rs[:, h, :], sm[:, h, :]).then_inc(q["rs"], 1)

                def normalise(i, h):
                    e.wait_ge(q["rs"], HG * i + h + 1)
                    for t in range(T):
                        x = PB[:, h, OFF[t]:OFF[t] + WID[t]]
                        ins = e.tensor_scalar(x, x, rs[:, h, t:t + 1], None, ALU.mult)
                    ins.then_inc(q["pn"], 1)

                def o_low(i, s, h):
                    e.wait_ge(q["oth"], HG * i + h + 1)
                    e.tensor_tensor(OTl[:, s, h, :], pO[:, 0:S], OTh[:, s, h, :].bitcast(F32), ALU.subtract
                                    ).then_inc(q["ot"], 1)

                def add_out(i):
                    e.wait_ge(q["f"], i + 1)
                    e.wait_ge(q["acc"], i)
                    r = R[:, ds(T * (i % 8), T), :]
                    o = pF[:, :].rearrange("p (t n) -> p t n", t=T)
                    if cross:
                        e.scalar_tensor_tensor(r, o, tanhg[:, 2:3], r, ALU.mult, ALU.add).then_inc(q["acc"], 1)
                    else:
                        e.tensor_tensor(r, o, r, ALU.add).then_inc(q["acc"], 1)

                def part(i, s, n):
                    if cross:
                        if n % 2 == 0:
                            rotate_q(i, s, n // 2)
                        else:
                            rotate_k(i, s, n // 2)
                    else:
                        take(i, s, n)

                def body(i, s, nxt):
                    n, last = 1 - s, islast(i)
                    if isfirst(i):
                        for k in range(NQ):
                            part(0, 0, k)
                        soft(0, 0, 0)
                        recip(0, 0)
                        normalise(0, 0)
                    for h in range(3):
                        soft(i, s, h + 1)
                        if not last and not cross:
                            part(i + 1, n, 2 * h)
                        elif not last and h:
                            rotate_k(i + 1, n, h - 1)
                        recip(i, h + 1)
                        normalise(i, h + 1)
                        o_low(i, s, h)
                        if not last and not cross:
                            part(i + 1, n, 2 * h + 1)
                        elif not last and h < 2:
                            rotate_q(i + 1, n, h)
                    if not last:
                        soft(i + 1, n, 0)
                    o_low(i, s, 3)
                    if not last:
                        recip(i + 1, 0)
                        normalise(i + 1, 0)
                    if not isfirst(i):
                        add_out(i - 1)
                    if last:
                        add_out(i)
                in_pairs(e, NI, body, 24)
                phase_end(e, name)

            def pool(e):
                if cross:
                    e.memset(VS[:, :, :, :], 0.0).then_inc(q["vz"], 1)
                    e.wait_ge(q["table"], 4)
                else:
                    e.wait_ge(q["const"], 64)

                def x_low(i, s):
                    low_x(e, s, i, q["xhi"], q["xs"])

                def w_low(i, s, nxt):
                    if nxt:
                        low_w(e, q["hi"], q["split"], cw_next, i, s, slot0)
                    else:
                        low_w(e, q["hi"], q["split"], cw_here, i, s, (i // 8 + 1 + slot0) % 2)

                def rotate(i, s, n):
                    x = (KR if n % 2 else QR)[:, n // 2, :]
                    e.wait_ge(q["taken"], NQ * i + n + 1)
                    apart(e, NQ * i + n + 1)
                    if not isfirst(i):
                        p, _ = use(i - 1, "qk", n, 1 - s) if not (isinstance(i, int) and i == 1) else use(0, "qk", n, 0)
                        e.wait_ge(q["tr"], p + 1)
                        apart(e, p + 1)
                    e.tensor_tensor(heads(x), heads(qb[:, n % 2, :]), table(cosT, n // 2, HG), ALU.mult
                                    ).then_inc(q["rc"], 1)
                    e.wait_ge(q["rc"], 4 * i + n + 1)
                    apart(e, 4 * i + n + 1)
                    e.wait_ge(q["rot"], 4 * i + n + 1)
                    apart(e, 4 * i + n + 1)
                    e.tensor_tensor(x, x, t2[:, n % 2, :], ALU.add).then_inc(q["rope"], 1)

                def rotate_q(i, s, t):
                    e.wait_ge(q["taken"], NQ * i + 2 * t + 1)
                    apart(e, NQ * i + 2 * t + 1)
                    x = QR[:, t, :]
                    if not isfirst(i):
                        p, _ = use(i - 1, "qk", t, 1 - s) if not (isinstance(i, int) and i == 1) else use(0, "qk", t, 0)
                        e.wait_ge(q["tr"], p + 1)
                        apart(e, p + 1)
                    e.tensor_tensor(heads(x), heads(qb[:, t, :]), table(cosT, t, HG), ALU.mult
                                    ).then_inc(q["rc"], 1)
                    e.wait_ge(q["rc"], T * i + t + 1)
                    apart(e, T * i + t + 1)
                    e.wait_ge(q["rot"], T * i + t + 1)
                    apart(e, T * i + t + 1)
                    e.tensor_tensor(x, x, t2[:, t, :], ALU.add).then_inc(q["rope"], 1)

                def inverse_norm_k(i, t):
                    e.wait_ge(q["taken"], NQ * i + 2 * t + 2)
                    apart(e, NQ * i + 2 * t + 2)
                    r = ssk[:, t:t + 1]
                    e.tensor_scalar(r, r, 1.0 / HD, 1e-6, ALU.mult, ALU.add).then_inc(q["rka"], 1)
                    e.wait_ge(q["rka"], T * i + t + 1)
                    apart(e, T * i + t + 1)
                    e.tensor_tensor(r, r, mhalf[:, 0:1], ALU.pow).then_inc(q["rk"], 1)

                def sum_k(i, t):
                    e.wait_ge(q["k1"], T * i + t + 1)
                    apart(e, T * i + t + 1)
                    e.tensor_tensor(KR[:, t, :], KR[:, t, :], tk[:, t, :], ALU.add).then_inc(q["rope"], 1)

                def inverse_norms_q(i, s):
                    e.wait_ge(q["taken"], NQ * i + 2 * T - 1)
                    apart(e, NQ * i + 2 * T - 1)
                    e.wait_ge(q["sct"], pos(HG * (i - 1)))
                    apart(e, HG * (i - 1))
                    a = nrq[:, s].rearrange("p t h -> p (t h)")
                    e.tensor_scalar(a, ssq[:, :, :].rearrange("p t h -> p (t h)"), HD * 1e-6, None, ALU.add
                                    ).then_inc(q["rqa"], 1)
                    e.wait_ge(q["rqa"], i + 1)
                    apart(e, i + 1)
                    e.tensor_tensor(a, a, mhalf[:, :], ALU.pow).then_inc(q["rqb"], 1)
                    e.wait_ge(q["rqb"], i + 1)
                    apart(e, i + 1)
                    e.tensor_scalar(a, a, -1.0, None, ALU.mult).then_inc(q["rq"], 1)

                def body(i, s, nxt):
                    n, last = 1 - s, islast(i)
                    if isfirst(i):
                        x_low(0, 0)
                        x_low(1, 1)
                        if cross:
                            for t in range(T):
                                rotate_q(0, 0, t)
                                inverse_norm_k(0, t)
                                sum_k(0, t)
                            inverse_norms_q(0, 0)
                        else:
                            for k in range(4):
                                rotate(0, 0, k)
                    if not (isinstance(i, int) and i >= NI - 2):
                        x_low(i + 2, s)
                    if cross and not last:
                        rotate_q(i + 1, n, 0)
                        inverse_norm_k(i + 1, 0)
                        w_low(i, s, nxt)
                        sum_k(i + 1, 0)
                        rotate_q(i + 1, n, 1)
                        inverse_norm_k(i + 1, 1)
                        inverse_norms_q(i + 1, n)
                        sum_k(i + 1, 1)
                    elif not last:
                        rotate(i + 1, n, 0)
                        rotate(i + 1, n, 1)
                        w_low(i, s, nxt)
                        rotate(i + 1, n, 2)
                        rotate(i + 1, n, 3)
                    else:
                        w_low(i, s, nxt)
                in_pairs(e, NI, body, 24)
                phase_end(e, name)

            close_phase(name)
            return Phase(sp, pool, act, dve, pe)

        if stop >= 2:
            lnp = sb("lnp", [P, 4, KD])
            s_lnp, s_sp = sem("s_lnp"), sem("s_spill")
            sc_bo = ExitStack()
            bo = sb("bo", [P, D], F32, sc_bo)

            def ln_sp(e):
                for j, n in enumerate(("ln1_w", "ln1_b", "ln2_w", "ln2_b")):
                    e.dma_start(lnp[:, j, :], d["f0_" + n]).then_inc(s_lnp, 16)
                e.dma_start(bo[:, :], d["f0_bo"].partition_broadcast(P)).then_inc(s_lnp, 16)
                e.dma_start(spill, R[:, :, :]).then_inc(s_sp, 16)

            def ln_wait(e):
                e.wait_ge(s_lnp, 80)
                e.wait_ge(s_sp, 16)

            n1 = layer_norm("n1", double=True, affine=(lnp[:, 0, :], lnp[:, 1, :]), after=bo)
            sc_bo.close()
            f0 = ExitStack()
            self0 = causal_attention("f0", f0, False, d["w_f0"], CW_F0, d["w_moe"], CW_MOE, 0)
            f0.close()

        def experts(scope):
            name = "moe"
            NM = D // P
            W2 = E * KD * D
            wg = sb("moe_wg", [P, KD, E], F32, scope)
            be1 = sb("moe_be1", [P, E * NM], F32, scope)
            be2 = sb("moe_be2", [P, E, D], F32, scope)
            before = sb("moe_before", [P, E, E], F32, scope)
            xc = sb("moe_x", [P, 2, KD, S], F32, scope)
            xsp = sb("moe_xs", [P, 2, T, D], F32, scope)
            HM = sb("moe_h", [P, 2, NM, S], F32, scope)
            HMh = sb("moe_hh", [P, 2, NM, S], F32R, scope)
            HMl = sb("moe_hl", [P, 2, NM, S], F32R, scope)
            lg = sb("moe_lg", [P, T, E], F32, scope)
            mx = sb("moe_mx", [P, T, 1], F32, scope)
            sm = sb("moe_sm", [P, T, 1], F32, scope)
            cmp = sb("moe_cmp", [P, T, E, E], F32, scope)
            eq = sb("moe_eq", [P, T, E, E], F32, scope)
            rank = sb("moe_rank", [P, T, E], F32, scope)
            is0 = sb("moe_is0", [P, T, E], F32, scope)
            is1 = sb("moe_is1", [P, T, E], F32, scope)
            tmp = sb("moe_tmp", [P, T, E], F32, scope)
            v2 = sb("moe_v2", [P, T, 1], F32, scope)
            w1 = sb("moe_w1", [P, T, 1], F32, scope)
            w2 = sb("moe_w2", [P, T, 1], F32, scope)
            comb = sb("moe_comb", [P, T, E], F32, scope)
            q = {x: sem("moe_" + x) for x in
                 ("raw0", "raw1", "hi", "split", "const", "xc", "xhi", "xs", "lg", "l1", "ex", "v", "cb",
                  "up", "ge", "hhi", "hlo", "dn", "dt", "acc", "spl0", "spl1", "y", "e2")}
            raw_in = [q["raw0"], q["raw1"]]
            spl = [q["spl0"], q["spl1"]]

            def sp(e):
                e.dma_start(wg[:, :, :].rearrange("p k e -> p (k e)"), d["w_gate"]).then_inc(q["const"], 16)
                e.dma_start(be1[:, :], d["be1"]).then_inc(q["const"], 16)
                e.dma_start(be2[:, :, :].rearrange("p e n -> p (e n)"),
                            d["be2"].partition_broadcast(P)).then_inc(q["const"], 16)
                e.dma_start(before[:, :, :].rearrange("p e n -> p (e n)"),
                            d["earlier"].partition_broadcast(P)).then_inc(q["const"], 16)

                def body(i, s, _):
                    e.wait_ge(q["y"], pos(i - 1))
                    e.dma_start(xsp[:, s], spill[:, ds(T * i, T), :]).then_inc(spl[s], 16)
                    stream_sp(e, raw_in, q["split"], d["w_x1"], CW_X1, i, s)
                in_pairs(e, B, body)
                phase_end(e, name)

            def pe(e):
                e.wait_ge(q["const"], 64)

                def gate(i, s):
                    e.wait_ge(q["xs"], i + 1)
                    e.wait_ge(q["l1"], i)
                    for t in range(T):
                        for k in range(KD):
                            ins = e.matmul(pT[:, 0, t * E:(t + 1) * E], xc[:, s, k, t * P:(t + 1) * P],
                                           wg[:, k, :], start=(k == 0), stop=(k == KD - 1))
                    ins.then_inc(q["lg"], 1)

                def up(i, s, x):
                    c = E * i + x
                    e.wait_ge(q["ge"], pos(c - 1))
                    for m in range(NM):
                        for k in range(KD):
                            w = slice((x * KD + k) * D + m * P, (x * KD + k) * D + (m + 1) * P)
                            o = pA[:, x % 2, m * S:(m + 1) * S]
                            e.matmul(o, Wh[:, 0, w], XSh[:, s, k, :], start=(k == 0), stop=False)
                            e.matmul(o, Wh[:, 0, w], XSl[:, s, k, :], start=False, stop=False)
                            ins = e.matmul(o, Wl[:, 0, w], XSh[:, s, k, :], start=False, stop=(k == KD - 1))
                    ins.then_inc(q["up"], 1)

                def down(i, x):
                    c = E * i + x
                    e.wait_ge(q["hlo"], c + 1)
                    e.wait_ge(q["dt"], pos(c - 1))
                    for t in range(T):
                        r = slice(t * P, (t + 1) * P)
                        for k in range(NM):
                            w = slice(W2 + (x * NM + k) * D, W2 + (x * NM + k + 1) * D)
                            ins = three(e, pS[:, x % 2, t * D:(t + 1) * D], HMh[:, x % 2, k, r],
                                        HMl[:, x % 2, k, r], Wh[:, 0, w], Wl[:, 0, w], k == 0, k == NM - 1)
                    ins.then_inc(q["dn"], 1)

                def body(i, s, _):
                    if isinstance(i, int) and i == 0:
                        gate(0, 0)
                        up(0, 0, 0)
                        up(0, 0, 1)
                    last = isinstance(i, int) and i == B - 1
                    for x in range(E):
                        down_next = None
                        if x < 2:
                            up_args = (i, s, x + 2)
                            up(*up_args)
                        elif not last:
                            if x == 2:
                                gate(i + 1, 1 - s)
                            up(i + 1, 1 - s, x - 2)
                        down(i, x)
                in_pairs(e, B, body)
                phase_end(e, name)

            def act(e):
                def gelu(i, s, x):
                    c = E * i + x
                    e.wait_ge(q["up"], c + 1)
                    e.wait_ge(q["hlo"], pos(c - 1))
                    for m in range(NM):
                        ins = e.activation(HM[:, x % 2, m, :], pA[:, x % 2, m * S:(m + 1) * S], ACT.Gelu,
                                           bias=be1[:, x * NM + m:x * NM + m + 1])
                    ins.then_inc(q["ge"], 1)

                e.wait_ge(q["const"], 64)

                def exps(i):
                    e.wait_ge(q["v"], GV * i + 2)
                    e.activation(lg[:, :, :], lg[:, :, :], ACT.Exp).then_inc(q["ex"], 1)
                    e.wait_ge(q["v"], GV * i + 9)
                    e.activation(v2[:, :, :], v2[:, :, :], ACT.Exp).then_inc(q["ex"], 1)

                def body(i, s, _):
                    exps(i)
                    for x in range(E):
                        gelu(i, s, x)
                in_pairs(e, B, body)
                phase_end(e, name)

            GV = 14

            def dve(e):
                e.wait_ge(q["const"], 64)

                def step(i, n, ins):
                    ins.then_inc(q["v"], 1)
                    e.wait_ge(q["v"], GV * i + n)

                def gates(i):
                    e.wait_ge(q["lg"], i + 1)
                    e.wait_ge(q["ex"], 2 * i)
                    ps = pT[:, 0, 0:T * E].rearrange("p (t e) -> p t e", t=T)
                    step(i, 1, e.tensor_reduce(mx[:, :, 0], ps, AX.X, ALU.max))
                    e.tensor_tensor(lg[:, :, :], ps, mx[:, :, :].to_broadcast([P, T, E]), ALU.subtract
                                    ).then_inc(q["l1"], 1)
                    e.wait_ge(q["l1"], i + 1)
                    step(i, 2, e.tensor_copy(tmp[:, :, :], lg[:, :, :]))
                    e.wait_ge(q["ex"], 2 * i + 1)
                    step(i, 3, e.tensor_reduce(sm[:, :, 0], lg[:, :, :], AX.X, ALU.add))
                    step(i, 4, e.reciprocal(sm[:, :, :], sm[:, :, :]))
                    step(i, 5, e.tensor_tensor(lg[:, :, :], lg[:, :, :], sm[:, :, :].to_broadcast([P, T, E]),
                                               ALU.mult))
                    for t in range(T):
                        mine = lg[:, t, :].unsqueeze(2).to_broadcast([P, E, E])
                        other = lg[:, t, :].unsqueeze(1).to_broadcast([P, E, E])
                        e.tensor_tensor(cmp[:, t], other, mine, ALU.is_gt)
                        ins = e.tensor_tensor(eq[:, t], other, mine, ALU.is_equal)
                    step(i, 6, ins)
                    for t in range(T):
                        ins = e.tensor_tensor(eq[:, t], eq[:, t], before[:, :, :], ALU.mult)
                    step(i, 7, ins)
                    ins = e.tensor_tensor(cmp[:, :, :, :], cmp[:, :, :, :], eq[:, :, :, :], ALU.add)
                    ins.then_inc(q["l2"], 1)
                    e.wait_ge(q["l2"], i + 1)
                    e.tensor_reduce(rank[:, :, :], cmp[:, :, :, :], AX.X, ALU.add).then_inc(q["l3"], 1)
                    e.wait_ge(q["l3"], i + 1)
                    e.wait_ge(q["dt"], E * i)
                    e.wait_ge(q["e2"], E * i)
                    e.tensor_scalar(is0[:, :, :], rank[:, :, :], 0.0, None, ALU.is_equal)
                    e.tensor_scalar(is1[:, :, :], rank[:, :, :], 1.0, None, ALU.is_equal).then_inc(q["l4"], 1)
                    e.wait_ge(q["l4"], i + 1)
                    step(i, 8, e.tensor_tensor(tmp[:, :, :], is1[:, :, :], lg[:, :, :], ALU.mult))
                    e.tensor_reduce(v2[:, :, 0], tmp[:, :, :], AX.X, ALU.add)
                    e.tensor_reduce(w1[:, :, 0], lg[:, :, :], AX.X, ALU.max).then_inc(q["l5"], 1)
                    e.wait_ge(q["l5"], i + 1)
                    step(i, 9, e.tensor_tensor(v2[:, :, :], v2[:, :, :], w1[:, :, :], ALU.subtract))
                    e.wait_ge(q["ex"], 2 * i + 2)
                    step(i, 10, e.tensor_scalar(w1[:, :, :], v2[:, :, :], 1.0, None, ALU.add))
                    step(i, 11, e.reciprocal(w1[:, :, :], w1[:, :, :]))
                    step(i, 12, e.tensor_tensor(w2[:, :, :], v2[:, :, :], w1[:, :, :], ALU.mult))
                    e.tensor_tensor(is0[:, :, :], is0[:, :, :], w1[:, :, :].to_broadcast([P, T, E]), ALU.mult)
                    step(i, 13, e.tensor_tensor(is1[:, :, :], is1[:, :, :], w2[:, :, :].to_broadcast([P, T, E]),
                                                ALU.mult))
                    step(i, 14, e.tensor_tensor(comb[:, :, :], is0[:, :, :], is1[:, :, :], ALU.add))

                def low(i, x):
                    c = E * i + x
                    e.wait_ge(q["hhi"], c + 1)
                    e.tensor_tensor(HMl[:, x % 2], HM[:, x % 2], HMh[:, x % 2].bitcast(F32), ALU.subtract
                                    ).then_inc(q["hlo"], 1)

                def combine(i, s, x):
                    c = E * i + x
                    e.wait_ge(q["dn"], c + 1)
                    e.wait_ge(q["e2"], c + 1)
                    for t in range(T):
                        r = R[:, ds(T * i + t), :].rearrange("p a n -> p (a n)")
                        ins = e.scalar_tensor_tensor(r, pS[:, x % 2, t * D:(t + 1) * D], comb[:, t, x:x + 1],
                                                     r, ALU.mult, ALU.add)
                    ins.then_inc(q["dt"], 1)
                    e.wait_ge(q["dt"], c + 1)

                def body(i, s, _):
                    gates(i)
                    for x in range(E):
                        low(i, x)
                        if x:
                            combine(i, s, x - 1)
                    combine(i, s, E - 1)
                    e.wait_ge(spl[s], 16 * (i // 2 + 1))
                    r = R[:, ds(T * i, T), :]
                    e.scalar_tensor_tensor(r, r, tanhg[:, 1:2], xsp[:, s], ALU.mult, ALU.add
                                           ).then_inc(q["y"], 1)
                in_pairs(e, B, body)
                phase_end(e, name)

            q.update({x: sem("moe_" + x) for x in ("l2", "l3", "l4", "l5")})
            tb = sb("moe_tb", [P, T, D], F32, scope)

            def pool(e):
                e.wait_ge(q["const"], 64)

                def xs(i, s):
                    src = XT[:, :, ds(i * S, S)]
                    e.wait_ge(q["up"], pos(E * (i - 1)))
                    apart(e, E * (i - 1))
                    e.wait_ge(q["lg"], pos(i - 1))
                    apart(e, i - 1)
                    e.tensor_copy(xc[:, s], src)
                    copy_x(e, s, i, q["xs"], q["xhi"])

                def high(i, x):
                    c = E * i + x
                    e.wait_ge(q["ge"], c + 1)
                    apart(e, c + 1)
                    e.wait_ge(q["dn"], pos(c - 1))
                    apart(e, c - 1)
                    e.tensor_copy(HMh[:, x % 2], HM[:, x % 2]).then_inc(q["hhi"], 1)

                def biases(i, x):
                    c = E * i + x
                    e.wait_ge(q["v"], GV * i + GV)
                    apart(e, GV * i + GV)
                    e.wait_ge(q["dt"], c)
                    apart(e, c)
                    for t in range(T):
                        ins = e.tensor_scalar(tb[:, t, :], be2[:, x, :], comb[:, t, x:x + 1], None, ALU.mult)
                    ins.then_inc(q["cb"], 1)
                    e.wait_ge(q["cb"], c + 1)
                    apart(e, c + 1)
                    r = R[:, ds(T * i, T), :]
                    e.tensor_tensor(r, r, tb[:, :, :], ALU.add).then_inc(q["e2"], 1)
                    e.wait_ge(q["e2"], c + 1)
                    apart(e, c + 1)

                def body(i, s, _):
                    if isinstance(i, int) and i == 0:
                        xs(0, 0)
                        xs(1, 1)
                    for x in range(E):
                        high(i, x)
                        biases(i, x)
                    split(e, raw_in, q["hi"], q["split"], CW_X1, i, s, 1)
                    if not (isinstance(i, int) and i >= B - 2):
                        xs(i + 2, s)
                in_pairs(e, B, body)
                phase_end(e, name)

            close_phase(name)
            return Phase(sp, pool, act, dve, pe)

        if stop >= 3:
            n2 = layer_norm("n2", affine=(lnp[:, 2, :], lnp[:, 3, :]))
            sc_moe = ExitStack()
            moe = experts(sc_moe)
            sc_moe.close()

        if stop >= 4:
            x1 = ExitStack()
            KT1 = sb("x1_KT", [P, NKV, B * SC], F32, x1)
            VC1 = sb("x1_VC", [P, B, NKV * HD], F32, x1)
            kn = sb("x1_kn", [P, 1], F32, x1)
            s_kn = sem("x1_kn")
            with ExitStack() as tmp:
                context1 = context("c1", tmp, d["x1_Wk"], d["x1_Wv"], KT1, kn, VC=VC1)
            n3 = layer_norm("n3")
            cross1 = causal_attention("x1", x1, True, d["w_x1"], CW_X1, d["w_ff"], CW_FF, 1, KT=KT1, VC=VC1)
            x1.close()

        def feed_forward(scope):
            name = "ff"
            WU, WD = KD * FW, 2 * KD * FW
            gs = sb("ff_gs", [P, FM], F32, scope)
            us = sb("ff_us", [P, FM], F32, scope)
            dsc = sb("ff_ds", [P, D], F32, scope)
            act_g = sb("ff_g", [P, 2, S], F32, scope)
            HDf = sb("ff_h", [P, 2, S], F32, scope)
            HDh = sb("ff_hh", [P, 2, FM, S], F32R, scope)
            HDl = sb("ff_hl", [P, 2, FM, S], F32R, scope)
            y = sb("ff_y", [P, T, D], F32, scope)
            q = {x: sem("ff_" + x) for x in ("const", "ds", "xhi", "xs", "gu", "g", "h", "hh", "hl", "f", "y",
                                            "acc")}

            def sp(e):
                e.dma_start(gs[:, :], d["ff_gs"]).then_inc(q["const"], 16)
                e.dma_start(us[:, :], d["ff_us"]).then_inc(q["const"], 16)
                e.dma_start(dsc[:, :], d["ff_ds"].partition_broadcast(P)).then_inc(q["const"], 16)

                def body(i, s, _):
                    e.wait_ge(q["acc"], i + 1)
                    e.dma_start(out[ds(i)].rearrange("b (t p) n -> p (b t) n", p=P), R[:, ds(T * i, T), :]
                                ).then_inc(out_done, 16)
                in_pairs(e, B, body)
                e.wait_ge(out_done, 16 * B)

            def pe(e):
                def up(i, s, m):
                    c = FM * i + m
                    e.wait_ge(q["xs"], i + 1)
                    e.wait_ge(q["h"], pos(c - 1))
                    for j, at in ((0, 0), (1, WU)):
                        o = pA[:, m % 2, j * S:(j + 1) * S]
                        for k in range(KD):
                            w = slice(at + k * FW + m * P, at + k * FW + (m + 1) * P)
                            e.matmul(o, Wh[:, 1, w], XSh[:, s, k, :], start=(k == 0), stop=False)
                            e.matmul(o, Wh[:, 1, w], XSl[:, s, k, :], start=False, stop=False)
                            ins = e.matmul(o, Wl[:, 1, w], XSh[:, s, k, :], start=False, stop=(k == KD - 1))
                    ins.then_inc(q["gu"], 1)

                def down(i, s):
                    e.wait_ge(q["hl"], FM * i + FM)
                    e.wait_ge(q["y"], i)
                    for t in range(T):
                        r = slice(t * P, (t + 1) * P)
                        for k in range(FM):
                            w = slice(WD + k * D, WD + (k + 1) * D)
                            ins = three(e, pF[:, t * D:(t + 1) * D], HDh[:, s, k, r], HDl[:, s, k, r],
                                        Wh[:, 1, w], Wl[:, 1, w], k == 0, k == FM - 1)
                    ins.then_inc(q["f"], 1)

                def body(i, s, _):
                    for m in range(FM):
                        up(i, s, m)
                        if m == 1 and not (isinstance(i, int) and i == 0):
                            down(i - 1, 1 - s)
                    if isinstance(i, int) and i == B - 1:
                        down(i, s)
                in_pairs(e, B, body)

            def act(e):
                e.wait_ge(q["const"], 48)

                def body(i, s, _):
                    for m in range(FM):
                        c = FM * i + m
                        e.wait_ge(q["gu"], c + 1)
                        e.wait_ge(q["h"], pos(c - 1))
                        e.activation(act_g[:, m % 2, :], pA[:, m % 2, 0:S], ACT.Silu, scale=gs[:, m:m + 1]
                                     ).then_inc(q["g"], 1)
                in_pairs(e, B, body)

            def dve(e):
                e.wait_ge(q["const"], 48)
                e.tensor_scalar(dsc[:, :], dsc[:, :], tanhg[:, 3:4], None, ALU.mult).then_inc(q["ds"], 1)
                e.wait_ge(q["ds"], 1)

                def result(i):
                    e.wait_ge(q["f"], i + 1)
                    e.wait_ge(q["acc"], i)
                    e.tensor_tensor(y[:, :, :], pF[:, :].rearrange("p (t n) -> p t n", t=T),
                                    bc(dsc[:, :], 1, T), ALU.mult).then_inc(q["y"], 1)

                def body(i, s, _):
                    for m in range(FM):
                        c = FM * i + m
                        e.wait_ge(q["g"], c + 1)
                        e.wait_ge(q["hl"], pos(c - 1))
                        e.scalar_tensor_tensor(HDf[:, m % 2, :], pA[:, m % 2, S:2 * S], us[:, m:m + 1],
                                               act_g[:, m % 2, :], ALU.mult, ALU.mult).then_inc(q["h"], 1)
                        if m == 3 and not (isinstance(i, int) and i == 0):
                            result(i - 1)
                    if isinstance(i, int) and i == B - 1:
                        result(i)
                in_pairs(e, B, body)

            def pool(e):
                def xs(i, s):
                    e.wait_ge(q["gu"], pos(FM * (i - 1)))
                    apart(e, FM * (i - 1))
                    copy_x(e, s, i, q["xs"], q["xhi"])

                def add(i):
                    e.wait_ge(q["y"], i + 1)
                    apart(e, i + 1)
                    r = R[:, ds(T * i, T), :]
                    e.tensor_tensor(r, r, y[:, :, :], ALU.add).then_inc(q["acc"], 1)

                def body(i, s, _):
                    if isinstance(i, int) and i == 0:
                        xs(0, 0)
                        xs(1, 1)
                    for m in range(FM):
                        c = FM * i + m
                        e.wait_ge(q["h"], c + 1)
                        apart(e, c + 1)
                        e.wait_ge(q["f"], pos(i - 1))
                        apart(e, i - 1)
                        e.tensor_copy(HDh[:, s, m, :], HDf[:, m % 2, :]).then_inc(q["hh"], 1)
                        e.wait_ge(q["hh"], c + 1)
                        apart(e, c + 1)
                        e.tensor_tensor(HDl[:, s, m, :], HDf[:, m % 2, :], HDh[:, s, m, :].bitcast(F32),
                                        ALU.subtract).then_inc(q["hl"], 1)
                        if m == 4 and not (isinstance(i, int) and i == 0):
                            add(i - 1)
                    if not (isinstance(i, int) and i >= B - 2):
                        xs(i + 2, s)
                    if isinstance(i, int) and i == B - 1:
                        add(i)
                in_pairs(e, B, body)

            close_phase(name)
            return Phase(sp, pool, act, dve, pe)

        if stop >= 5:
            n4 = layer_norm("n4")
            sc_ff = ExitStack()
            ffn1 = feed_forward(sc_ff)
            sc_ff.close()

        def dump_sp(sp):
            sp.dma_start(out.rearrange("b (t p) n -> p (b t) n", p=P), R[:, :, :]).then_inc(out_done, 16)
            sp.wait_ge(out_done, 16)

        block = ctx.enter_context(nc.Block())

        @block.sync
        def _(sp):
            init_sp(sp)
            init_all(sp)
            pre0.sync(sp)
            context0.sync(sp)
            n0.sync(sp)
            cross0.sync(sp)
            if stop >= 2:
                ln_sp(sp)
                n1.sync(sp)
                self0.sync(sp)
            if stop >= 3:
                n2.sync(sp)
                moe.sync(sp)
            if stop >= 4:
                sp.dma_start(kn[:, :], d["x1_kn"]).then_inc(s_kn, 16)
                context1.sync(sp)
                n3.sync(sp)
                cross1.sync(sp)
            if stop >= 5:
                n4.sync(sp)
                ffn1.sync(sp)
            if stop < 99:
                dump_sp(sp)

        @block.gpsimd
        def _(pool):
            init_pool(pool)
            init_all(pool)
            context0.gpsimd(pool)
            n0.gpsimd(pool)
            cross0.gpsimd(pool)
            if stop >= 2:
                ln_wait(pool)
                n1.gpsimd(pool)
                self0.gpsimd(pool)
            if stop >= 3:
                n2.gpsimd(pool)
                moe.gpsimd(pool)
            if stop >= 4:
                context1.gpsimd(pool)
                n3.gpsimd(pool)
                cross1.gpsimd(pool)
            if stop >= 5:
                n4.gpsimd(pool)
                ffn1.gpsimd(pool)

        @block.scalar
        def _(act):
            init_act(act)
            init_all(act)
            pre0.scalar(act)
            context0.scalar(act)
            n0.scalar(act)
            cross0.scalar(act)
            if stop >= 2:
                ln_wait(act)
                n1.scalar(act)
                self0.scalar(act)
            if stop >= 3:
                n2.scalar(act)
                moe.scalar(act)
            if stop >= 4:
                act.wait_ge(s_kn, 16)
                context1.scalar(act)
                n3.scalar(act)
                cross1.scalar(act)
            if stop >= 5:
                n4.scalar(act)
                ffn1.scalar(act)

        @block.vector
        def _(dve):
            init_all(dve)
            pre0.vector(dve)
            context0.vector(dve)
            n0.vector(dve)
            cross0.vector(dve)
            if stop >= 2:
                ln_wait(dve)
                n1.vector(dve)
                self0.vector(dve)
            if stop >= 3:
                n2.vector(dve)
                moe.vector(dve)
            if stop >= 4:
                context1.vector(dve)
                n3.vector(dve)
                cross1.vector(dve)
            if stop >= 5:
                n4.vector(dve)
                ffn1.vector(dve)

        @block.tensor
        def _(pe):
            init_all(pe)
            context0.tensor(pe)
            n0.tensor(pe)
            cross0.tensor(pe)
            if stop >= 2:
                n1.tensor(pe)
                self0.tensor(pe)
            if stop >= 3:
                n2.tensor(pe)
                moe.tensor(pe)
            if stop >= 4:
                context1.tensor(pe)
                n3.tensor(pe)
                cross1.tensor(pe)
            if stop >= 5:
                n4.tensor(pe)
                ffn1.tensor(pe)


def layout(v):
    a = {k: np.asarray(x) for k, x in v.items()}
    c = np.ascontiguousarray

    def steps(groups):
        w = np.stack(groups)
        n = w.shape[0]
        return c(w.reshape(n, P, 8, -1).transpose(0, 2, 1, 3).reshape(n * 8, P, -1))

    def rows(w):
        return w.reshape(-1, P, w.shape[1]).transpose(1, 0, 2).reshape(P, -1)

    def cols(w, g, n=GW):
        return rows(w[:, g * n:(g + 1) * n])

    def col(x):
        return c(x.reshape(-1, P).T)

    o = {"x": a["x"], "ctxT": c(a["ctx_2048"].reshape(B * SC, D).T), "mask": a["mask_1xSxS2_ff0"]}
    o["gates"] = c(np.stack([a["g_xattn"][0], a["g_ffn"][0], a["g_xattn"][1], a["g_ffn"][1]]))
    o["ident"] = np.eye(P, dtype=np.float32)
    x0 = "L0_xattn_"
    o["w_x0"] = steps([np.concatenate([cols(a[x0 + "Wq"], g), rows(a[x0 + "Wo"][g * GW:(g + 1) * GW])], 1)
                       for g in range(G)])
    o["x0_Wk"], o["x0_Wv"] = a[x0 + "Wk"], a[x0 + "Wv"]
    o["x0_bq"], o["x0_bk"], o["x0_bv"] = a[x0 + "bq"], a[x0 + "bk"], col(a[x0 + "bv"])
    o["x0_w"] = c(np.stack([a[x0 + "qn_w"], a[x0 + "kn_w"]], 1))
    f0 = "L0_ffn_"
    o["w_f0"] = steps([np.concatenate([cols(a[f0 + "wq"], g), cols(a[f0 + "wk"], g), cols(a[f0 + "wv"], g),
                                       rows(a[f0 + "wo"][g * GW:(g + 1) * GW])], 1) for g in range(G)])
    o["f0_b"] = c(np.concatenate([a[f0 + n].reshape(G, 1, GW) for n in ("bq", "bk", "bv")], 1).reshape(-1))
    o["f0_bo"] = a[f0 + "bo"]
    for n in ("ln1_w", "ln1_b", "ln2_w", "ln2_b"):
        o["f0_" + n] = col(a[f0 + n])
    inv = (1.0 / np.float32(10000.0) ** (np.arange(0, HD, 2, dtype=np.float32) / np.float32(HD))).astype(np.float32)
    fr = np.arange(S, dtype=np.float32)[:, None] * inv[None]
    o["cos"] = c(np.concatenate([np.cos(fr), np.cos(fr)], 1).astype(np.float32))
    o["sin"] = c(np.concatenate([-np.sin(fr), np.sin(fr)], 1).astype(np.float32))
    tri = np.where(np.arange(P)[None] > np.arange(P)[:, None], np.float32(NEG), np.float32(0)).astype(np.float32)
    z = np.zeros((P, P), np.float32)
    o["mask_f0"] = c(np.concatenate([tri, z, tri], 1))
    o["mask_x1"] = c(np.concatenate([tri, z, z, tri], 1))
    o["w_moe"] = steps([np.concatenate([rows(a[f0 + "we1"][e]) for e in range(E)]
                                       + [rows(a[f0 + "we2"][e]) for e in range(E)], 1)])
    o["w_gate"] = c(rows(a[f0 + "w_gate"]))
    o["be1"] = col(a[f0 + "be1"].reshape(-1))
    o["be2"] = c(a[f0 + "be2"].reshape(-1))
    earlier = np.tril(np.ones((E, E), np.float32), -1)
    o["earlier"] = c(earlier.reshape(-1))
    x1 = "L1_xattn_"
    o["w_x1"] = steps([np.concatenate([cols(a[x1 + "wq"], g),
                                       rows(np.concatenate([a[x1 + "wk"][:, g * HD:(g + 1) * HD],
                                                            a[x1 + "wv"][:, g * HD:(g + 1) * HD]], 1)),
                                       rows(a[x1 + "wo"][g * GW:(g + 1) * GW])], 1) for g in range(G)])
    o["x1_Wk"], o["x1_Wv"] = a[x1 + "wk_ctx"], a[x1 + "wv_ctx"]
    qn, kn = a[x1 + "q_norm_w"], a[x1 + "k_norm_w"]

    def swap(w):
        return np.concatenate([w[H2:], w[:H2]])
    o["x1_w"] = c(np.concatenate([qn, swap(qn), kn, swap(kn)]))
    o["x1_kn"] = col(kn)
    f1 = "L1_ffn_"
    pad = FW - a[f1 + "gate_w"].shape[0]

    def padded(w):
        return np.concatenate([w, np.zeros((pad, *w.shape[1:]), np.float32)])
    o["w_ff"] = steps([np.concatenate([rows(padded(a[f1 + "gate_w"]).T), rows(padded(a[f1 + "up_w"]).T),
                                       rows(padded(a[f1 + "down_w"].T))], 1)])
    o["ff_gs"], o["ff_us"] = col(padded(a[f1 + "gate_s"])), col(padded(a[f1 + "up_s"]))
    o["ff_ds"] = a[f1 + "down_s"]
    return o


def kernel(**inputs):
    import concourse.bacc as bacc
    from concourse.bass_utils import run_bass_kernel_spmd

    nc = bacc.Bacc("TRN2", target_bir_lowering=False, num_devices=1)
    arrays = layout(inputs)
    aps = {k: nc.dram_tensor(f"in_{k}", x.shape, mybir.dt.from_np(x.dtype), kind="ExternalInput").ap()
           for k, x in arrays.items()}
    out = nc.dram_tensor("out", (B, S, D), F32, kind="ExternalOutput").ap()
    spill = nc.dram_tensor("x_spill", (P, B * T, D), F32).ap()
    build(nc, aps, out, spill)
    r = run_bass_kernel_spmd(nc, [{f"in_{k}": x for k, x in arrays.items()}], core_ids=[0])
    return r.results[0]["out"]
```
